# Optimizing a Trainium2 kernel written in Bass

```python
import numpy as np
import jax
import jax.numpy as jnp

def _softmax(x, axis=-1):
    return jax.nn.softmax(x, axis=axis)

def _gelu(x):
    return jax.nn.gelu(x, approximate=True)

def _silu(x):
    return jax.nn.silu(x)

def _sigmoid(x):
    return jax.nn.sigmoid(x)

def _layernorm(x, axis=-1, eps=1e-05):
    m = jnp.mean(x, axis=axis, keepdims=True)
    v = jnp.var(x, axis=axis, keepdims=True)
    return (x - m) / jnp.sqrt(v + eps)

def _scatter_add(tgt, idx, src, axis=0):
    return tgt.at[idx].add(src)

def _segment_sum(src, seg, n):
    return jax.ops.segment_sum(src, seg, n)
kernel_name = 'mk_adaln_d1_jaxref_r4_d02860'

def setup_inputs(seed: int=0):
    np.random.seed(seed)
    _w = jnp.asarray

    def _L0_attn_setup():
        import jax, jax.numpy as jnp
        import numpy as np
        D_MODEL = 256
        N_HEADS = 16
        D_FF = 1024
        D_STATE = 16
        D_CONV = 4
        EXPAND = 2
        D_INNER = D_MODEL * EXPAND
        DT_RANK = D_MODEL // 16
        BATCH = 4
        SEQ = 256

        def _ln(x, w, b):
            m = jnp.mean(x, axis=-1, keepdims=True)
            v = jnp.var(x, axis=-1, keepdims=True)
            return (x - m) / jnp.sqrt(v + 1e-05) * w + b
        key = jax.random.key(seed)
        ks = jax.random.split(key, 32)
        s = 0.02
        inp = {}
        inp['x'] = jax.random.normal(ks[0], (BATCH, SEQ, D_MODEL), jnp.float32)
        inp['ln1_w'] = jnp.ones((D_MODEL,), jnp.float32)
        inp['ln1_b'] = jnp.zeros((D_MODEL,), jnp.float32)
        inp['ln2_w'] = jnp.ones((D_MODEL,), jnp.float32)
        inp['ln2_b'] = jnp.zeros((D_MODEL,), jnp.float32)
        inp['q_w'] = jax.random.normal(ks[1], (D_MODEL, D_MODEL), jnp.float32) * s
        inp['q_b'] = jnp.zeros((D_MODEL,), jnp.float32)
        inp['k_w'] = jax.random.normal(ks[2], (D_MODEL, D_MODEL), jnp.float32) * s
        inp['k_b'] = jnp.zeros((D_MODEL,), jnp.float32)
        inp['v_w'] = jax.random.normal(ks[3], (D_MODEL, D_MODEL), jnp.float32) * s
        inp['v_b'] = jnp.zeros((D_MODEL,), jnp.float32)
        inp['o_w'] = jax.random.normal(ks[4], (D_MODEL, D_MODEL), jnp.float32) * s
        inp['o_b'] = jnp.zeros((D_MODEL,), jnp.float32)
        inp['in_proj_w'] = jax.random.normal(ks[5], (D_MODEL, 2 * D_INNER), jnp.float32) * s
        inp['conv_w'] = jax.random.normal(ks[6], (D_INNER, D_CONV), jnp.float32) * 0.2
        inp['conv_b'] = jnp.zeros((D_INNER,), jnp.float32)
        inp['x_proj_w'] = jax.random.normal(ks[7], (D_INNER, DT_RANK + 2 * D_STATE), jnp.float32) * s
        dt_std = DT_RANK ** (-0.5)
        inp['dt_w'] = jax.random.uniform(ks[8], (DT_RANK, D_INNER), jnp.float32, -dt_std, dt_std)
        dt = jnp.exp(jax.random.uniform(ks[9], (D_INNER,), jnp.float32) * (np.log(0.1) - np.log(0.001)) + np.log(0.001))
        inp['dt_b'] = dt + jnp.log(-jnp.expm1(-dt))
        A = jnp.tile(jnp.arange(1, D_STATE + 1, dtype=jnp.float32), (D_INNER, 1))
        inp['A_log'] = jnp.log(A)
        inp['D_param'] = jnp.ones((D_INNER,), jnp.float32)
        inp['ssm_out_w'] = jax.random.normal(ks[10], (D_INNER, D_MODEL), jnp.float32) * s
        inp['mix_weight'] = jnp.full((D_MODEL,), 0.5, jnp.float32)
        inp['ffn_w1'] = jax.random.normal(ks[11], (D_MODEL, D_FF), jnp.float32) * s
        inp['ffn_b1'] = jnp.zeros((D_FF,), jnp.float32)
        inp['ffn_w2'] = jax.random.normal(ks[12], (D_FF, D_MODEL), jnp.float32) * s
        inp['ffn_b2'] = jnp.zeros((D_MODEL,), jnp.float32)
        return inp
    _L0_attn_in = _L0_attn_setup()

    def _L0_ffn_setup():
        import jax, jax.numpy as jnp
        import numpy as np
        B, S, D, O, E, R, TOP_K = (4, 256, 256, 256, 8, 16, 2)
        SCALING = 32.0 / 16.0
        NEG_INF = -1000000000.0
        key = jax.random.key(seed)
        ks = jax.random.split(key, 6)
        return {'x': jax.random.normal(ks[0], (B, S, D), jnp.float32), 'base_w': jax.random.normal(ks[1], (O, D), jnp.float32) * 0.02, 'base_b': jnp.zeros((O,), jnp.float32), 'lora_A': jax.random.normal(ks[2], (E, D, R), jnp.float32) * 0.02, 'lora_B': jax.random.normal(ks[3], (E, R, O), jnp.float32) * 0.02, 'router_w': jax.random.normal(ks[4], (E, D), jnp.float32) * 0.02, 'router_b': jnp.zeros((E,), jnp.float32)}
    _L0_ffn_in = _L0_ffn_setup()
    _L0_c = _w((lambda *s: np.random.randn(*s).astype(np.float32) * 0.05)(32, 256))
    _L0_wmod = _w((lambda *s: np.random.randn(*s).astype(np.float32) * 0.05)(256, 6 * 256) * 256 ** (-0.5))
    _d = {'L0_attn_x': _L0_attn_in['x'], 'L0_attn_ln1_w': _L0_attn_in['ln1_w'], 'L0_attn_ln1_b': _L0_attn_in['ln1_b'], 'L0_attn_ln2_w': _L0_attn_in['ln2_w'], 'L0_attn_ln2_b': _L0_attn_in['ln2_b'], 'L0_attn_q_w': _L0_attn_in['q_w'], 'L0_attn_q_b': _L0_attn_in['q_b'], 'L0_attn_k_w': _L0_attn_in['k_w'], 'L0_attn_k_b': _L0_attn_in['k_b'], 'L0_attn_v_w': _L0_attn_in['v_w'], 'L0_attn_v_b': _L0_attn_in['v_b'], 'L0_attn_o_w': _L0_attn_in['o_w'], 'L0_attn_o_b': _L0_attn_in['o_b'], 'L0_attn_in_proj_w': _L0_attn_in['in_proj_w'], 'L0_attn_conv_w': _L0_attn_in['conv_w'], 'L0_attn_conv_b': _L0_attn_in['conv_b'], 'L0_attn_x_proj_w': _L0_attn_in['x_proj_w'], 'L0_attn_dt_w': _L0_attn_in['dt_w'], 'L0_attn_dt_b': _L0_attn_in['dt_b'], 'L0_attn_A_log': _L0_attn_in['A_log'], 'L0_attn_D_param': _L0_attn_in['D_param'], 'L0_attn_ssm_out_w': _L0_attn_in['ssm_out_w'], 'L0_attn_mix_weight': _L0_attn_in['mix_weight'], 'L0_attn_ffn_w1': _L0_attn_in['ffn_w1'], 'L0_attn_ffn_b1': _L0_attn_in['ffn_b1'], 'L0_attn_ffn_w2': _L0_attn_in['ffn_w2'], 'L0_attn_ffn_b2': _L0_attn_in['ffn_b2'], 'L0_ffn_base_w': _L0_ffn_in['base_w'], 'L0_ffn_base_b': _L0_ffn_in['base_b'], 'L0_ffn_lora_A': _L0_ffn_in['lora_A'], 'L0_ffn_lora_B': _L0_ffn_in['lora_B'], 'L0_ffn_router_w': _L0_ffn_in['router_w'], 'L0_ffn_router_b': _L0_ffn_in['router_b'], 'L0_c': _L0_c, 'L0_wmod': _L0_wmod}
    _x0 = _d['L0_attn_x']
    _d['L0_attn_x'] = jax.random.normal(jax.random.fold_in(jax.random.key(seed), 1), (32, 512, 256), dtype=_x0.dtype)
    del _x0
    return _d

def reference(L0_attn_x, L0_attn_ln1_w, L0_attn_ln1_b, L0_attn_ln2_w, L0_attn_ln2_b, L0_attn_q_w, L0_attn_q_b, L0_attn_k_w, L0_attn_k_b, L0_attn_v_w, L0_attn_v_b, L0_attn_o_w, L0_attn_o_b, L0_attn_in_proj_w, L0_attn_conv_w, L0_attn_conv_b, L0_attn_x_proj_w, L0_attn_dt_w, L0_attn_dt_b, L0_attn_A_log, L0_attn_D_param, L0_attn_ssm_out_w, L0_attn_mix_weight, L0_attn_ffn_w1, L0_attn_ffn_b1, L0_attn_ffn_w2, L0_attn_ffn_b2, L0_ffn_base_w, L0_ffn_base_b, L0_ffn_lora_A, L0_ffn_lora_B, L0_ffn_router_w, L0_ffn_router_b, L0_c, L0_wmod):

    def _L0_attn_ref(x, ln1_w, ln1_b, ln2_w, ln2_b, q_w, q_b, k_w, k_b, v_w, v_b, o_w, o_b, in_proj_w, conv_w, conv_b, x_proj_w, dt_w, dt_b, A_log, D_param, ssm_out_w, mix_weight, ffn_w1, ffn_b1, ffn_w2, ffn_b2):
        import jax, jax.numpy as jnp
        import numpy as np
        D_MODEL = 256
        N_HEADS = 16
        D_FF = 1024
        D_STATE = 16
        D_CONV = 4
        EXPAND = 2
        D_INNER = D_MODEL * EXPAND
        DT_RANK = D_MODEL // 16
        BATCH = 4
        SEQ = 256

        def _ln(x, w, b):
            m = jnp.mean(x, axis=-1, keepdims=True)
            v = jnp.var(x, axis=-1, keepdims=True)
            return (x - m) / jnp.sqrt(v + 1e-05) * w + b
        B, L, Dm = x.shape
        H = N_HEADS
        hd = Dm // H
        xn = _ln(x, ln1_w, ln1_b)
        q = (xn @ q_w + q_b).reshape(B, L, H, hd)
        k = (xn @ k_w + k_b).reshape(B, L, H, hd)
        v = (xn @ v_w + v_b).reshape(B, L, H, hd)
        scores = jnp.einsum('bqhd,bkhd->bhqk', q, k) * hd ** (-0.5)
        causal = jnp.tril(jnp.ones((L, L), bool))
        scores = jnp.where(causal[None, None], scores, -jnp.inf)
        attn = jax.nn.softmax(scores, axis=-1)
        attn_out = jnp.einsum('bhqk,bkhd->bqhd', attn, v).reshape(B, L, Dm) @ o_w + o_b
        xz = xn @ in_proj_w
        Di = xz.shape[-1] // 2
        x_ssm, z = (xz[..., :Di], xz[..., Di:])
        K = conv_w.shape[1]
        xp = jnp.pad(x_ssm, ((0, 0), (K - 1, 0), (0, 0)))
        x_c = sum((xp[:, j:j + L, :] * conv_w[:, j] for j in range(K))) + conv_b
        x_c = jax.nn.silu(x_c)
        x_dbc = x_c @ x_proj_w
        R = dt_w.shape[0]
        N = A_log.shape[1]
        dt = jax.nn.softplus(x_dbc[..., :R] @ dt_w + dt_b)
        Bm = x_dbc[..., R:R + N]
        Cm = x_dbc[..., R + N:]
        A = -jnp.exp(A_log)

        def step(h, inp):
            xt, dtt, Bt, Ct = inp
            h = jnp.exp(dtt[..., None] * A) * h + (xt * dtt)[..., None] * Bt[:, None, :]
            y = jnp.einsum('bn,bdn->bd', Ct, h)
            return (h, y)
        h0 = jnp.zeros((B, Di, N), x.dtype)
        _, ys = jax.lax.scan(step, h0, (x_c.swapaxes(0, 1), dt.swapaxes(0, 1), Bm.swapaxes(0, 1), Cm.swapaxes(0, 1)))
        y = ys.swapaxes(0, 1)
        y = (y + x_c * D_param) * jax.nn.silu(z)
        ssm_out = y @ ssm_out_w
        alpha = jax.nn.sigmoid(mix_weight)
        x = x + alpha * attn_out + (1.0 - alpha) * ssm_out
        h2 = _ln(x, ln2_w, ln2_b)
        ffn = jax.nn.gelu(h2 @ ffn_w1 + ffn_b1, approximate=False) @ ffn_w2 + ffn_b2
        return x + ffn

    def _L0_ffn_ref(x, base_w, base_b, lora_A, lora_B, router_w, router_b):
        import jax, jax.numpy as jnp
        import numpy as np
        B, S, D, O, E, R, TOP_K = (4, 256, 256, 256, 8, 16, 2)
        SCALING = 32.0 / 16.0
        NEG_INF = -1000000000.0
        result = jnp.einsum('bsd,od->bso', x, base_w) + base_b
        ax = jnp.einsum('bsd,edr->bser', x, lora_A)
        bax = jnp.einsum('bser,ero->bseo', ax, lora_B)
        logits = jnp.einsum('bsd,ed->bse', x, router_w) + router_b
        kth = jax.lax.top_k(logits, TOP_K)[0][..., -1:]
        masked = jnp.where(logits < kth, NEG_INF, logits)
        expert_weights = jax.nn.softmax(masked, axis=-1)
        return result + SCALING * jnp.einsum('bse,bseo->bso', expert_weights, bax)
    x = L0_attn_x
    mod = (_silu(L0_c) @ L0_wmod).reshape(L0_c.shape[0], 6, 1, -1)
    sa, ca, ga, sb, cb, gb = (mod[:, 0], mod[:, 1], mod[:, 2], mod[:, 3], mod[:, 4], mod[:, 5])
    ga = (2 * (ga >= 0) - 1) * jnp.maximum(jnp.abs(ga), 0.25)
    gb = (2 * (gb >= 0) - 1) * jnp.maximum(jnp.abs(gb), 0.25)
    h = _layernorm(x, axis=-1) * (1 + ca) + sa
    x = x + ga * _L0_attn_ref(h, L0_attn_ln1_w, L0_attn_ln1_b, L0_attn_ln2_w, L0_attn_ln2_b, L0_attn_q_w, L0_attn_q_b, L0_attn_k_w, L0_attn_k_b, L0_attn_v_w, L0_attn_v_b, L0_attn_o_w, L0_attn_o_b, L0_attn_in_proj_w, L0_attn_conv_w, L0_attn_conv_b, L0_attn_x_proj_w, L0_attn_dt_w, L0_attn_dt_b, L0_attn_A_log, L0_attn_D_param, L0_attn_ssm_out_w, L0_attn_mix_weight, L0_attn_ffn_w1, L0_attn_ffn_b1, L0_attn_ffn_w2, L0_attn_ffn_b2)
    h = _layernorm(x, axis=-1) * (1 + cb) + sb
    x = x + gb * _L0_ffn_ref(h, L0_ffn_base_w, L0_ffn_base_b, L0_ffn_lora_A, L0_ffn_lora_B, L0_ffn_router_w, L0_ffn_router_b)
    return x

_drawn_inputs = setup_inputs


def setup_inputs(seed=0):
    import zlib

    import numpy as np

    out = dict(_drawn_inputs(seed))
    spreads = {'L0_attn_ln1_w': (1.0, 0.2),
     'L0_attn_ln1_b': (0.0, 0.1),
     'L0_attn_ln2_w': (1.0, 0.2),
     'L0_attn_ln2_b': (0.0, 0.1),
     'L0_attn_q_b': (0.0, 0.1),
     'L0_attn_k_b': (0.0, 0.1),
     'L0_attn_v_b': (0.0, 0.1),
     'L0_attn_o_b': (0.0, 0.1),
     'L0_attn_conv_b': (0.0, 0.1),
     'L0_attn_D_param': (1.0, 0.2),
     'L0_attn_mix_weight': (0.5, 0.2),
     'L0_attn_ffn_b1': (0.0, 0.1),
     'L0_attn_ffn_b2': (0.0, 0.1),
     'L0_ffn_base_b': (0.0, 0.1),
     'L0_ffn_router_b': (0.0, 0.1)}
    factors = {}
    for name, (base, spread) in spreads.items():
        noise = np.random.default_rng([zlib.crc32(name.encode()), seed]).standard_normal(out[name].shape)
        drawn = base * np.exp(spread * noise) if base else spread * noise
        out[name] = jnp.asarray(drawn.astype(out[name].dtype))
    for name, factor in factors.items():
        out[name] = (out[name] * factor).astype(out[name].dtype)
    return out
```

```python
from contextlib import ExitStack

import concourse.bass as bass
from concourse import mybir

ALU = mybir.AluOpType
ACT = mybir.ActivationFunctionType
F32 = mybir.dt.float32
BF16 = mybir.dt.bfloat16
AX_X = mybir.AxisListType.X

B, L, D = 32, 512, 256
P = 128
TB = L // P
KT = D // P
H, HD = 16, 16
G = 4
NG = H // G
DI = 2 * D
J = DI // P
N = 16
R = 16
K_CONV = 4
FF = 4 * D
FT = FF // P
E, LR = 8, 16
EPS = 1e-5
LORA_SCALE = 2.0
SOFTPLUS_CAP = 80.0
JP = 2
UNITS = N * J // JP
RING = 4
AR = 2
BC_SLOTS = 3
Q_PART = [0, 0, 1, 1, 0, 2]
K_PART = [0, 1, 0, 1, 2, 0]
TERMS = len(Q_PART)
QK_ROWS = TERMS * HD
MASKED = -1e30

FIN = ["gate", "yt0", "yt1", "yt2", "yt3", "sso0", "sso1", "l2s", "l2a", "h2t0", "h2t1",
       "f1_0", "f1_1", "f1_2", "f1_3", "f1_4", "f1_5", "f1_6", "f1_7", "gelu", "f2_0", "f2_1",
       "x2", "l3a", "h3t0", "h3t1", "route", "route2", "lora", "axt", "out0", "out1", "put"]
Z = ["z0", "z1", "z2", "z3", "zsilu", "v0", "v1"]
ATT = (["ld0", "mx0", "mt0"] + [f"st0_{k}" for k in range(TB)] + ["on0"]
       + ["ld1", "mx1", "mt1"] + [f"st1_{k}" for k in range(TB)] + ["on1"]
       + ["ld2", "mx2", "mt2"] + [f"st2_{k}" for k in range(TB)] + ["on2"]
       + ["ld3", "mx3", "mt3"] + [f"st3_{k}" for k in range(TB)] + ["on3"]
       + ["ot0", "ot1", "op0", "op1"])
PREP = ["load", "l0s", "l0a", "l1a", "xt0", "xt1", "qk0", "qk1", "qk2", "qk3",
        "xs0", "xs1", "xs2", "xs3", "xsilu", "xp", "dt0", "dt1", "dt2", "dt3", "sp", "u"]


class Signal:

    def __init__(self, sem, per):
        self.sem, self.per = sem, per


class Batch:

    def __init__(self, reg, off):
        self.reg, self.off = reg, off

    @property
    def index(self):
        return self.off if self.reg is None else self.reg * 2 + self.off

    def next(self, n=1):
        return Batch(self.reg, self.off + n)

    def at(self, signal, n=None):
        n = signal.per if n is None else n
        fixed = self.off * signal.per + n
        return fixed if self.reg is None else self.reg * (2 * signal.per) + fixed

    def wait(self, engine, signal, n=None):
        engine.wait_ge(signal.sem, self.at(signal, n))

    def wait_last(self, engine, signal, n=None):
        n = signal.per if n is None else n
        if self.reg is None and self.off == 0:
            return
        engine.wait_ge(signal.sem, self.next(-1).at(signal, n))


class Bank:

    def __init__(self):
        self.last = None

    def fill(self, pe, b, freed_by, n):
        if self.last is not None:
            before, signal, count = self.last
            before.wait(pe, signal, count)
        self.last = b, freed_by, n

    def into_loop(self, reg):
        b, signal, n = self.last
        self.last = Batch(reg, b.off), signal, n

    def out_of_loop(self, turns):
        b, signal, n = self.last
        self.last = Batch(None, b.off + turns - 2), signal, n


def adaln_block(nc: bass.Bass, d, out):
    ctx = ExitStack()
    with ctx:
        def sb(name, shape, dt=F32):
            return ctx.enter_context(nc.sbuf_tensor(name, shape, dt))

        def pb(name):
            return ctx.enter_context(nc.psum_tensor(name, [P, 512], F32))

        def sem(name):
            return ctx.enter_context(nc.semaphore(name))

        def sig(name, per):
            return Signal(sem(name), per)

        def dram(name, shape, dt=F32):
            return nc.dram_tensor(name, shape, dt).ap()

        mod_rows = dram("mod_rows", (B, 6 * D))
        mod_cols = dram("mod_cols", (B, P, 2 * KT))
        hres_d = dram("hres_d", (B, L, D))
        qk_d = dram("qk_d", (B, 2, 3, D, L), BF16)
        bc_d = dram("bc_d", (B, 2 * N, L))
        ones_d = dram("ones_d", (2, G, L), BF16)

        w_in = sb("w_in", [P, KT, 2 * DI])
        w_qkv = sb("w_qkv", [P, 3, KT, D])
        w_o = sb("w_o", [P, KT, D])
        w_ssm = sb("w_ssm", [P, J, D])
        w_f1 = sb("w_f1", [P, KT, FF])
        w_f2 = sb("w_f2", [P, FT, D])
        w_xp = sb("w_xp", [P, J, P])
        w_dt = sb("w_dt", [P, DI])
        w_base = sb("w_base", [P, KT, D])
        w_la = sb("w_la", [P, KT, E * LR])
        w_lb = sb("w_lb", [P, D])
        w_rt = sb("w_rt", [P, KT, E])
        ident = sb("ident", [P, P])
        identb = sb("identb", [P, P], BF16)
        mask_qk = sb("mask_qk", [P, P], BF16)
        mask_kq = sb("mask_kq", [P, P], BF16)
        A = sb("A", [P, J, N])
        D_par = sb("D_par", [P, J])
        conv_w = sb("conv_w", [P, J, K_CONV])
        conv_b = sb("conv_b", [P, J])
        dt_b = sb("dt_b", [P, J])
        ln1 = sb("ln1", [P, 2, KT])
        ln2 = sb("ln2", [P, 2, KT])
        qkv_b = sb("qkv_b", [P, 3, KT])
        f1_b = sb("f1_b", [P, FT])
        ob_row = sb("ob_row", [P, D])
        f2b_row = sb("f2b_row", [P, D])
        bb_row = sb("bb_row", [P, D])
        rb_row = sb("rb_row", [P, E])
        eps4 = sb("eps4", [P, TB])
        mhalf4 = sb("mhalf4", [P, TB])

        dts = sb("dts", [P, 2, J, L])
        us = sb("us", [P, 2, J, L])
        xc = sb("xc", [P, J, L])
        zs = sb("zs", [P, TB, DI])
        ygT = sb("ygT", [P, J, L])
        decay = sb("decay", [P, AR, JP, L])
        state = sb("state", [P, RING, JP, L])
        bc = sb("bc", [P, BC_SLOTS, 2, L])

        xt = sb("xt", [P, TB, D])
        ht = sb("ht", [P, TB, D])
        mod_a = sb("mod_a", [P, 2, D])
        xnT = sb("xnT", [P, KT, L])
        qkf = sb("qkf", [P, L])
        qkp = sb("qkp", [P, 3, L], BF16)
        dbc = sb("dbc", [P, L])
        vt = sb("vt", [P, TB, H, HD + 1])

        def stats_tiles(name):
            return (sb(name + "_st", [P, TB, 6]), sb(name + "_mv", [P, TB, 2]),
                    sb(name + "_ve", [P, TB]), sb(name + "_rs", [P, TB]))

        lns = [stats_tiles(f"ln{n}") for n in range(4)]

        REGION = 8704
        region = sb("region", [P, REGION])
        at = [0]

        def view(words, dt=F32):
            v = region[:, at[0]:at[0] + words]
            at[0] += words
            assert at[0] <= REGION
            return v if dt == F32 else v.bitcast(dt)

        Qs, Ks = [], []
        for s in range(2):
            Qs.append(view(G * L // 2, BF16).rearrange("p (h t) -> p h t", h=G))
            Ks.append(view(G * L // 2, BF16).rearrange("p (h t) -> p h t", h=G))
        probs = view(G * L).rearrange("p (h t) -> p h t", h=G)
        oT = view(L)
        otok = view(TB * D).rearrange("p (t f) -> p t f", t=TB)
        aoT = view(KT * L).rearrange("p (k t) -> p k t", k=KT)
        at[0] = 0
        gT = view(FT * L).rearrange("p (f t) -> p f t", f=FT)
        h2T = view(KT * L).rearrange("p (k t) -> p k t", k=KT)
        nrm = view(TB * D).rearrange("p (t f) -> p t f", t=TB)
        xr = view(TB * D).rearrange("p (t f) -> p t f", t=TB)
        ax = view(TB * E * LR).rearrange("p (t f) -> p t f", t=TB)
        axT = view(L)
        mod_g = view(2 * D).rearrange("p (a f) -> p a f", a=2)
        at[0] = 0
        c_raw = view(D)
        cT = view(KT * 32).rearrange("p (k b) -> p k b", k=KT)
        w_mod = view(KT * 6 * D).rearrange("p (k n) -> p k n", k=KT)
        base_raw = view(KT * D).rearrange("p (o k) -> p o k", o=KT)
        rt_raw = view(D)
        mods = view(6 * D)
        alpha = view(D)
        nalpha = view(D)
        mod_t = view(2 * KT * 32).rearrange("p (b c) -> p b c", c=2 * KT)
        ones_b = view(G * L // 2, BF16)
        sgn = view(D)
        mag = view(D)

        held = sb("held", [P, 1])
        x1 = sb("x1", [P, TB, D])
        mod_f = sb("mod_f", [P, 2 * KT])
        mx = sb("mx", [P, 2, 16])
        nmx = sb("nmx", [P, P])
        mrow = sb("mrow", [16, 2, P], BF16)
        rden = sb("rden", [P, TB, G])
        lg = sb("lg", [P, TB, E])
        top = sb("top", [P, TB, 8])
        keep = sb("keep", [P, TB, E])
        ew = sb("ew", [P, TB, E])
        esum = sb("esum", [P, TB])

        pY = [pb(f"pY{t}") for t in range(TB)]
        pM = pb("pM")
        pS = pb("pS")
        pT = pb("pT")
        pO = pb("pO")

        w_loaded = sem("w_loaded")
        built = sem("built")
        pool_c, dve_c, act_c, pe_c = sem("pool_c"), sem("dve_c"), sem("act_c"), sem("pe_c")
        mod_stored, ones_stored = sem("mod_stored"), sem("ones_stored")
        x_in, moda_in = sig("x_in", 16), sig("moda_in", 16)
        bn = [sig(f"bn{n}", TB) for n in range(4)]
        mv = [sig(f"mv{n}", TB) for n in range(4)]
        ve = [sig(f"ve{n}", 1) for n in range(4)]
        rs = [sig(f"rs{n}", 1) for n in range(4)]
        n0 = sig("n0", TB)
        h_made = sig("h_made", 3)
        hres_out = sig("hres_out", 16)
        n1 = sig("n1", TB)
        xt_ps, xt_ok = sig("xt_ps", KT), sig("xt_ok", KT)
        qk_ps, qk_f, qk_s, qk_out = sig("qk_ps", 4), sig("qk_f", 4), sig("qk_s", 16), sig("qk_out", 64)
        v_ps, v_ok = sig("v_ps", 2), sig("v_ok", 2)
        xs_ps, xs_a, xs_c, xc_ok = sig("xs_ps", J), sig("xs_a", J), sig("xs_c", 3 * J), sig("xc_ok", 1)
        xp_ps, xp_ok, bc_out = sig("xp_ps", 1), sig("xp_ok", 1), sig("bc_out", 16)
        dt_ps, dt_x, dt_m, dt_e, dt_ok, u_ok = (sig("dt_ps", J), sig("dt_x", J), sig("dt_m", 1),
                                                sig("dt_e", 2), sig("dt_ok", 1), sig("u_ok", 1))
        xd_ok, d_done = sig("xd_ok", J), sig("d_done", 1)
        bc_in = [sem(f"bc_in{s}") for s in range(BC_SLOTS)]
        a_ok, b_ok, s_ok, p_ok, y_ok = (sig("a_ok", UNITS * JP), sig("b_ok", UNITS), sig("s_ok", UNITS),
                                        sig("p_ok", UNITS), sig("y_ok", UNITS))
        z_ps, z_raw, z_ok = sig("z_ps", TB), sig("z_raw", TB), sig("z_ok", 1)
        qks_in = [sig(f"qks_in{s}", 2 * (2 * TERMS + 1) * 16) for s in range(2)]
        s_ps, s_free, mx_ok = sig("s_ps", 12 * NG), sig("s_free", 11 * NG), sig("mx_ok", NG)
        nm_ok, mr_ok, mrow_in = sig("nm_ok", NG), sig("mr_ok", 2 * NG), sig("mrow_in", 32 * NG)
        t_ps, p_exp, pv_ok = sig("t_ps", H * TB), sig("p_exp", H * TB), sig("pv_ok", H * TB)
        o_ev, ot_ps, rd_ok, on_ok = sig("o_ev", NG), sig("ot_ps", NG), sig("rd_ok", NG), sig("on_ok", NG)
        at_ps, at_ok, op_ps, x1p_in, x1p_ok = (sig("at_ps", KT), sig("at_ok", KT), sig("op_ps", 2),
                                               sig("x1p_in", 16), sig("x1p_ok", 2))
        gated = sig("gated", TB)
        yt_ps, yt_ok, so_ps, x1_ok = sig("yt_ps", J), sig("yt_ok", J), sig("so_ps", 2), sig("x1_ok", 2)
        n2, h2_ps, h2_ok, x1b = sig("n2", TB), sig("h2_ps", KT), sig("h2_ok", KT), sig("x1b", 1)
        f1_ps, f1_raw, g_ok = sig("f1_ps", FT), sig("f1_raw", FT), sig("g_ok", 1)
        f2_ps, r_ok = sig("f2_ps", 2), sig("r_ok", 2)
        xr_in, modg_in, modf_in, x2_ok = sig("xr_in", 16), sig("modg_in", 32), sig("modf_in", 16), sig("x2_ok", 2)
        n3, h3_ps, h3_ok = sig("n3", TB), sig("h3_ps", KT), sig("h3_ok", KT)
        rt_ps, rt_c, ex_ok, ew_ok = sig("rt_ps", 1), sig("rt_c", 7), sig("ex_ok", 1), sig("ew_ok", 4)
        la_ps, ax_ok, axt_ps, axt_ok = sig("la_ps", 1), sig("ax_ok", 1), sig("axt_ps", 1), sig("axt_ok", 1)
        out_ps, o_sum, o_gb, o_fin, out_done = (sig("out_ps", 2), sig("o_sum", 2), sig("o_gb", 1),
                                                sig("o_fin", 1), sig("out_done", 16))

        block = ctx.enter_context(nc.Block())

        def last_of_attention(b, eng):
            b.wait(eng, op_ps)

        def drive(eng, unit, step, banks=()):
            def turn(b, first, last):
                if not first:
                    fin = b.next(-1)
                for k, names in enumerate(SCHEDULE):
                    unit(b, k)
                    for name in names:
                        if name in FIN_SET:
                            if not first:
                                step(name, fin)
                        elif name in PREP_SET:
                            if not last:
                                step(name, b.next(1))
                        else:
                            step(name, b)

            for name in PREP:
                step(name, Batch(None, 0))
            turn(Batch(None, 0), True, False)
            with eng.Fori(0, (B - 2) // 2) as i:
                for bank in banks:
                    bank.into_loop(i)
                turn(Batch(i, 1), False, False)
                turn(Batch(i, 2), False, False)
            for bank in banks:
                bank.out_of_loop(B - 2)
            turn(Batch(None, B - 1), False, True)
            for name in FIN:
                step(name, Batch(None, B - 1))

        def parity(b):
            return b.off % 2

        @block.sync
        def _(sp):
            n_loads = [0]

            def load(dst, src):
                n_loads[0] += 1
                sp.dma_start(dst, src).then_inc(w_loaded, 16)

            sp.wait_ge(built, CLEARED)
            load(c_raw[0:B, :], d["c"])
            load(w_mod, d["wmod"].rearrange("(k p) n -> p k n", p=P))
            load(w_in[:], d["in_proj_w"].rearrange("(k p) n -> p k n", p=P))
            for n, w in enumerate(("q", "k", "v")):
                load(w_qkv[:, n], d[w + "_w"].rearrange("(k p) n -> p k n", p=P))
            load(w_o[:], d["o_w"].rearrange("(k p) n -> p k n", p=P))
            load(w_ssm[:], d["ssm_out_w"].rearrange("(j p) n -> p j n", p=P))
            load(w_f1[:], d["ffn_w1"].rearrange("(k p) n -> p k n", p=P))
            load(w_f2[:], d["ffn_w2"].rearrange("(f p) n -> p f n", p=P))
            load(w_dt[0:R, :], d["dt_w"])
            load(base_raw, d["base_w"].rearrange("(o p) k -> p o k", p=P))
            load(rt_raw[0:E, :], d["router_w"])
            load(w_lb[:], d["lora_B"].rearrange("e r o -> (e r) o"))
            load(A[:], d["A_log"].rearrange("(j p) n -> p j n", p=P))
            load(conv_w[:], d["conv_w"].rearrange("(j p) k -> p j k", p=P))
            for row, name in ((ob_row, "o_b"), (f2b_row, "ffn_b2"), (bb_row, "base_b"), (rb_row, "router_b")):
                load(row[:], d[name].partition_broadcast(P))
            load(alpha, d["mix_weight"].partition_broadcast(P))
            with nc.allow_non_contiguous_dma(reason="small vectors, one element per partition"):
                load(w_xp[:, :, 0:R + 2 * N], d["x_proj_w"].rearrange("(j p) n -> p j n", p=P))
                for k in range(KT):
                    load(w_la[:, k, :].rearrange("p (e r) -> p e r", e=E),
                         d["lora_A"][:, k * P:(k + 1) * P, :].rearrange("e p r -> p e r"))
                load(D_par[:], d["D_param"].rearrange("(j p) -> p j", p=P))
                load(conv_b[:], d["conv_b"].rearrange("(j p) -> p j", p=P))
                load(dt_b[:], d["dt_b"].rearrange("(j p) -> p j", p=P))
                load(f1_b[:], d["ffn_b1"].rearrange("(j p) -> p j", p=P))
                for n, w in enumerate(("w", "b")):
                    load(ln1[:, n], d["ln1_" + w].rearrange("(j p) -> p j", p=P))
                    load(ln2[:, n], d["ln2_" + w].rearrange("(j p) -> p j", p=P))
                for n, w in enumerate(("q", "k", "v")):
                    load(qkv_b[:, n], d[w + "_b"].rearrange("(j p) -> p j", p=P))
            assert n_loads[0] == N_LOADS, n_loads[0]
            sp.wait_ge(dve_c, MODS_DONE)
            sp.dma_start(ones_d.rearrange("o h t -> o (h t)"), ones_b[0:2, :]).then_inc(ones_stored, 16)
            sp.wait_ge(ones_stored, 16)
            sp.dma_start(mod_rows, mods[0:B, :]).then_inc(mod_stored, 16)
            sp.dma_start(mod_cols.rearrange("b p c -> p b c"), mod_t).then_inc(mod_stored, 16)
            sp.wait_ge(mod_stored, 32)

            def bc_row(b, n):
                g = n // BC_SLOTS
                slot = n % BC_SLOTS
                if n >= BC_SLOTS:
                    last = (n - BC_SLOTS + 1) * J // JP
                    b.wait(sp, b_ok, last)
                    b.wait(sp, p_ok, last)
                else:
                    row = N - (N - slot - 1) % BC_SLOTS - 1
                    b.wait_last(sp, b_ok, (row + 1) * J // JP)
                    b.wait_last(sp, p_ok, (row + 1) * J // JP)
                if n == 0:
                    b.wait(sp, bc_out)
                src = bc_d[b.index].rearrange("(a n) t -> n a t", a=2)[n]
                sp.dma_start(bc[:, slot], src.partition_broadcast(P)).then_inc(bc_in[slot], 16)

            def unit(b, k):
                if k == 0:
                    for n in range(BC_SLOTS):
                        bc_row(b, n)
                elif k % (J // JP) == 0:
                    n = k // (J // JP) + BC_SLOTS - 1
                    if n < N:
                        bc_row(b, n)

            def step(name, b):
                if name == "load":
                    b.wait_last(sp, hres_out)
                    b.wait_last(sp, h_made)
                    sp.dma_start(xt[:], d["x"][b.index].rearrange("(t p) f -> p t f", p=P)).then_inc(x_in.sem, 16)
                    sp.dma_start(mod_a[:].rearrange("p a f -> p (a f)"),
                                 mod_rows[b.index, 0:2 * D].partition_broadcast(P)).then_inc(moda_in.sem, 16)
                elif name == "l1a":
                    b.wait(sp, h_made)
                    sp.dma_start(hres_d[b.index].rearrange("(t p) f -> p t f", p=P), xt[:]).then_inc(hres_out.sem, 16)
                elif name[:2] == "qk":
                    n = int(name[2])
                    b.wait(sp, qk_s, 4 * n + 4)
                    sp.dma_start(qk_d[b.index, n // 2, :, (n % 2) * P:(n % 2 + 1) * P].rearrange("c p t -> p c t"),
                                 qkp[:]).then_inc(qk_out.sem, 16)
                elif name == "xp":
                    b.wait(sp, xp_ok)
                    sp.dma_start(bc_d[b.index], dbc[R:R + 2 * N, :]).then_inc(bc_out.sem, 16)
                elif name[:2] == "ld":
                    g = int(name[2])
                    s = g % 2
                    if g == 0:
                        b.wait(sp, qk_out)
                        b.wait_last(sp, o_fin)
                    if g >= 2:
                        b.wait(sp, t_ps, (g - 1) * G * TB)
                    for op, tiles, parts in ((0, Qs, Q_PART), (1, Ks, K_PART)):
                        for c, part in enumerate(parts):
                            src = qk_d[b.index, op, part].rearrange("(h r) t -> r h t", r=HD)[:, g * G:(g + 1) * G, :]
                            sp.dma_start(tiles[s][c * HD:(c + 1) * HD], src).then_inc(qks_in[s].sem, 16)
                    sp.dma_start(Ks[s][QK_ROWS:QK_ROWS + 2], ones_d).then_inc(qks_in[s].sem, 16)
                elif name[:2] == "mt":
                    g = int(name[2])
                    b.wait(sp, mr_ok, 2 * g + 2)
                    for part in range(2):
                        dst = Qs[g % 2][QK_ROWS + part:QK_ROWS + part + 1].rearrange("o h (q p) -> o (h q) p", p=P)
                        sp.dma_start(dst, mrow[:, part, :]).then_inc(mrow_in.sem, 16)
                elif name == "ot0":
                    b.wait_last(sp, x2_ok, 1)
                    b.wait(sp, hres_out)
                    sp.dma_start(x1[:], hres_d[b.index].rearrange("(t p) f -> p t f", p=P)).then_inc(x1p_in.sem, 16)
                elif name == "gate":
                    last_of_attention(b, sp)
                    b.wait(sp, at_ok)
                    b.wait_last(sp, o_fin)
                    b.wait_last(sp, h3_ok)
                    sp.dma_start(xr, d["x"][b.index].rearrange("(t p) f -> p t f", p=P)).then_inc(xr_in.sem, 16)
                    for a, col in ((0, 2), (1, 5)):
                        sp.dma_start(mod_g[:, a], mod_rows[b.index, col * D:(col + 1) * D].partition_broadcast(P))\
                          .then_inc(modg_in.sem, 16)
                    sp.dma_start(mod_f[:], mod_cols[b.index]).then_inc(modf_in.sem, 16)
                elif name == "put":
                    b.wait(sp, o_fin)
                    sp.dma_start(out[b.index].rearrange("(t p) f -> p t f", p=P), nrm).then_inc(out_done.sem, 16)

            drive(sp, unit, step)
            sp.wait_ge(out_done.sem, 16 * B)
            sp.wait_ge(hres_out.sem, 16 * B)
            sp.wait_ge(qk_out.sem, 64 * B)
            sp.wait_ge(bc_out.sem, 16 * B)

        @block.gpsimd
        def _(pool):
            count = [0]

            def link(ins):
                count[0] += 1
                ins.then_inc(pool_c, 1)
                pool.wait_ge(pool_c, count[0])

            for tile, value in ((c_raw, 0.0), (rt_raw, 0.0), (w_xp[:], 0.0), (w_dt[:], 0.0)):
                nc.gpsimd.memset(tile, value).then_inc(built, 1)
            nc.gpsimd.memset(eps4[:], EPS).then_inc(built, 1)
            nc.gpsimd.memset(mhalf4[:], -0.5).then_inc(built, 1)
            nc.gpsimd.memset(decay[:], 0.0).then_inc(built, 1)
            nc.gpsimd.memset(vt[:], 1.0).then_inc(built, 1)
            nc.gpsimd.memset(nmx[:], 0.0).then_inc(built, 1)
            nc.gpsimd.memset(ones_b, 1.0).then_inc(built, 1)
            link(nc.gpsimd.memset(ident[:], 0.0))
            nc.gpsimd.affine_select(out=ident[:], in_=ident[:], compare_op=ALU.not_equal, fill=1.0,
                                    base=0, pattern=[[-1, P]], channel_multiplier=1).then_inc(built, 1)
            m0, m1 = aoT[:, 0, 0:P], aoT[:, 1, 0:P]
            link(nc.gpsimd.memset(aoT, 0.0))
            nc.gpsimd.affine_select(out=m0, in_=m0, compare_op=ALU.is_ge, fill=MASKED,
                                    base=0, pattern=[[-1, P]], channel_multiplier=1).then_inc(built, 1)
            nc.gpsimd.affine_select(out=m1, in_=m1, compare_op=ALU.is_ge, fill=MASKED,
                                    base=0, pattern=[[1, P]], channel_multiplier=-1).then_inc(built, 1)

            def rstd(b, n):
                b.wait(pool, mv[n])
                nc.gpsimd.tensor_tensor(lns[n][2][:], lns[n][1][:, :, 1], eps4[:], ALU.add).then_inc(ve[n].sem, 1)
                b.wait(pool, ve[n])
                nc.gpsimd.tensor_tensor(lns[n][3][:], lns[n][2][:], mhalf4[:], ALU.pow).then_inc(rs[n].sem, 1)

            def row(ap):
                return ap.unsqueeze(1).broadcast_to([P, TB, D])

            def unit(b, k):
                n, jp = k // (J // JP), k % (J // JP)
                if k == 0:
                    b.wait(pool, u_ok)
                if jp == 0:
                    slot = n % BC_SLOTS
                    per = len(range(slot, N, BC_SLOTS))
                    b.wait(pool, Signal(bc_in[slot], 16 * per), 16 * (n // BC_SLOTS + 1))
                if k >= RING:
                    b.wait(pool, y_ok, k - RING + 1)
                else:
                    b.wait_last(pool, y_ok, UNITS + k - RING + 1)
                par = parity(b)
                nc.gpsimd.tensor_tensor(state[:, k % RING], us[:, par, jp * JP:(jp + 1) * JP, :],
                                        bc[:, n % BC_SLOTS, 0, :].unsqueeze(1).broadcast_to([P, JP, L]),
                                        ALU.mult).then_inc(b_ok.sem, 1)

            def step(name, b):
                if name == "l0s":
                    rstd(b, 0)
                elif name == "l0a":
                    b.wait(pool, n0)
                    b.wait(pool, moda_in)
                    b.wait_last(pool, xt_ps)
                    nc.gpsimd.tensor_tensor(ht[:], xt[:], row(mod_a[:, 1, :]), ALU.mult).then_inc(h_made.sem, 1)
                    b.wait(pool, h_made, 1)
                    nc.gpsimd.tensor_tensor(ht[:], ht[:], row(mod_a[:, 0, :]), ALU.add).then_inc(h_made.sem, 1)
                    b.wait(pool, h_made, 2)
                    nc.gpsimd.tensor_tensor(xt[:], ht[:], row(ob_row[:]), ALU.add).then_inc(h_made.sem, 1)
                elif name == "l1a":
                    rstd(b, 1)
                elif name == "u":
                    par = parity(b)
                    b.wait(pool, dt_ok)
                    nc.gpsimd.tensor_tensor(us[:, par], dts[:, par], xc[:], ALU.mult).then_inc(u_ok.sem, 1)
                elif name == "l2s":
                    rstd(b, 2)
                elif name == "f1_0":
                    b.wait(pool, n2)
                    nc.gpsimd.tensor_tensor(x1[:], x1[:], row(f2b_row[:]), ALU.add).then_inc(x1b.sem, 1)
                elif name == "x2":
                    b.wait(pool, r_ok)
                    b.wait(pool, modg_in)
                    b.wait(pool, xr_in)
                    nc.gpsimd.tensor_tensor(nrm, x1[:], row(mod_g[:, 0, :]), ALU.mult).then_inc(x2_ok.sem, 1)
                    b.wait(pool, x2_ok, 1)
                    nc.gpsimd.tensor_tensor(xr, xr, nrm, ALU.add).then_inc(x2_ok.sem, 1)
                elif name == "l3a":
                    rstd(b, 3)
                elif name == "put":
                    b.wait(pool, o_sum)
                    nc.gpsimd.tensor_tensor(nrm, nrm, row(mod_g[:, 1, :]), ALU.mult).then_inc(o_gb.sem, 1)
                    b.wait(pool, o_gb)
                    nc.gpsimd.tensor_tensor(nrm, nrm, xr, ALU.add).then_inc(o_fin.sem, 1)

            pool.wait_ge(built, BUILT)
            drive(pool, unit, step)

        @block.scalar
        def _(act):
            act.wait_ge(w_loaded, 16 * N_LOADS)
            act.activation(alpha, alpha, ACT.Sigmoid).then_inc(act_c, 1)
            act.activation(A[:], A[:], ACT.Exp).then_inc(act_c, 1)
            act.activation(c_raw, c_raw, ACT.Silu).then_inc(act_c, 1)
            act.wait_ge(act_c, 3)
            act.activation(A[:], A[:], ACT.Copy, scale=-1.0).then_inc(act_c, 1)
            act.wait_ge(built, BUILT)
            act.wait_ge(act_c, 4)

            def unit(b, k):
                n, jp = k // (J // JP), k % (J // JP)
                par = parity(b)
                if k == 0:
                    b.wait(act, dt_ok)
                if k >= AR:
                    b.wait(act, s_ok, k - AR + 1)
                else:
                    b.wait_last(act, s_ok, UNITS + k - AR + 1)
                for jj in range(JP):
                    j = jp * JP + jj
                    act.activation(decay[:, k % AR, jj, 1:L], dts[:, par, j, 1:L], ACT.Exp,
                                   scale=A[:, j, n:n + 1]).then_inc(a_ok.sem, 1)

            def step(name, b):
                if name[:2] == "xt":
                    k = int(name[2])
                    b.wait(act, xt_ps, k + 1)
                    if k == 0:
                        b.wait_last(act, z_ps)
                        b.wait_last(act, xs_ps)
                        b.wait_last(act, v_ps)
                    act.activation(xnT[:, k], pM[:], ACT.Identity, scale=ln1[:, 0, k:k + 1],
                                   bias=ln1[:, 1, k:k + 1]).then_inc(xt_ok.sem, 1)
                elif name[:2] == "qk":
                    n = int(name[2])
                    b.wait(act, qk_ps, n + 1)
                    if n:
                        b.wait(act, qk_s, 4 * n)
                    else:
                        b.wait_last(act, qk_s)
                    act.activation(qkf[:], pM[:], ACT.Identity, bias=qkv_b[:, n // 2, n % 2:n % 2 + 1])\
                       .then_inc(qk_f.sem, 1)
                elif name[0] == "v":
                    n = int(name[1])
                    b.wait(act, v_ps, n + 1)
                    b.wait_last(act, pv_ok)
                    act.activation(vt[:, 2 * n:2 * n + 2, :, 0:HD],
                                   pM[:].rearrange("p (t h r) -> p t h r", t=2, h=H),
                                   ACT.Copy).then_inc(v_ok.sem, 1)
                elif name[:3] in ("xs0", "xs1", "xs2", "xs3"):
                    j = int(name[2])
                    b.wait(act, xs_ps, j + 1)
                    b.wait_last(act, d_done)
                    act.activation(xc[:, j], pM[:], ACT.Identity, scale=conv_w[:, j, K_CONV - 1:K_CONV],
                                   bias=conv_b[:, j:j + 1]).then_inc(xs_a.sem, 1)
                elif name == "xsilu":
                    b.wait(act, xs_c)
                    act.activation(xc[:], xc[:], ACT.Silu).then_inc(xc_ok.sem, 1)
                elif name == "xp":
                    b.wait(act, xp_ps)
                    b.wait_last(act, bc_out)
                    b.wait_last(act, dt_ps)
                    act.activation(dbc[:], pM[:], ACT.Copy).then_inc(xp_ok.sem, 1)
                elif name[:2] == "dt":
                    j = int(name[2])
                    b.wait(act, dt_ps, j + 1)
                    if not (b.reg is None and b.off < 2):
                        b.next(-2).wait(act, b_ok)
                    act.activation(us[:, parity(b), j], pM[:], ACT.Identity, bias=dt_b[:, j:j + 1])\
                       .then_inc(dt_x.sem, 1)
                elif name == "sp":
                    par = parity(b)
                    b.wait(act, dt_m)
                    act.activation(dts[:, par], dts[:, par], ACT.Exp).then_inc(dt_e.sem, 1)
                    b.wait(act, dt_e, 1)
                    act.activation(dts[:, par], dts[:, par], ACT.Ln, bias=1.0).then_inc(dt_e.sem, 1)
                elif name in ("z0", "z1", "z2", "z3"):
                    n = int(name[1])
                    b.wait(act, z_ps, n + 1)
                    b.wait_last(act, yt_ps)
                    act.activation(zs[:, n], pM[:], ACT.Copy).then_inc(z_raw.sem, 1)
                elif name == "zsilu":
                    b.wait(act, z_raw)
                    act.activation(zs[:], zs[:], ACT.Silu).then_inc(z_ok.sem, 1)
                elif name[:2] == "st":
                    g, kb = int(name[2]), int(name[4])
                    for h in range(G):
                        e = (g * TB + kb) * G + h
                        n = L - kb * P
                        b.wait(act, t_ps, e + 1)
                        if e >= G:
                            b.wait(act, pv_ok, e - G + 1)
                        else:
                            b.wait_last(act, o_fin)
                        act.activation(probs[:, h, 0:n], pT[:, 0:n], ACT.Exp, scale=HD ** -0.5)\
                           .then_inc(p_exp.sem, 1)
                elif name[:2] == "on":
                    g = int(name[2])
                    b.wait(act, pv_ok, (g + 1) * G * TB)
                    if g:
                        b.wait(act, ot_ps, g)
                    else:
                        b.wait_last(act, o_fin)
                    act.activation(oT, pO[:], ACT.Copy).then_inc(o_ev.sem, 1)
                elif name[:2] == "ot":
                    k = int(name[2])
                    b.wait(act, at_ps, k + 1)
                    act.activation(aoT[:, k], pM[:], ACT.Identity, bias=qkv_b[:, 2, k:k + 1])\
                       .then_inc(at_ok.sem, 1)
                elif name[:2] == "yt":
                    j = int(name[2])
                    b.wait(act, yt_ps, j + 1)
                    b.wait_last(act, so_ps)
                    act.activation(ygT[:, j], pM[:], ACT.Copy).then_inc(yt_ok.sem, 1)
                elif name[:3] == "h2t":
                    k = int(name[3])
                    b.wait(act, h2_ps, k + 1)
                    act.activation(h2T[:, k], pM[:], ACT.Identity, scale=ln2[:, 0, k:k + 1],
                                   bias=ln2[:, 1, k:k + 1]).then_inc(h2_ok.sem, 1)
                elif name[:3] == "f1_":
                    f = int(name[3])
                    b.wait(act, f1_ps, f + 1)
                    act.activation(gT[:, f], pM[:], ACT.Identity, bias=f1_b[:, f:f + 1])\
                       .then_inc(f1_raw.sem, 1)
                elif name == "gelu":
                    b.wait(act, f1_raw)
                    act.activation(gT, gT, ACT.Gelu).then_inc(g_ok.sem, 1)
                elif name[:3] == "h3t":
                    k = int(name[3])
                    b.wait(act, h3_ps, k + 1)
                    b.wait(act, modf_in)
                    act.activation(h2T[:, k], pM[:], ACT.Identity, scale=mod_f[:, KT + k:KT + k + 1],
                                   bias=mod_f[:, k:k + 1]).then_inc(h3_ok.sem, 1)
                elif name == "route2":
                    b.wait(act, rt_c)
                    act.activation(ew[:], lg[:], ACT.Exp).then_inc(ex_ok.sem, 1)
                elif name == "axt":
                    b.wait(act, axt_ps)
                    act.activation(axT, pM[:], ACT.Copy).then_inc(axt_ok.sem, 1)

            drive(act, unit, step)

        @block.tensor
        def _(pe):
            pe.wait_ge(w_loaded, 16 * N_LOADS)
            pe.wait_ge(built, BUILT)
            pe.wait_ge(act_c, 3)
            n_pe = [0]

            def done(ins, read_by):
                n_pe[0] += 1
                ins.then_inc(pe_c, 1)
                pe.wait_ge(dve_c, read_by)

            for k in range(KT):
                t = pe.transpose(pM[:, k * P:(k + 1) * P], c_raw[:, k * P:(k + 1) * P], ident[:])
            done(t, 1)
            for n in range(3):
                for k in range(KT):
                    t = pe.matmul(pM[0:B, :], cT[:, k, :], w_mod[:, k, n * 512:(n + 1) * 512],
                                  start=(k == 0), stop=(k == KT - 1))
                done(t, 2 + n)
            for o in range(KT):
                for k in range(KT):
                    t = pe.transpose(pM[:, (o * KT + k) * P:(o * KT + k + 1) * P],
                                     base_raw[:, o, k * P:(k + 1) * P], ident[:])
            done(t, 5)
            for k in range(KT):
                t = pe.transpose(pM[:, k * P:(k + 1) * P], rt_raw[:, k * P:(k + 1) * P], ident[:])
            done(t, 6)
            pe.wait_ge(dve_c, MODS_READY)
            for c in range(2 * KT):
                t = pe.transpose(pM[:, c * P:(c + 1) * P], mods[:, 3 * D + c * P:3 * D + (c + 1) * P], ident[:])
            done(t, MODS_DONE)
            pe.wait_ge(dve_c, DVE_SETUP)

            bank = Bank()

            def unit(b, k):
                if k == 0:
                    b.wait(pe, xd_ok)
                    b.wait_last(pe, gated)
                    for j in range(J):
                        for t in range(TB):
                            ins = pe.matmul(pY[t][:, j * P:(j + 1) * P], xc[:, j, t * P:(t + 1) * P], ident[:],
                                            is_transpose=True, start=(j == 0), stop=False, skip_group_check=True)
                    ins.then_inc(d_done.sem, 1)
                if k == UNITS - 1:
                    adds = (k - 1, k)
                elif k == 0:
                    adds = ()
                else:
                    adds = (k - 1,)
                for a in adds:
                    b.wait(pe, p_ok, a + 1)
                    for jj in range(JP):
                        j = (a % (J // JP)) * JP + jj
                        for t in range(TB):
                            ins = pe.matmul(pY[t][:, j * P:(j + 1) * P], state[:, a % RING, jj, t * P:(t + 1) * P],
                                            ident[:], is_transpose=True, start=False,
                                            stop=(a >= UNITS - J // JP), skip_group_check=True)
                    ins.then_inc(y_ok.sem, 1)

            def turned(src, sig_, b, freed_by, n):
                bank.fill(pe, b, freed_by, n)
                for t in range(TB):
                    ins = pe.transpose(pM[:, t * P:(t + 1) * P], src(t), ident[:])
                ins.then_inc(sig_.sem, 1)

            def step(name, b):
                if name[:2] == "xt":
                    k = int(name[2])
                    b.wait(pe, n1)
                    turned(lambda t: ht[:, t, k * P:(k + 1) * P], xt_ps, b, xt_ok, k + 1)
                elif name[:2] == "qk":
                    n = int(name[2])
                    b.wait(pe, xt_ok)
                    bank.fill(pe, b, qk_f, n + 1)
                    for k in range(KT):
                        ins = pe.matmul(pM[:], w_qkv[:, n // 2, k, (n % 2) * P:(n % 2 + 1) * P], xnT[:, k],
                                        start=(k == 0), stop=(k == KT - 1))
                    ins.then_inc(qk_ps.sem, 1)
                elif name[0] == "v":
                    n = int(name[1])
                    bank.fill(pe, b, v_ok, n + 1)
                    for t in range(2):
                        for k in range(KT):
                            ins = pe.matmul(pM[:, t * D:(t + 1) * D], xnT[:, k, (2 * n + t) * P:(2 * n + t + 1) * P],
                                            w_qkv[:, 2, k, :], start=(k == 0), stop=(k == KT - 1))
                    ins.then_inc(v_ps.sem, 1)
                elif name in ("xs0", "xs1", "xs2", "xs3"):
                    j = int(name[2])
                    bank.fill(pe, b, xs_c, 3 * j + 3)
                    for k in range(KT):
                        ins = pe.matmul(pM[:], w_in[:, k, j * P:(j + 1) * P], xnT[:, k],
                                        start=(k == 0), stop=(k == KT - 1))
                    ins.then_inc(xs_ps.sem, 1)
                elif name == "xp":
                    b.wait(pe, xc_ok)
                    bank.fill(pe, b, xp_ok, 1)
                    for j in range(J):
                        ins = pe.matmul(pM[:], w_xp[:, j, :], xc[:, j], start=(j == 0), stop=(j == J - 1))
                    ins.then_inc(xp_ps.sem, 1)
                elif name[:2] == "dt":
                    j = int(name[2])
                    b.wait(pe, xp_ok)
                    bank.fill(pe, b, dt_x, j + 1)
                    pe.matmul(pM[:], w_dt[:, j * P:(j + 1) * P], dbc[:], start=True, stop=True)\
                      .then_inc(dt_ps.sem, 1)
                elif name in ("z0", "z1", "z2", "z3"):
                    n = int(name[1])
                    b.wait(pe, xt_ok)
                    bank.fill(pe, b, z_raw, n + 1)
                    for k in range(KT):
                        ins = pe.matmul(pM[:], xnT[:, k, n * P:(n + 1) * P], w_in[:, k, DI:2 * DI],
                                        start=(k == 0), stop=(k == KT - 1))
                    ins.then_inc(z_ps.sem, 1)
                elif name[:2] == "mx":
                    g = int(name[2])
                    q, kk = Qs[g % 2], Ks[g % 2]
                    b.wait(pe, qks_in[g % 2], (g // 2 + 1) * (2 * TERMS + 1) * 16)
                    e = 11 * g
                    if g:
                        b.wait(pe, mr_ok, 2 * g)
                    else:
                        b.wait_last(pe, mr_ok)
                    for qb, heads in MAX_FILLS:
                        n = (qb + 1) * P
                        if e > 11 * g:
                            b.wait(pe, s_free, e)
                        for s, h in enumerate(heads):
                            pe.matmul(pS[:, s * n:(s + 1) * n], q[0:QK_ROWS, h, qb * P:(qb + 1) * P],
                                      kk[0:QK_ROWS, h, 0:n], start=True, stop=False, skip_group_check=True)
                            ins = pe.matmul(pS[:, (s + 1) * n - P:(s + 1) * n], identb[:], mask_qk[:],
                                            start=False, stop=True, skip_group_check=True)
                        ins.then_inc(s_ps.sem, 1)
                        e += 1
                elif name[:2] == "mt":
                    g = int(name[2])
                    b.wait(pe, nm_ok, g + 1)
                    b.wait(pe, s_free, 11 * g + 11)
                    pe.transpose(pS[:, 0:P], nmx[:], ident[:]).then_inc(s_ps.sem, 1)
                elif name[:2] == "st":
                    g, kb = int(name[2]), int(name[4])
                    q, kk = Qs[g % 2], Ks[g % 2]
                    if kb == 0:
                        b.wait(pe, mrow_in, 32 * (g + 1))
                        b.wait(pe, v_ok)
                    for h in range(G):
                        e = (g * TB + kb) * G + h
                        if e:
                            b.wait(pe, p_exp, e)
                        else:
                            b.wait_last(pe, p_exp)
                        n = L - kb * P
                        pe.matmul(pT[:, 0:n], kk[0:QK_ROWS + 2, h, kb * P:(kb + 1) * P],
                                  q[0:QK_ROWS + 2, h, kb * P:L], start=True, stop=False, skip_group_check=True)
                        pe.matmul(pT[:, 0:P], identb[:], mask_kq[:], start=False, stop=True,
                                  skip_group_check=True).then_inc(t_ps.sem, 1)
                    for h in range(G):
                        e = (g * TB + kb) * G + h
                        n = L - kb * P
                        b.wait(pe, p_exp, e + 1)
                        if e == g * TB * G:
                            if g:
                                b.wait(pe, o_ev, g)
                            else:
                                b.wait_last(pe, o_ev)
                        pe.matmul(pO[32 * h:32 * h + HD + 1, kb * P:L], vt[:, kb, g * G + h, :],
                                  probs[:, h, 0:n], start=(kb == 0), stop=(kb == TB - 1),
                                  skip_group_check=True).then_inc(pv_ok.sem, 1)
                elif name[:2] == "on":
                    g = int(name[2])
                    b.wait(pe, o_ev, g + 1)
                    turned(lambda t: oT[:, t * P:(t + 1) * P], ot_ps, b, on_ok, g + 1)
                elif name[:2] == "ot":
                    k = int(name[2])
                    b.wait(pe, on_ok)
                    turned(lambda t: otok[:, t, k * P:(k + 1) * P], at_ps, b, at_ok, k + 1)
                elif name[:2] == "op":
                    n = int(name[2])
                    b.wait(pe, at_ok)
                    bank.fill(pe, b, x1p_ok, n + 1)
                    for t in range(2):
                        for k in range(KT):
                            ins = pe.matmul(pM[:, t * D:(t + 1) * D], aoT[:, k, (2 * n + t) * P:(2 * n + t + 1) * P],
                                            w_o[:, k, :], start=(k == 0), stop=(k == KT - 1))
                    ins.then_inc(op_ps.sem, 1)
                elif name[:2] == "yt":
                    j = int(name[2])
                    b.wait(pe, gated)
                    turned(lambda t: zs[:, t, j * P:(j + 1) * P], yt_ps, b, yt_ok, j + 1)
                elif name[:3] == "sso":
                    n = int(name[3])
                    b.wait(pe, yt_ok)
                    bank.fill(pe, b, x1_ok, n + 1)
                    for t in range(2):
                        for j in range(J):
                            ins = pe.matmul(pM[:, t * D:(t + 1) * D], ygT[:, j, (2 * n + t) * P:(2 * n + t + 1) * P],
                                            w_ssm[:, j, :], start=(j == 0), stop=(j == J - 1))
                    ins.then_inc(so_ps.sem, 1)
                elif name[:3] == "h2t":
                    k = int(name[3])
                    b.wait(pe, n2)
                    turned(lambda t: nrm[:, t, k * P:(k + 1) * P], h2_ps, b, h2_ok, k + 1)
                elif name[:3] == "f1_":
                    f = int(name[3])
                    b.wait(pe, h2_ok)
                    bank.fill(pe, b, f1_raw, f + 1)
                    for k in range(KT):
                        ins = pe.matmul(pM[:], w_f1[:, k, f * P:(f + 1) * P], h2T[:, k],
                                        start=(k == 0), stop=(k == KT - 1))
                    ins.then_inc(f1_ps.sem, 1)
                elif name[:3] == "f2_":
                    n = int(name[3])
                    b.wait(pe, g_ok)
                    bank.fill(pe, b, r_ok, n + 1)
                    for t in range(2):
                        for f in range(FT):
                            ins = pe.matmul(pM[:, t * D:(t + 1) * D], gT[:, f, (2 * n + t) * P:(2 * n + t + 1) * P],
                                            w_f2[:, f, :], start=(f == 0), stop=(f == FT - 1))
                    ins.then_inc(f2_ps.sem, 1)
                elif name[:3] == "h3t":
                    k = int(name[3])
                    b.wait(pe, n3)
                    turned(lambda t: nrm[:, t, k * P:(k + 1) * P], h3_ps, b, h3_ok, k + 1)
                elif name == "route":
                    b.wait(pe, h3_ok)
                    bank.fill(pe, b, rt_c, 1)
                    for t in range(TB):
                        for k in range(KT):
                            ins = pe.matmul(pM[:, t * E:(t + 1) * E], h2T[:, k, t * P:(t + 1) * P], w_rt[:, k, :],
                                            start=(k == 0), stop=(k == KT - 1))
                    ins.then_inc(rt_ps.sem, 1)
                elif name == "lora":
                    bank.fill(pe, b, ax_ok, 1)
                    for t in range(TB):
                        for k in range(KT):
                            ins = pe.matmul(pM[:, t * P:(t + 1) * P], h2T[:, k, t * P:(t + 1) * P], w_la[:, k, :],
                                            start=(k == 0), stop=(k == KT - 1))
                    ins.then_inc(la_ps.sem, 1)
                elif name == "axt":
                    b.wait(pe, ax_ok)
                    turned(lambda t: ax[:, t, :], axt_ps, b, axt_ok, 1)
                elif name in ("out0", "out1"):
                    n = int(name[3])
                    b.wait(pe, axt_ok)
                    bank.fill(pe, b, o_sum, n + 1)
                    for t in range(2):
                        tok = slice((2 * n + t) * P, (2 * n + t + 1) * P)
                        for k in range(KT):
                            pe.matmul(pM[:, t * D:(t + 1) * D], h2T[:, k, tok], w_base[:, k, :],
                                      start=(k == 0), stop=False)
                        ins = pe.matmul(pM[:, t * D:(t + 1) * D], axT[:, tok], w_lb[:], start=False, stop=True)
                    ins.then_inc(out_ps.sem, 1)

            drive(pe, unit, step, [bank])

        @block.vector
        def _(dve):
            count = [0]

            def link(ins):
                count[0] += 1
                ins.then_inc(dve_c, 1)
                dve.wait_ge(dve_c, count[0])

            v = nc.vector
            dve.wait_ge(built, BUILT)
            dve.wait_ge(w_loaded, 16 * N_LOADS)
            dve.wait_ge(pe_c, 1)
            link(v.tensor_copy(cT, pM[:].rearrange("p (k b) -> p k b", b=P)[:, 0:KT, 0:B]))
            for n in range(3):
                dve.wait_ge(pe_c, 2 + n)
                link(v.tensor_copy(mods[0:B, n * 512:(n + 1) * 512], pM[0:B, :]))
            dve.wait_ge(pe_c, 5)
            link(v.tensor_copy(w_base[:].rearrange("p k (o q) -> p o k q", o=KT),
                               pM[:].rearrange("p (o k q) -> p o k q", o=KT, k=KT)))
            dve.wait_ge(pe_c, 6)
            link(v.tensor_copy(w_rt[:], pM[:].rearrange("p (k q) -> p k q", q=P)[:, 0:KT, 0:E]))
            for c in (1, 4):
                link(v.tensor_scalar(mods[0:B, c * D:(c + 1) * D], mods[0:B, c * D:(c + 1) * D], 1.0, None, ALU.add))
            for c in (2, 5):
                gate = mods[0:B, c * D:(c + 1) * D]
                link(v.tensor_scalar(sgn[0:B], gate, 0.0, 2.0, ALU.is_ge, ALU.mult))
                link(v.scalar_tensor_tensor(out=mag[0:B], in0=sgn[0:B], scalar=-1.0, in1=gate,
                                            op0=ALU.add, op1=ALU.mult))
                link(v.tensor_scalar(mag[0:B], mag[0:B], 0.25, None, ALU.max))
                link(v.scalar_tensor_tensor(out=gate, in0=sgn[0:B], scalar=-1.0, in1=mag[0:B],
                                            op0=ALU.add, op1=ALU.mult))
            assert count[0] == MODS_READY
            dve.wait_ge(pe_c, 7)
            link(v.tensor_copy(mod_t.rearrange("p b c -> p c b"),
                               pM[:].rearrange("p (c q) -> p c q", q=P)[:, :, 0:B]))
            assert count[0] == MODS_DONE
            link(v.tensor_copy(identb[:], ident[:]))
            link(v.tensor_copy(mask_qk[:], aoT[:, 0, 0:P]))
            link(v.tensor_copy(mask_kq[:], aoT[:, 1, 0:P]))
            dve.wait_ge(act_c, 1)
            link(v.tensor_scalar(nalpha, alpha, -1.0, 1.0, ALU.mult, ALU.add))
            link(v.tensor_tensor(w_o[:], w_o[:], alpha.unsqueeze(1).broadcast_to([P, KT, D]), ALU.mult))
            link(v.tensor_tensor(ob_row[:], ob_row[:], alpha, ALU.mult))
            link(v.tensor_tensor(w_ssm[:], w_ssm[:], nalpha.unsqueeze(1).broadcast_to([P, J, D]), ALU.mult))
            link(v.memset(pO[:], 0.0))
            assert count[0] == DVE_SETUP, count[0]

            def stats(b, n, src):
                st, mvt, _, _ = lns[n]
                for t in range(TB):
                    v.bn_stats(st[:, t, :], src[:, t, :]).then_inc(bn[n].sem, 1)
                b.wait(dve, bn[n])
                v.memset(held[:], 0.0)
                for t in range(TB):
                    v.bn_aggr(mvt[:, t, :], st[:, t, :]).then_inc(mv[n].sem, 1)

            def normalise(b, n, dst, src, sig_):
                _, mvt, _, rst = lns[n]
                b.wait(dve, rs[n])
                for t in range(TB):
                    v.tensor_scalar(dst[:, t, :], src[:, t, :], mvt[:, t, 0:1], rst[:, t:t + 1],
                                    ALU.subtract, ALU.mult).then_inc(sig_.sem, 1)

            def times_c(b, k):
                n = k // (J // JP)
                b.wait(dve, s_ok, k + 1)
                v.tensor_tensor(state[:, k % RING], state[:, k % RING],
                                bc[:, n % BC_SLOTS, 1, :].unsqueeze(1).broadcast_to([P, JP, L]),
                                ALU.mult).then_inc(p_ok.sem, 1)

            def unit(b, k):
                b.wait(dve, a_ok, JP * (k + 1))
                b.wait(dve, b_ok, k + 1)
                v.tensor_tensor_scan(state[:, k % RING].rearrange("p j t -> p (j t)"),
                                     decay[:, k % AR].rearrange("p j t -> p (j t)"),
                                     state[:, k % RING].rearrange("p j t -> p (j t)"),
                                     0.0, ALU.mult, ALU.add).then_inc(s_ok.sem, 1)
                if k:
                    times_c(b, k - 1)
                if k == UNITS - 1:
                    times_c(b, k)

            def step(name, b):
                if name == "l0s":
                    b.wait(dve, x_in)
                    stats(b, 0, xt)
                elif name == "l0a":
                    normalise(b, 0, xt, xt, n0)
                elif name == "l1a":
                    b.wait(dve, h_made, 2)
                    stats(b, 1, ht)
                    b.wait(dve, h_made)
                    normalise(b, 1, ht, ht, n1)
                elif name[:2] == "qk":
                    n = int(name[2])
                    b.wait(dve, qk_f, n + 1)
                    if n:
                        b.wait(dve, qk_out, 16 * n)
                    else:
                        b.wait_last(dve, qk_out)
                    v.tensor_copy(qkp[:, 0], qkf[:]).then_inc(qk_s.sem, 1)
                    b.wait(dve, qk_s, 4 * n + 1)
                    v.tensor_tensor(qkf[:], qkf[:], qkp[:, 0], ALU.subtract).then_inc(qk_s.sem, 1)
                    b.wait(dve, qk_s, 4 * n + 2)
                    v.tensor_copy(qkp[:, 1], qkf[:]).then_inc(qk_s.sem, 1)
                    b.wait(dve, qk_s, 4 * n + 3)
                    v.tensor_tensor(qkp[:, 2], qkf[:], qkp[:, 1], ALU.subtract).then_inc(qk_s.sem, 1)
                elif name in ("xs0", "xs1", "xs2", "xs3"):
                    j = int(name[2])
                    b.wait(dve, xs_a, j + 1)
                    for s in range(1, K_CONV):
                        if s > 1:
                            b.wait(dve, xs_c, 3 * j + s - 1)
                        v.scalar_tensor_tensor(
                            out=xc[:, j, s:L], in0=pM[:, 0:L - s],
                            scalar=conv_w[:, j, K_CONV - 1 - s:K_CONV - s], in1=xc[:, j, s:L],
                            op0=ALU.mult, op1=ALU.add).then_inc(xs_c.sem, 1)
                elif name == "sp":
                    par = parity(b)
                    b.wait(dve, dt_x)
                    v.tensor_scalar(dts[:, par], us[:, par], SOFTPLUS_CAP, None, ALU.min).then_inc(dt_m.sem, 1)
                    b.wait(dve, dt_e)
                    v.tensor_tensor(dts[:, par], dts[:, par], us[:, par], ALU.max).then_inc(dt_ok.sem, 1)
                elif name == "u":
                    b.wait(dve, u_ok)
                    for j in range(J):
                        v.tensor_scalar(xc[:, j], xc[:, j], D_par[:, j:j + 1], None, ALU.mult).then_inc(xd_ok.sem, 1)
                elif name[:2] == "mx":
                    g = int(name[2])
                    if g:
                        b.wait(dve, nm_ok, g)
                    else:
                        b.wait_last(dve, nm_ok)
                    e = 12 * g
                    mxv = mx[:, g % 2].rearrange("p (h q) -> p h q", q=TB)
                    for qb, heads in MAX_FILLS:
                        n = (qb + 1) * P
                        b.wait(dve, s_ps, e + 1)
                        v.tensor_reduce(mxv[:, heads[0]:heads[-1] + 1, qb],
                                        pS[:, 0:len(heads) * n].rearrange("p (h k) -> p h k", k=n),
                                        AX_X, ALU.max).then_inc(s_free.sem, 1)
                        e += 1
                    b.wait(dve, s_free, 11 * g + 11)
                    v.tensor_scalar(nmx[:, 0:16], mx[:, g % 2], -1.0, None, ALU.mult).then_inc(nm_ok.sem, 1)
                elif name[:2] == "mt":
                    g = int(name[2])
                    b.wait(dve, s_ps, 12 * g + 12)
                    if g:
                        b.wait(dve, mrow_in, 32 * g)
                    else:
                        b.wait_last(dve, mrow_in)
                    v.tensor_copy(mrow[:, 0], pS[0:16, 0:P]).then_inc(mr_ok.sem, 1)
                    b.wait(dve, mr_ok, 2 * g + 1)
                    v.tensor_tensor(mrow[:, 1], pS[0:16, 0:P], mrow[:, 0], ALU.subtract)\
                     .then_inc(mr_ok.sem, 1)
                elif name[:2] == "on":
                    g = int(name[2])
                    ps = pM[:].rearrange("p (t h r) -> p t h r", t=TB, r=32)
                    b.wait(dve, ot_ps, g + 1)
                    if g:
                        b.wait(dve, on_ok, g)
                    v.reciprocal(rden[:], ps[:, :, :, HD]).then_inc(rd_ok.sem, 1)
                    b.wait(dve, rd_ok, g + 1)
                    v.tensor_tensor(otok[:, :, g * G * HD:(g + 1) * G * HD].rearrange("p t (h r) -> p t h r", r=HD),
                                    ps[:, :, :, 0:HD], rden[:].unsqueeze(3).broadcast_to([P, TB, G, HD]),
                                    ALU.mult).then_inc(on_ok.sem, 1)
                elif name[:2] == "op":
                    n = int(name[2])
                    b.wait(dve, op_ps, n + 1)
                    b.wait(dve, x1p_in)
                    v.tensor_tensor(x1[:, 2 * n:2 * n + 2], x1[:, 2 * n:2 * n + 2],
                                    pM[:].rearrange("p (t f) -> p t f", t=2), ALU.add)\
                     .then_inc(x1p_ok.sem, 1)
                elif name == "gate":
                    b.wait(dve, y_ok)
                    b.wait(dve, z_ok)
                    for t in range(TB):
                        v.tensor_tensor(zs[:, t], zs[:, t], pY[t][:], ALU.mult).then_inc(gated.sem, 1)
                elif name[:3] == "sso":
                    n = int(name[3])
                    b.wait(dve, so_ps, n + 1)
                    b.wait(dve, x1p_ok)
                    v.tensor_tensor(x1[:, 2 * n:2 * n + 2], x1[:, 2 * n:2 * n + 2],
                                    pM[:].rearrange("p (t f) -> p t f", t=2), ALU.add)\
                     .then_inc(x1_ok.sem, 1)
                elif name == "l2s":
                    b.wait(dve, x1_ok)
                    stats(b, 2, x1)
                elif name == "l2a":
                    last_of_attention(b, dve)
                    b.wait_last(dve, out_done)
                    normalise(b, 2, nrm, x1, n2)
                elif name[:3] == "f2_":
                    n = int(name[3])
                    b.wait(dve, f2_ps, n + 1)
                    b.wait(dve, x1b)
                    v.tensor_tensor(x1[:, 2 * n:2 * n + 2], x1[:, 2 * n:2 * n + 2],
                                    pM[:].rearrange("p (t f) -> p t f", t=2), ALU.add)\
                     .then_inc(r_ok.sem, 1)
                elif name == "l3a":
                    b.wait(dve, x2_ok)
                    stats(b, 3, xr)
                    normalise(b, 3, nrm, xr, n3)
                elif name == "route":
                    b.wait(dve, rt_ps)
                    v.tensor_tensor(lg[:], pM[:, 0:TB * E].rearrange("p (t e) -> p t e", e=E),
                                    rb_row[:].unsqueeze(1).broadcast_to([P, TB, E]), ALU.add)\
                     .then_inc(rt_c.sem, 1)
                    b.wait(dve, rt_c, 1)
                    v.memset(held[:], 0.0)
                    for t in range(TB):
                        v.max(top[:, t, :], lg[:, t, :]).then_inc(rt_c.sem, 1)
                    b.wait(dve, rt_c, 5)
                    v.tensor_tensor(keep[:], lg[:], top[:, :, 1:2].broadcast_to([P, TB, E]), ALU.is_ge)\
                     .then_inc(rt_c.sem, 1)
                    b.wait(dve, rt_c, 6)
                    v.tensor_tensor(lg[:], lg[:], top[:, :, 0:1].broadcast_to([P, TB, E]), ALU.subtract)\
                     .then_inc(rt_c.sem, 1)
                elif name == "route2":
                    b.wait(dve, ex_ok)
                    v.tensor_tensor(ew[:], ew[:], keep[:], ALU.mult).then_inc(ew_ok.sem, 1)
                    b.wait(dve, ew_ok, 1)
                    v.tensor_reduce(esum[:], ew[:], AX_X, ALU.add).then_inc(ew_ok.sem, 1)
                    b.wait(dve, ew_ok, 2)
                    v.reciprocal(esum[:], esum[:]).then_inc(ew_ok.sem, 1)
                    b.wait(dve, ew_ok, 3)
                    v.scalar_tensor_tensor(out=ew[:], in0=ew[:], scalar=LORA_SCALE,
                                           in1=esum[:].unsqueeze(2).broadcast_to([P, TB, E]),
                                           op0=ALU.mult, op1=ALU.mult).then_inc(ew_ok.sem, 1)
                elif name == "lora":
                    b.wait(dve, la_ps)
                    b.wait(dve, ew_ok)
                    v.tensor_tensor(ax.rearrange("p t (e r) -> p t e r", e=E),
                                    pM[:].rearrange("p (t e r) -> p t e r", t=TB, e=E),
                                    ew[:].unsqueeze(3).broadcast_to([P, TB, E, LR]), ALU.mult)\
                     .then_inc(ax_ok.sem, 1)
                elif name in ("out0", "out1"):
                    n = int(name[3])
                    b.wait(dve, out_ps, n + 1)
                    v.tensor_tensor(nrm[:, 2 * n:2 * n + 2], pM[:].rearrange("p (t f) -> p t f", t=2),
                                    bb_row[:].unsqueeze(1).broadcast_to([P, 2, D]), ALU.add)\
                     .then_inc(o_sum.sem, 1)

            drive(dve, unit, step)


MAX_FILLS = ([(3, [h]) for h in range(G)] + [(2, [h]) for h in range(G)]
             + [(1, [0, 1]), (1, [2, 3]), (0, [0, 1, 2, 3])])
N_LOADS = 35
CLEARED = 4
BUILT = 13
MODS_READY = 16
MODS_DONE = MODS_READY + 1
DVE_SETUP = MODS_DONE + 8

FIN_SET, PREP_SET = set(FIN), set(PREP)


def make_schedule():
    slots = [[] for _ in range(UNITS)]

    def spread(names, first, last):
        for n, name in enumerate(names):
            slots[first + n * (last - first) // len(names)].append(name)

    spread(FIN, 0, 18)
    spread(Z, 3, 8)
    spread(PREP, 4, 32)
    spread(ATT, 18, 32)
    return slots


SCHEDULE = make_schedule()

_INS = ["x", "ln1_w", "ln1_b", "ln2_w", "ln2_b", "q_w", "q_b", "k_w", "k_b", "v_w", "v_b", "o_w", "o_b",
        "in_proj_w", "conv_w", "conv_b", "x_proj_w", "dt_w", "dt_b", "A_log", "D_param", "ssm_out_w",
        "mix_weight", "ffn_w1", "ffn_b1", "ffn_w2", "ffn_b2"]
_INS = {**{n: "L0_attn_" + n for n in _INS},
        **{n: "L0_ffn_" + n for n in ("base_w", "base_b", "lora_A", "lora_B", "router_w", "router_b")},
        "c": "L0_c", "wmod": "L0_wmod"}


def kernel(**inputs):
    import numpy as _np
    import concourse.bacc as _bacc
    from concourse import mybir as _mybir
    from concourse.bass_utils import run_bass_kernel_spmd as _run

    nc = _bacc.Bacc("TRN2", target_bir_lowering=False, num_devices=1)
    arrays, args = {}, {}
    for name, full in _INS.items():
        a = _np.ascontiguousarray(inputs[full])
        arrays[f"in_{name}_dram"] = a
        args[name] = nc.dram_tensor(f"in_{name}_dram", a.shape, _mybir.dt.from_np(a.dtype), kind="ExternalInput").ap()
    out = nc.dram_tensor("out_dram", (B, L, D), _mybir.dt.float32, kind="ExternalOutput").ap()
    adaln_block(nc, args, out)
    r = _run(nc, [arrays], core_ids=[0])
    return r.results[0]["out_dram"]
```

```python
from contextlib import ExitStack

import concourse.bass as bass
from concourse import mybir

ALU = mybir.AluOpType
ACT = mybir.ActivationFunctionType
F32 = mybir.dt.float32
BF16 = mybir.dt.bfloat16
AX_X = mybir.AxisListType.X

B, L, D = 32, 512, 256
P = 128
TB = L // P
KT = D // P
H, HD = 16, 16
G = 4
NG = H // G
DI = 2 * D
J = DI // P
N = 16
R = 16
K_CONV = 4
FF = 4 * D
FT = FF // P
E, LR = 8, 16
EPS = 1e-5
LORA_SCALE = 2.0
SOFTPLUS_CAP = 80.0
JP = 2
UNITS = N * J // JP
BANKS = 3
RING = 4
AR = 4
BC_SLOTS = 4
ACT_LEAD = 2
POOL_LEAD = 1
PE_LAG = 2
PE_START = 3
Q_PART = [0, 0, 1, 1, 0, 2]
K_PART = [0, 1, 0, 1, 2, 0]
TERMS = len(Q_PART)
PV_LAG = 2
QK_ROWS = TERMS * HD
MASKED = -1e30

FIN = ["gate", "yt0", "yt1", "yt2", "yt3", "sso0", "sso1", "l2s", "l2a", "h2t0", "h2t1",
       "f1_0", "f1_1", "f1_2", "f1_3", "f1_4", "f1_5", "f1_6", "f1_7", "gelu", "f2_0", "f2_1",
       "x2", "l3a", "h3t0", "h3t1", "route", "route2", "lora", "axt", "out0", "out1", "put"]
Z = ["z0", "z1", "z2", "z3", "zsilu", "v0", "v1"]
ATT = (["ld0", "mx0a", "mx0b", "mx0c", "mt0", "ld1", "mx1a", "mx1b", "mx1c", "mt1"]
       + [f"st0_{k}" for k in range(TB)] + ["on0", "ld2", "mx2a", "mx2b", "mx2c", "mt2"]
       + [f"st1_{k}" for k in range(TB)] + ["on1", "ld3", "mx3a", "mx3b", "mx3c", "mt3"]
       + [f"st2_{k}" for k in range(TB)] + ["on2"]
       + [f"st3_{k}" for k in range(TB)] + ["on3", "ot0", "ot1", "op0", "op1"])
PREP = ["load", "l0s", "l0a", "l1a", "xt0", "xt1", "qk0", "qk1", "qk2", "qk3",
        "xs0", "xs1", "xs2", "xs3", "xsilu", "xp", "dt0", "dt1", "dt2", "dt3", "sp", "u"]


class Signal:

    def __init__(self, sem, per):
        self.sem, self.per = sem, per


class Batch:

    def __init__(self, reg, off):
        self.reg, self.off = reg, off

    @property
    def index(self):
        return self.off if self.reg is None else self.reg * 2 + self.off

    def next(self, n=1):
        return Batch(self.reg, self.off + n)

    def at(self, signal, n=None):
        n = signal.per if n is None else n
        fixed = self.off * signal.per + n
        return fixed if self.reg is None else self.reg * (2 * signal.per) + fixed

    def wait(self, engine, signal, n=None):
        engine.wait_ge(signal.sem, self.at(signal, n))

    def wait_last(self, engine, signal, n=None):
        n = signal.per if n is None else n
        if self.reg is None and self.off == 0:
            return
        engine.wait_ge(signal.sem, self.next(-1).at(signal, n))


class Bank:

    def __init__(self):
        self.last = None

    def fill(self, pe, b, freed_by, n):
        if self.last is not None:
            before, signal, count = self.last
            before.wait(pe, signal, count)
        self.last = b, freed_by, n

    def into_loop(self, reg):
        b, signal, n = self.last
        self.last = Batch(reg, b.off), signal, n
        self.entry = b.off, signal, n

    def out_of_loop(self, turns):
        b, signal, n = self.last
        assert self.entry == (b.off - 2, signal, n)
        self.last = Batch(None, b.off + turns - 2), signal, n


def adaln_block(nc: bass.Bass, d, out):
    ctx = ExitStack()
    with ctx:
        def sb(name, shape, dt=F32):
            return ctx.enter_context(nc.sbuf_tensor(name, shape, dt))

        def pb(name):
            return ctx.enter_context(nc.psum_tensor(name, [P, 512], F32))

        def sem(name):
            return ctx.enter_context(nc.semaphore(name))

        def sig(name, per):
            return Signal(sem(name), per)

        def dram(name, shape, dt=F32):
            return nc.dram_tensor(name, shape, dt).ap()

        mod_rows = dram("mod_rows", (B, 6 * D))
        mod_cols = dram("mod_cols", (B, P, 2 * KT))
        hres_d = dram("hres_d", (B, L, D))
        qk_d = dram("qk_d", (B, 2, 3, D, L), BF16)
        bc_d = dram("bc_d", (B, 2 * N, L))
        ones_d = dram("ones_d", (2, G, L), BF16)

        w_in = sb("w_in", [P, KT, 2 * DI])
        w_qkv = sb("w_qkv", [P, 3, KT, D])
        w_o = sb("w_o", [P, KT, D])
        w_ssm = sb("w_ssm", [P, J, D])
        w_f1 = sb("w_f1", [P, KT, FF])
        w_f2 = sb("w_f2", [P, FT, D])
        w_xp = sb("w_xp", [P, J, P])
        w_dt = sb("w_dt", [P, DI])
        w_base = sb("w_base", [P, KT, D])
        w_la = sb("w_la", [P, KT, E * LR])
        w_lb = sb("w_lb", [P, D])
        w_rt = sb("w_rt", [P, KT, E])
        ident = sb("ident", [P, P])
        identb = sb("identb", [P, P], BF16)
        mask_qk = sb("mask_qk", [P, P], BF16)
        A = sb("A", [P, J, N])
        D_par = sb("D_par", [P, J])
        conv_w = sb("conv_w", [P, J, K_CONV])
        conv_b = sb("conv_b", [P, J])
        dt_b = sb("dt_b", [P, J])
        ln1 = sb("ln1", [P, 2, KT])
        ln2 = sb("ln2", [P, 2, KT])
        qkv_b = sb("qkv_b", [P, 3, KT])
        f1_b = sb("f1_b", [P, FT])
        ob_row = sb("ob_row", [P, D])
        f2b_row = sb("f2b_row", [P, D])
        bb_row = sb("bb_row", [P, D])
        rb_row = sb("rb_row", [P, E])
        eps4 = sb("eps4", [P, TB])
        mhalf4 = sb("mhalf4", [P, TB])

        dts = sb("dts", [P, 2, J, L])
        us = sb("us", [P, 2, J, L])
        xc = sb("xc", [P, J, L])
        zs = sb("zs", [P, TB, DI])
        decay = sb("decay", [P, AR, JP, L])
        state = sb("state", [P, RING, JP, L])
        bc = sb("bc", [P, BC_SLOTS, 2, L])

        xt = sb("xt", [P, TB, D])
        ht = sb("ht", [P, TB, D])
        mod_a = sb("mod_a", [P, 2, D])
        xnT = sb("xnT", [P, KT, L])
        qkp = sb("qkp", [P, 3, L], BF16)
        dbc = sb("dbc", [P, L])
        qkf = dbc
        vt = sb("vt", [P, TB, H, HD + 1])

        def stats_tiles(name):
            return (sb(name + "_st", [P, TB, 6]), sb(name + "_mv", [P, TB, 2]), sb(name + "_rs", [P, TB]))

        lns = [stats_tiles(f"ln{n}") for n in range(4)]

        REGION = 8704
        region = sb("region", [P, REGION])
        at = [0]

        def view(words, dt=F32):
            v = region[:, at[0]:at[0] + words]
            at[0] += words
            assert at[0] <= REGION
            return v if dt == F32 else v.bitcast(dt)

        Qs, Ks = [], []
        for s in range(2):
            Qs.append(view(G * L // 2, BF16).rearrange("p (h t) -> p h t", h=G))
            Ks.append(view(G * L // 2, BF16).rearrange("p (h t) -> p h t", h=G))
        probs = view(G * L).rearrange("p (h t) -> p h t", h=G)
        oT = view(L)
        otok = view(TB * D).rearrange("p (t f) -> p t f", t=TB)
        aoT = view(KT * L).rearrange("p (k t) -> p k t", k=KT)
        at[0] = 0
        gT = view(FT * L).rearrange("p (f t) -> p f t", f=FT)
        ygT = gT[:, 0:J]
        h2T = view(KT * L).rearrange("p (k t) -> p k t", k=KT)
        nrm = view(TB * D).rearrange("p (t f) -> p t f", t=TB)
        xr = view(TB * D).rearrange("p (t f) -> p t f", t=TB)
        ax = view(TB * E * LR).rearrange("p (t f) -> p t f", t=TB)
        axT = view(L)
        mod_g = view(2 * D).rearrange("p (a f) -> p a f", a=2)
        at[0] = 0
        c_raw = view(D)
        cT = view(KT * B).rearrange("p (k b) -> p k b", k=KT)
        w_mod = view(KT * 6 * D).rearrange("p (k n) -> p k n", k=KT)
        base_raw = view(KT * D).rearrange("p (o k) -> p o k", o=KT)
        rt_raw = view(D)
        mods = view(6 * D)
        alpha = view(D)
        nalpha = view(D)
        mod_t = view(2 * KT * B).rearrange("p (b c) -> p b c", c=2 * KT)
        ones_b = view(G * L // 2, BF16)
        sgn = view(D)
        mag = view(D)
        mask_f = view(P)

        held = sb("held", [P, 1])
        x1 = sb("x1", [P, TB, D])
        mod_f = sb("mod_f", [P, 2 * KT])
        mx = sb("mx", [P, 2, 16])
        nmx = sb("nmx", [P, 16])
        mrow = sb("mrow", [16, 2, P], BF16)
        rden = sb("rden", [P, TB, G])
        lg = sb("lg", [P, TB, E])
        top = sb("top", [P, TB, 8])
        keep = sb("keep", [P, TB, E])
        ew = top
        esum = sb("esum", [P, TB])

        pY = [pb(f"pY{t}") for t in range(TB)]
        pM = [pb(f"pM{m}") for m in range(BANKS)]
        pO = pb("pO")

        w_loaded = sem("w_loaded")
        built = sem("built")
        pool_c, dve_c, act_c, pe_c = sem("pool_c"), sem("dve_c"), sem("act_c"), sem("pe_c")
        mod_stored, ones_stored = sem("mod_stored"), sem("ones_stored")
        x_in, moda_in = sig("x_in", 16), sig("moda_in", 16)
        bn = [sig(f"bn{n}", TB) for n in range(4)]
        mv = [sig(f"mv{n}", TB) for n in range(4)]
        ve = [sig(f"ve{n}", 1) for n in range(4)]
        rs = [sig(f"rs{n}", 1) for n in range(4)]
        n0 = sig("n0", TB)
        h_made = sig("h_made", 3)
        hres_out = sig("hres_out", 16)
        n1 = sig("n1", TB)
        xt_ps, xt_ok = sig("xt_ps", KT), sig("xt_ok", KT)
        qk_ps, qk_f, qk_s, qk_out = sig("qk_ps", 4), sig("qk_f", 4), sig("qk_s", 16), sig("qk_out", 64)
        v_ps, v_ok = sig("v_ps", 2), sig("v_ok", 2)
        xs_ps, xs_a, xs_c, xc_ok = sig("xs_ps", J), sig("xs_a", J), sig("xs_c", 3 * J), sig("xc_ok", 1)
        xp_ps, xp_ok, bc_out = sig("xp_ps", 1), sig("xp_ok", 1), sig("bc_out", 16)
        dt_ps, dt_x, dt_m, dt_e, dt_ok, u_ok = (sig("dt_ps", J), sig("dt_x", J), sig("dt_m", 1),
                                                sig("dt_e", 2), sig("dt_ok", 1), sig("u_ok", 1))
        xd_ok, d_done = sig("xd_ok", J), sig("d_done", 1)
        bc_in = [sem(f"bc_in{s}") for s in range(BC_SLOTS)]
        a_ok, b_ok, s_ok, p_ok, y_ok = (sig("a_ok", UNITS * JP), sig("b_ok", UNITS), sig("s_ok", UNITS),
                                        sig("p_ok", UNITS), sig("y_ok", UNITS))
        z_ps, z_raw, z_ok = sig("z_ps", TB), sig("z_raw", TB), sig("z_ok", 1)
        qks_in = [sig(f"qks_in{s}", 2 * (2 * TERMS + 1) * 16) for s in range(2)]
        s_ps, mx_ok = sig("s_ps", 12 * NG), sig("mx_ok", 11 * NG)
        nm_ok, mr_ok, mrow_in = sig("nm_ok", NG), sig("mr_ok", 2 * NG), sig("mrow_in", 32 * NG)
        t_ps, p_exp, pv_ok = sig("t_ps", H * TB), sig("p_exp", H * TB), sig("pv_ok", H * TB)
        o_ev, ot_ps, rd_ok, on_ok = sig("o_ev", NG), sig("ot_ps", NG), sig("rd_ok", NG), sig("on_ok", NG)
        at_ps, at_ok, op_ps, x1p_in, x1p_ok = (sig("at_ps", KT), sig("at_ok", KT), sig("op_ps", 2),
                                               sig("x1p_in", 16), sig("x1p_ok", 2))
        gated = sig("gated", TB)
        yt_ps, yt_ok, so_ps, x1_ok = sig("yt_ps", J), sig("yt_ok", J), sig("so_ps", 2), sig("x1_ok", 2)
        n2, h2_ps, h2_ok, x1b = sig("n2", TB), sig("h2_ps", KT), sig("h2_ok", KT), sig("x1b", 1)
        f1_ps, f1_raw, g_ok = sig("f1_ps", FT), sig("f1_raw", FT), sig("g_ok", 1)
        f2_ps, r_ok = sig("f2_ps", 2), sig("r_ok", 2)
        xr_in, modg_in, modf_in, x2_ok = sig("xr_in", 16), sig("modg_in", 32), sig("modf_in", 16), sig("x2_ok", 2)
        n3, h3_ps, h3_ok = sig("n3", TB), sig("h3_ps", KT), sig("h3_ok", KT)
        rt_ps, rt_c, ex_ok, ew_ok = sig("rt_ps", 1), sig("rt_c", 7), sig("ex_ok", 1), sig("ew_ok", 4)
        la_ps, ax_ok, axt_ps, axt_ok = sig("la_ps", 1), sig("ax_ok", 1), sig("axt_ps", 1), sig("axt_ok", 1)
        out_ps, o_sum, o_gb, o_fin, out_done = (sig("out_ps", 2), sig("o_sum", 2), sig("o_gb", 1),
                                                sig("o_fin", 1), sig("out_done", 16))

        block = ctx.enter_context(nc.Block())

        def last_of_attention(b, eng):
            b.wait(eng, op_ps)

        def drive(eng, unit, step, banks=(), before=None, after=None):
            def turn(b, first, last):
                for k, names in enumerate(SCHEDULE):
                    unit(b, k, first, last)
                    for name in names:
                        if name in FIN_SET:
                            if not first:
                                step(name, b.next(-1))
                        elif name in PREP_SET:
                            if not last:
                                step(name, b.next(1))
                        else:
                            step(name, b)

            for name in PREP:
                step(name, Batch(None, 0))
            if before:
                before(Batch(None, 0))
            turn(Batch(None, 0), True, False)
            with eng.Fori(0, (B - 2) // 2) as i:
                for bank in banks:
                    bank.into_loop(i)
                turn(Batch(i, 1), False, False)
                turn(Batch(i, 2), False, False)
            for bank in banks:
                bank.out_of_loop(B - 2)
            turn(Batch(None, B - 1), False, True)
            if after:
                after(Batch(None, B - 1))
            for name in FIN:
                step(name, Batch(None, B - 1))

        def parity(b):
            return b.off % 2

        @block.sync
        def _(sp):
            n_loads = [0]

            def load(dst, src):
                n_loads[0] += 1
                sp.dma_start(dst, src).then_inc(w_loaded, 16)

            sp.wait_ge(built, CLEARED)
            load(c_raw[0:B, :], d["c"])
            load(w_mod, d["wmod"].rearrange("(k p) n -> p k n", p=P))
            load(w_in[:], d["in_proj_w"].rearrange("(k p) n -> p k n", p=P))
            for n, w in enumerate(("q", "k", "v")):
                load(w_qkv[:, n], d[w + "_w"].rearrange("(k p) n -> p k n", p=P))
            load(w_o[:], d["o_w"].rearrange("(k p) n -> p k n", p=P))
            load(w_ssm[:], d["ssm_out_w"].rearrange("(j p) n -> p j n", p=P))
            load(w_f1[:], d["ffn_w1"].rearrange("(k p) n -> p k n", p=P))
            load(w_f2[:], d["ffn_w2"].rearrange("(f p) n -> p f n", p=P))
            load(w_dt[0:R, :], d["dt_w"])
            load(base_raw, d["base_w"].rearrange("(o p) k -> p o k", p=P))
            load(rt_raw[0:E, :], d["router_w"])
            load(w_lb[:], d["lora_B"].rearrange("e r o -> (e r) o"))
            load(A[:], d["A_log"].rearrange("(j p) n -> p j n", p=P))
            load(conv_w[:], d["conv_w"].rearrange("(j p) k -> p j k", p=P))
            for row, name in ((ob_row, "o_b"), (f2b_row, "ffn_b2"), (bb_row, "base_b"), (rb_row, "router_b")):
                load(row[:], d[name].partition_broadcast(P))
            load(alpha, d["mix_weight"].partition_broadcast(P))
            with nc.allow_non_contiguous_dma(reason="small vectors, one element per partition"):
                load(w_xp[:, :, 0:R + 2 * N], d["x_proj_w"].rearrange("(j p) n -> p j n", p=P))
                for k in range(KT):
                    load(w_la[:, k, :].rearrange("p (e r) -> p e r", e=E),
                         d["lora_A"][:, k * P:(k + 1) * P, :].rearrange("e p r -> p e r"))
                load(D_par[:], d["D_param"].rearrange("(j p) -> p j", p=P))
                load(conv_b[:], d["conv_b"].rearrange("(j p) -> p j", p=P))
                load(dt_b[:], d["dt_b"].rearrange("(j p) -> p j", p=P))
                load(f1_b[:], d["ffn_b1"].rearrange("(j p) -> p j", p=P))
                for n, w in enumerate(("w", "b")):
                    load(ln1[:, n], d["ln1_" + w].rearrange("(j p) -> p j", p=P))
                    load(ln2[:, n], d["ln2_" + w].rearrange("(j p) -> p j", p=P))
                for n, w in enumerate(("q", "k", "v")):
                    load(qkv_b[:, n], d[w + "_b"].rearrange("(j p) -> p j", p=P))
            assert n_loads[0] == N_LOADS, n_loads[0]
            sp.wait_ge(dve_c, MODS_DONE)
            sp.dma_start(ones_d.rearrange("o h t -> o (h t)"), ones_b[0:2, :]).then_inc(ones_stored, 16)
            sp.wait_ge(ones_stored, 16)
            sp.dma_start(mod_rows, mods[0:B, :]).then_inc(mod_stored, 16)
            sp.dma_start(mod_cols.rearrange("b p c -> p b c"), mod_t).then_inc(mod_stored, 16)
            sp.wait_ge(mod_stored, 32)

            def bc_row(b, n):
                g = n // BC_SLOTS
                slot = n % BC_SLOTS
                if n >= BC_SLOTS:
                    last = (n - BC_SLOTS + 1) * J // JP
                    b.wait(sp, b_ok, last)
                    b.wait(sp, p_ok, last)
                else:
                    row = N - (N - slot - 1) % BC_SLOTS - 1
                    b.wait_last(sp, b_ok, (row + 1) * J // JP)
                    b.wait_last(sp, p_ok, (row + 1) * J // JP)
                if n == 0:
                    b.wait(sp, bc_out)
                src = bc_d[b.index].rearrange("(a n) t -> n a t", a=2)[n]
                sp.dma_start(bc[:, slot], src.partition_broadcast(P)).then_inc(bc_in[slot], 16)

            def unit(b, k, first, last):
                if k == 0:
                    for n in range(BC_SLOTS - 1):
                        bc_row(b, n)
                elif k % (J // JP) == 0:
                    n = k // (J // JP) + BC_SLOTS - 2
                    if n < N:
                        bc_row(b, n)

            def step(name, b):
                if name == "load":
                    b.wait_last(sp, hres_out)
                    b.wait_last(sp, h_made)
                    sp.dma_start(xt[:], d["x"][b.index].rearrange("(t p) f -> p t f", p=P)).then_inc(x_in.sem, 16)
                    sp.dma_start(mod_a[:].rearrange("p a f -> p (a f)"),
                                 mod_rows[b.index, 0:2 * D].partition_broadcast(P)).then_inc(moda_in.sem, 16)
                elif name == "l1a":
                    b.wait(sp, h_made)
                    sp.dma_start(hres_d[b.index].rearrange("(t p) f -> p t f", p=P), xt[:]).then_inc(hres_out.sem, 16)
                elif name[:2] == "qk":
                    n = int(name[2])
                    b.wait(sp, qk_s, 4 * n + 4)
                    sp.dma_start(qk_d[b.index, n // 2, :, (n % 2) * P:(n % 2 + 1) * P].rearrange("c p t -> p c t"),
                                 qkp[:]).then_inc(qk_out.sem, 16)
                elif name == "xp":
                    b.wait(sp, xp_ok)
                    sp.dma_start(bc_d[b.index], dbc[R:R + 2 * N, :]).then_inc(bc_out.sem, 16)
                elif name[:2] == "ld":
                    g = int(name[2])
                    s = g % 2
                    if g == 0:
                        b.wait(sp, qk_out)
                        b.wait_last(sp, o_fin)
                    if g >= 2:
                        b.wait(sp, t_ps, (g - 1) * G * TB)
                    for op, tiles, parts in ((0, Qs, Q_PART), (1, Ks, K_PART)):
                        for c, part in enumerate(parts):
                            src = qk_d[b.index, op, part].rearrange("(h r) t -> r h t", r=HD)[:, g * G:(g + 1) * G, :]
                            sp.dma_start(tiles[s][c * HD:(c + 1) * HD], src).then_inc(qks_in[s].sem, 16)
                    sp.dma_start(Ks[s][QK_ROWS:QK_ROWS + 2], ones_d).then_inc(qks_in[s].sem, 16)
                elif name[:2] == "mt":
                    g = int(name[2])
                    b.wait(sp, mr_ok, 2 * g + 2)
                    for part in range(2):
                        dst = Qs[g % 2][QK_ROWS + part:QK_ROWS + part + 1].rearrange("o h (q p) -> o (h q) p", p=P)
                        sp.dma_start(dst, mrow[:, part, :]).then_inc(mrow_in.sem, 16)
                elif name == "ot0":
                    b.wait_last(sp, x2_ok, 1)
                    b.wait(sp, hres_out)
                    sp.dma_start(x1[:], hres_d[b.index].rearrange("(t p) f -> p t f", p=P)).then_inc(x1p_in.sem, 16)
                elif name == "gate":
                    last_of_attention(b, sp)
                    b.wait(sp, at_ok)
                    b.wait_last(sp, o_fin)
                    b.wait_last(sp, h3_ok)
                    sp.dma_start(xr, d["x"][b.index].rearrange("(t p) f -> p t f", p=P)).then_inc(xr_in.sem, 16)
                    for a, col in ((0, 2), (1, 5)):
                        sp.dma_start(mod_g[:, a], mod_rows[b.index, col * D:(col + 1) * D].partition_broadcast(P))\
                          .then_inc(modg_in.sem, 16)
                    sp.dma_start(mod_f[:], mod_cols[b.index]).then_inc(modf_in.sem, 16)
                elif name == "put":
                    b.wait(sp, o_fin)
                    sp.dma_start(out[b.index].rearrange("(t p) f -> p t f", p=P), nrm).then_inc(out_done.sem, 16)

            drive(sp, unit, step)
            sp.wait_ge(out_done.sem, 16 * B)
            sp.wait_ge(hres_out.sem, 16 * B)
            sp.wait_ge(qk_out.sem, 64 * B)
            sp.wait_ge(bc_out.sem, 16 * B)

        @block.gpsimd
        def _(pool):
            count = [0]

            def link(ins):
                count[0] += 1
                ins.then_inc(pool_c, 1)
                pool.wait_ge(pool_c, count[0])

            for tile, value in ((c_raw, 0.0), (rt_raw, 0.0), (w_xp[:], 0.0), (w_dt[:], 0.0)):
                nc.gpsimd.memset(tile, value).then_inc(built, 1)
            nc.gpsimd.memset(eps4[:], EPS).then_inc(built, 1)
            nc.gpsimd.memset(mhalf4[:], -0.5).then_inc(built, 1)
            nc.gpsimd.memset(decay[:], 0.0).then_inc(built, 1)
            nc.gpsimd.memset(vt[:], 1.0).then_inc(built, 1)
            nc.gpsimd.memset(ones_b, 1.0).then_inc(built, 1)
            link(nc.gpsimd.memset(ident[:], 0.0))
            nc.gpsimd.affine_select(out=ident[:], in_=ident[:], compare_op=ALU.not_equal, fill=1.0,
                                    base=0, pattern=[[-1, P]], channel_multiplier=1).then_inc(built, 1)
            link(nc.gpsimd.memset(mask_f, 0.0))
            nc.gpsimd.affine_select(out=mask_f, in_=mask_f, compare_op=ALU.is_ge, fill=MASKED,
                                    base=0, pattern=[[-1, P]], channel_multiplier=1).then_inc(built, 1)

            def rstd(b, n):
                b.wait(pool, mv[n])
                nc.gpsimd.tensor_tensor(lns[n][2][:], lns[n][1][:, :, 1], eps4[:], ALU.add).then_inc(ve[n].sem, 1)
                b.wait(pool, ve[n])
                nc.gpsimd.tensor_tensor(lns[n][2][:], lns[n][2][:], mhalf4[:], ALU.pow).then_inc(rs[n].sem, 1)

            def row(ap):
                return ap.unsqueeze(1).broadcast_to([P, TB, D])

            def unit(b, k, first, last):
                if k < UNITS - POOL_LEAD:
                    fill_state(b, k + POOL_LEAD)
                elif not last:
                    fill_state(b.next(1), k + POOL_LEAD - UNITS)

            def start(b):
                for k in range(POOL_LEAD):
                    fill_state(b, k)

            def fill_state(b, k):
                n, jp = k // (J // JP), k % (J // JP)
                if k == 0:
                    b.wait(pool, u_ok)
                if jp == 0:
                    slot = n % BC_SLOTS
                    per = len(range(slot, N, BC_SLOTS))
                    b.wait(pool, Signal(bc_in[slot], 16 * per), 16 * (n // BC_SLOTS + 1))
                if k >= RING:
                    b.wait(pool, y_ok, k - RING + 1)
                else:
                    b.wait_last(pool, y_ok, UNITS + k - RING + 1)
                par = parity(b)
                nc.gpsimd.tensor_tensor(state[:, k % RING], us[:, par, jp * JP:(jp + 1) * JP, :],
                                        bc[:, n % BC_SLOTS, 0, :].unsqueeze(1).broadcast_to([P, JP, L]),
                                        ALU.mult).then_inc(b_ok.sem, 1)

            def step(name, b):
                if name == "l0s":
                    rstd(b, 0)
                elif name == "l0a":
                    b.wait(pool, n0)
                    b.wait(pool, moda_in)
                    b.wait_last(pool, xt_ps)
                    nc.gpsimd.tensor_tensor(ht[:], xt[:], row(mod_a[:, 1, :]), ALU.mult).then_inc(h_made.sem, 1)
                    b.wait(pool, h_made, 1)
                    nc.gpsimd.tensor_tensor(ht[:], ht[:], row(mod_a[:, 0, :]), ALU.add).then_inc(h_made.sem, 1)
                    b.wait(pool, h_made, 2)
                    nc.gpsimd.tensor_tensor(xt[:], ht[:], row(ob_row[:]), ALU.add).then_inc(h_made.sem, 1)
                elif name == "l1a":
                    rstd(b, 1)
                elif name == "u":
                    par = parity(b)
                    b.wait(pool, dt_ok)
                    nc.gpsimd.tensor_tensor(us[:, par], dts[:, par], xc[:], ALU.mult).then_inc(u_ok.sem, 1)
                elif name == "l2s":
                    rstd(b, 2)
                elif name == "f1_0":
                    b.wait(pool, n2)
                    nc.gpsimd.tensor_tensor(x1[:], x1[:], row(f2b_row[:]), ALU.add).then_inc(x1b.sem, 1)
                elif name == "x2":
                    b.wait(pool, r_ok)
                    b.wait(pool, modg_in)
                    b.wait(pool, xr_in)
                    nc.gpsimd.tensor_tensor(nrm, x1[:], row(mod_g[:, 0, :]), ALU.mult).then_inc(x2_ok.sem, 1)
                    b.wait(pool, x2_ok, 1)
                    nc.gpsimd.tensor_tensor(xr, xr, nrm, ALU.add).then_inc(x2_ok.sem, 1)
                elif name == "l3a":
                    rstd(b, 3)
                elif name == "put":
                    b.wait(pool, o_sum)
                    nc.gpsimd.tensor_tensor(nrm, nrm, row(mod_g[:, 1, :]), ALU.mult).then_inc(o_gb.sem, 1)
                    b.wait(pool, o_gb)
                    nc.gpsimd.tensor_tensor(nrm, nrm, xr, ALU.add).then_inc(o_fin.sem, 1)

            pool.wait_ge(built, BUILT)
            drive(pool, unit, step, before=start)

        @block.scalar
        def _(act):
            act.wait_ge(w_loaded, 16 * N_LOADS)
            act.activation(alpha, alpha, ACT.Sigmoid).then_inc(act_c, 1)
            act.activation(A[:], A[:], ACT.Exp).then_inc(act_c, 1)
            act.activation(c_raw, c_raw, ACT.Silu).then_inc(act_c, 1)
            act.wait_ge(act_c, 3)
            act.activation(A[:], A[:], ACT.Copy, scale=-1.0).then_inc(act_c, 1)
            act.wait_ge(built, BUILT)
            act.wait_ge(act_c, 4)

            def unit(b, k, first, last):
                if k < UNITS - ACT_LEAD:
                    decays(b, k + ACT_LEAD)
                elif not last:
                    decays(b.next(1), k + ACT_LEAD - UNITS)

            def start(b):
                for k in range(ACT_LEAD):
                    decays(b, k)

            def decays(b, k):
                n, jp = k // (J // JP), k % (J // JP)
                par = parity(b)
                if k == 0:
                    b.wait(act, dt_ok)
                if k >= AR:
                    b.wait(act, s_ok, k - AR + 1)
                else:
                    b.wait_last(act, s_ok, UNITS + k - AR + 1)
                for jj in range(JP):
                    j = jp * JP + jj
                    act.activation(decay[:, k % AR, jj, 1:L], dts[:, par, j, 1:L], ACT.Exp,
                                   scale=A[:, j, n:n + 1]).then_inc(a_ok.sem, 1)

            def step(name, b):
                if name[:2] == "xt":
                    k = int(name[2])
                    b.wait(act, xt_ps, k + 1)
                    if k == 0:
                        b.wait_last(act, z_ps)
                        b.wait_last(act, xs_ps)
                        b.wait_last(act, v_ps)
                    act.activation(xnT[:, k], pM[bank_of(name, 0)][:], ACT.Identity, scale=ln1[:, 0, k:k + 1],
                                   bias=ln1[:, 1, k:k + 1]).then_inc(xt_ok.sem, 1)
                elif name[:2] == "qk":
                    n = int(name[2])
                    b.wait(act, qk_ps, n + 1)
                    if n:
                        b.wait(act, qk_s, 4 * n)
                    else:
                        b.wait_last(act, qk_s)
                        b.wait_last(act, dt_ps)
                        b.wait_last(act, bc_out)
                    act.activation(qkf[:], pM[bank_of(name, 0)][:], ACT.Identity, bias=qkv_b[:, n // 2, n % 2:n % 2 + 1])\
                       .then_inc(qk_f.sem, 1)
                elif name[0] == "v":
                    n = int(name[1])
                    b.wait(act, v_ps, n + 1)
                    b.wait_last(act, pv_ok)
                    act.activation(vt[:, 2 * n:2 * n + 2, :, 0:HD],
                                   pM[bank_of(name, 0)][:].rearrange("p (t h r) -> p t h r", t=2, h=H),
                                   ACT.Copy).then_inc(v_ok.sem, 1)
                elif name[:3] in ("xs0", "xs1", "xs2", "xs3"):
                    j = int(name[2])
                    b.wait(act, xs_ps, j + 1)
                    b.wait_last(act, d_done)
                    act.activation(xc[:, j], pM[bank_of(name, 0)][:], ACT.Identity, scale=conv_w[:, j, K_CONV - 1:K_CONV],
                                   bias=conv_b[:, j:j + 1]).then_inc(xs_a.sem, 1)
                elif name == "xsilu":
                    b.wait(act, xs_c)
                    act.activation(xc[:], xc[:], ACT.Silu).then_inc(xc_ok.sem, 1)
                elif name == "xp":
                    b.wait(act, xp_ps)
                    b.wait(act, qk_s)
                    act.activation(dbc[:], pM[bank_of(name, 0)][:], ACT.Copy).then_inc(xp_ok.sem, 1)
                elif name[:2] == "dt":
                    j = int(name[2])
                    b.wait(act, dt_ps, j + 1)
                    if not (b.reg is None and b.off < 2):
                        b.next(-2).wait(act, b_ok)
                    act.activation(us[:, parity(b), j], pM[bank_of(name, 0)][:], ACT.Identity, bias=dt_b[:, j:j + 1])\
                       .then_inc(dt_x.sem, 1)
                elif name == "sp":
                    par = parity(b)
                    b.wait(act, dt_m)
                    act.activation(dts[:, par], dts[:, par], ACT.Exp).then_inc(dt_e.sem, 1)
                    b.wait(act, dt_e, 1)
                    act.activation(dts[:, par], dts[:, par], ACT.Ln, bias=1.0).then_inc(dt_e.sem, 1)
                elif name in ("z0", "z1", "z2", "z3"):
                    n = int(name[1])
                    b.wait(act, z_ps, n + 1)
                    b.wait_last(act, yt_ps)
                    act.activation(zs[:, n], pM[bank_of(name, 0)][:], ACT.Copy).then_inc(z_raw.sem, 1)
                elif name == "zsilu":
                    b.wait(act, z_raw)
                    act.activation(zs[:], zs[:], ACT.Silu).then_inc(z_ok.sem, 1)
                elif name[:2] == "st":
                    g, kb = int(name[2]), int(name[4])
                    for h in range(G):
                        e = (g * TB + kb) * G + h
                        n = L - kb * P
                        b.wait(act, t_ps, e + 1)
                        if e >= G:
                            b.wait(act, pv_ok, e - G + 1)
                        else:
                            b.wait_last(act, o_fin)
                        act.activation(probs[:, h, 0:n], pM[bank_of(name, h)][:, 0:n], ACT.Exp, scale=HD ** -0.5)\
                           .then_inc(p_exp.sem, 1)
                elif name[:2] == "on":
                    g = int(name[2])
                    b.wait(act, pv_ok, (g + 1) * G * TB)
                    if g:
                        b.wait(act, ot_ps, g)
                    else:
                        b.wait_last(act, o_fin)
                    act.activation(oT, pO[:], ACT.Copy).then_inc(o_ev.sem, 1)
                elif name[:2] == "ot":
                    k = int(name[2])
                    b.wait(act, at_ps, k + 1)
                    act.activation(aoT[:, k], pM[bank_of(name, 0)][:], ACT.Identity, bias=qkv_b[:, 2, k:k + 1])\
                       .then_inc(at_ok.sem, 1)
                elif name[:2] == "yt":
                    j = int(name[2])
                    b.wait(act, yt_ps, j + 1)
                    b.wait_last(act, so_ps)
                    act.activation(ygT[:, j], pM[bank_of(name, 0)][:], ACT.Copy).then_inc(yt_ok.sem, 1)
                elif name[:3] == "h2t":
                    k = int(name[3])
                    b.wait(act, h2_ps, k + 1)
                    act.activation(h2T[:, k], pM[bank_of(name, 0)][:], ACT.Identity, scale=ln2[:, 0, k:k + 1],
                                   bias=ln2[:, 1, k:k + 1]).then_inc(h2_ok.sem, 1)
                elif name[:3] == "f1_":
                    f = int(name[3])
                    b.wait(act, f1_ps, f + 1)
                    act.activation(gT[:, f], pM[bank_of(name, 0)][:], ACT.Identity, bias=f1_b[:, f:f + 1])\
                       .then_inc(f1_raw.sem, 1)
                elif name == "gelu":
                    b.wait(act, f1_raw)
                    act.activation(gT, gT, ACT.Gelu).then_inc(g_ok.sem, 1)
                elif name[:3] == "h3t":
                    k = int(name[3])
                    b.wait(act, h3_ps, k + 1)
                    b.wait(act, modf_in)
                    act.activation(h2T[:, k], pM[bank_of(name, 0)][:], ACT.Identity, scale=mod_f[:, KT + k:KT + k + 1],
                                   bias=mod_f[:, k:k + 1]).then_inc(h3_ok.sem, 1)
                elif name == "route2":
                    b.wait(act, rt_c)
                    act.activation(ew[:], lg[:], ACT.Exp).then_inc(ex_ok.sem, 1)
                elif name == "axt":
                    b.wait(act, axt_ps)
                    act.activation(axT, pM[bank_of(name, 0)][:], ACT.Copy).then_inc(axt_ok.sem, 1)

            drive(act, unit, step, before=start)

        @block.tensor
        def _(pe):
            pe.wait_ge(w_loaded, 16 * N_LOADS)
            pe.wait_ge(built, BUILT)
            pe.wait_ge(act_c, 3)
            n_pe = [0]

            def done(ins, read_by):
                n_pe[0] += 1
                ins.then_inc(pe_c, 1)
                pe.wait_ge(dve_c, read_by)

            for k in range(KT):
                t = pe.transpose(pM[0][:, k * P:(k + 1) * P], c_raw[:, k * P:(k + 1) * P], ident[:])
            done(t, 1)
            for n in range(3):
                for k in range(KT):
                    t = pe.matmul(pM[0][0:B, :], cT[:, k, :], w_mod[:, k, n * 512:(n + 1) * 512],
                                  start=(k == 0), stop=(k == KT - 1))
                done(t, 2 + n)
            for o in range(KT):
                for k in range(KT):
                    t = pe.transpose(pM[0][:, (o * KT + k) * P:(o * KT + k + 1) * P],
                                     base_raw[:, o, k * P:(k + 1) * P], ident[:])
            done(t, 5)
            for k in range(KT):
                t = pe.transpose(pM[0][:, k * P:(k + 1) * P], rt_raw[:, k * P:(k + 1) * P], ident[:])
            done(t, 6)
            pe.wait_ge(dve_c, MODS_READY)
            for c in range(2 * KT):
                t = pe.transpose(pM[0][:, c * P:(c + 1) * P], mods[:, 3 * D + c * P:3 * D + (c + 1) * P], ident[:])
            done(t, MODS_DONE)
            pe.wait_ge(dve_c, DVE_SETUP)

            banks = [Bank() for _ in range(BANKS)]

            def next_bank(name, i, b, freed_by, n):
                banks[bank_of(name, i)].fill(pe, b, freed_by, n)
                return pM[bank_of(name, i)]


            def skip_part(b):
                b.wait(pe, xd_ok)
                b.wait_last(pe, gated)
                for j in range(J):
                    for t in range(TB):
                        ins = pe.matmul(pY[t][:, j * P:(j + 1) * P], xc[:, j, t * P:(t + 1) * P], ident[:],
                                        is_transpose=True, start=(j == 0), stop=False, skip_group_check=True)
                ins.then_inc(d_done.sem, 1)

            def add(b, a):
                b.wait(pe, p_ok, a + 1)
                for jj in range(JP):
                    j = (a % (J // JP)) * JP + jj
                    for t in range(TB):
                        ins = pe.matmul(pY[t][:, j * P:(j + 1) * P], state[:, a % RING, jj, t * P:(t + 1) * P],
                                        ident[:], is_transpose=True, start=False,
                                        stop=(a >= UNITS - J // JP), skip_group_check=True)
                ins.then_inc(y_ok.sem, 1)

            def unit(b, k, first, last):
                if k < PE_LAG:
                    if not first:
                        add(b.next(-1), UNITS - PE_LAG + k)
                elif k == PE_START:
                    skip_part(b)
                    for a in range(PE_START - PE_LAG + 1):
                        add(b, a)
                elif k > PE_START:
                    add(b, k - PE_LAG)

            def finish(b):
                for a in range(UNITS - PE_LAG, UNITS):
                    add(b, a)

            def turned(name, src, sig_, b, freed_by, n):
                ps = next_bank(name, 0, b, freed_by, n)
                for t in range(TB):
                    ins = pe.transpose(ps[:, t * P:(t + 1) * P], src(t), ident[:])
                ins.then_inc(sig_.sem, 1)

            def probs_v(b, e):
                g, kb, h = e // (TB * G), e // G % TB, e % G
                if e % (TB * G) == 0:
                    b.wait(pe, v_ok)
                    if g:
                        b.wait(pe, o_ev, g)
                    else:
                        b.wait_last(pe, o_ev)
                b.wait(pe, p_exp, e + 1)
                pe.matmul(pO[32 * h:32 * h + HD + 1, kb * P:L], vt[:, kb, g * G + h, :],
                          probs[:, h, 0:L - kb * P], start=(kb == 0), stop=(kb == TB - 1),
                          skip_group_check=True).then_inc(pv_ok.sem, 1)

            def step(name, b):
                if name[:2] == "xt":
                    k = int(name[2])
                    b.wait(pe, n1)
                    turned(name, lambda t: ht[:, t, k * P:(k + 1) * P], xt_ps, b, xt_ok, k + 1)
                elif name[:2] == "qk":
                    n = int(name[2])
                    b.wait(pe, xt_ok)
                    ps = next_bank(name, 0, b, qk_f, n + 1)
                    for k in range(KT):
                        ins = pe.matmul(ps[:], w_qkv[:, n // 2, k, (n % 2) * P:(n % 2 + 1) * P], xnT[:, k],
                                        start=(k == 0), stop=(k == KT - 1))
                    ins.then_inc(qk_ps.sem, 1)
                elif name[0] == "v":
                    n = int(name[1])
                    ps = next_bank(name, 0, b, v_ok, n + 1)
                    for t in range(2):
                        for k in range(KT):
                            ins = pe.matmul(ps[:, t * D:(t + 1) * D], xnT[:, k, (2 * n + t) * P:(2 * n + t + 1) * P],
                                            w_qkv[:, 2, k, :], start=(k == 0), stop=(k == KT - 1))
                    ins.then_inc(v_ps.sem, 1)
                elif name in ("xs0", "xs1", "xs2", "xs3"):
                    j = int(name[2])
                    ps = next_bank(name, 0, b, xs_c, 3 * j + 3)
                    for k in range(KT):
                        ins = pe.matmul(ps[:], w_in[:, k, j * P:(j + 1) * P], xnT[:, k],
                                        start=(k == 0), stop=(k == KT - 1))
                    ins.then_inc(xs_ps.sem, 1)
                elif name == "xp":
                    b.wait(pe, xc_ok)
                    ps = next_bank(name, 0, b, xp_ok, 1)
                    for j in range(J):
                        ins = pe.matmul(ps[:], w_xp[:, j, :], xc[:, j], start=(j == 0), stop=(j == J - 1))
                    ins.then_inc(xp_ps.sem, 1)
                elif name[:2] == "dt":
                    j = int(name[2])
                    b.wait(pe, xp_ok)
                    ps = next_bank(name, 0, b, dt_x, j + 1)
                    pe.matmul(ps[:], w_dt[:, j * P:(j + 1) * P], dbc[:], start=True, stop=True)\
                      .then_inc(dt_ps.sem, 1)
                elif name in ("z0", "z1", "z2", "z3"):
                    n = int(name[1])
                    b.wait(pe, xt_ok)
                    ps = next_bank(name, 0, b, z_raw, n + 1)
                    for k in range(KT):
                        ins = pe.matmul(ps[:], xnT[:, k, n * P:(n + 1) * P], w_in[:, k, DI:2 * DI],
                                        start=(k == 0), stop=(k == KT - 1))
                    ins.then_inc(z_ps.sem, 1)
                elif name[:2] == "mx":
                    g = int(name[2])
                    q, kk = Qs[g % 2], Ks[g % 2]
                    if name[3] == "a":
                        b.wait(pe, qks_in[g % 2], (g // 2 + 1) * (2 * TERMS + 1) * 16)
                    for i, e in enumerate(MAX_PART[name[3]]):
                        qb, heads = MAX_FILLS[e]
                        n = (qb + 1) * P
                        ps = next_bank(name, i, b, mx_ok, 11 * g + e + 1)
                        for s, h in enumerate(heads):
                            pe.matmul(ps[:, s * n:(s + 1) * n], q[0:QK_ROWS, h, qb * P:(qb + 1) * P],
                                      kk[0:QK_ROWS, h, 0:n], start=True, stop=False, skip_group_check=True)
                            ins = pe.matmul(ps[:, (s + 1) * n - P:(s + 1) * n], identb[:], mask_qk[:],
                                            start=False, stop=True, skip_group_check=True)
                        ins.then_inc(s_ps.sem, 1)
                elif name[:2] == "mt":
                    g = int(name[2])
                    b.wait(pe, nm_ok, g + 1)
                    ps = next_bank(name, 0, b, mr_ok, 2 * g + 2)
                    pe.transpose(ps[0:16, 0:P], nmx[:], ident[:]).then_inc(s_ps.sem, 1)
                elif name[:2] == "st":
                    g, kb = int(name[2]), int(name[4])
                    q, kk = Qs[g % 2], Ks[g % 2]
                    if kb == 0:
                        b.wait(pe, mrow_in, 32 * (g + 1))
                    for h in range(G):
                        e = (g * TB + kb) * G + h
                        n = L - kb * P
                        ps = next_bank(name, h, b, p_exp, e + 1)
                        pe.matmul(ps[:, 0:n], kk[0:QK_ROWS + 2, h, kb * P:(kb + 1) * P],
                                  q[0:QK_ROWS + 2, h, kb * P:L], start=True, stop=False, skip_group_check=True)
                        pe.matmul(ps[:, 0:P], mask_qk[:], identb[:], start=False, stop=True,
                                  skip_group_check=True).then_inc(t_ps.sem, 1)
                        if kb * G + h >= PV_LAG:
                            probs_v(b, e - PV_LAG)
                    if kb == TB - 1:
                        for late in range(PV_LAG):
                            probs_v(b, e - PV_LAG + 1 + late)
                elif name[:2] == "on":
                    g = int(name[2])
                    b.wait(pe, o_ev, g + 1)
                    turned(name, lambda t: oT[:, t * P:(t + 1) * P], ot_ps, b, on_ok, g + 1)
                elif name[:2] == "ot":
                    k = int(name[2])
                    b.wait(pe, on_ok)
                    turned(name, lambda t: otok[:, t, k * P:(k + 1) * P], at_ps, b, at_ok, k + 1)
                elif name[:2] == "op":
                    n = int(name[2])
                    b.wait(pe, at_ok)
                    ps = next_bank(name, 0, b, x1p_ok, n + 1)
                    for t in range(2):
                        for k in range(KT):
                            ins = pe.matmul(ps[:, t * D:(t + 1) * D], aoT[:, k, (2 * n + t) * P:(2 * n + t + 1) * P],
                                            w_o[:, k, :], start=(k == 0), stop=(k == KT - 1))
                    ins.then_inc(op_ps.sem, 1)
                elif name[:2] == "yt":
                    j = int(name[2])
                    b.wait(pe, gated)
                    turned(name, lambda t: zs[:, t, j * P:(j + 1) * P], yt_ps, b, yt_ok, j + 1)
                elif name[:3] == "sso":
                    n = int(name[3])
                    b.wait(pe, yt_ok)
                    ps = next_bank(name, 0, b, x1_ok, n + 1)
                    for t in range(2):
                        for j in range(J):
                            ins = pe.matmul(ps[:, t * D:(t + 1) * D], ygT[:, j, (2 * n + t) * P:(2 * n + t + 1) * P],
                                            w_ssm[:, j, :], start=(j == 0), stop=(j == J - 1))
                    ins.then_inc(so_ps.sem, 1)
                elif name[:3] == "h2t":
                    k = int(name[3])
                    b.wait(pe, n2)
                    turned(name, lambda t: nrm[:, t, k * P:(k + 1) * P], h2_ps, b, h2_ok, k + 1)
                elif name[:3] == "f1_":
                    f = int(name[3])
                    b.wait(pe, h2_ok)
                    ps = next_bank(name, 0, b, f1_raw, f + 1)
                    for k in range(KT):
                        ins = pe.matmul(ps[:], w_f1[:, k, f * P:(f + 1) * P], h2T[:, k],
                                        start=(k == 0), stop=(k == KT - 1))
                    ins.then_inc(f1_ps.sem, 1)
                elif name[:3] == "f2_":
                    n = int(name[3])
                    b.wait(pe, g_ok)
                    ps = next_bank(name, 0, b, r_ok, n + 1)
                    for t in range(2):
                        for f in range(FT):
                            ins = pe.matmul(ps[:, t * D:(t + 1) * D], gT[:, f, (2 * n + t) * P:(2 * n + t + 1) * P],
                                            w_f2[:, f, :], start=(f == 0), stop=(f == FT - 1))
                    ins.then_inc(f2_ps.sem, 1)
                elif name[:3] == "h3t":
                    k = int(name[3])
                    b.wait(pe, n3)
                    turned(name, lambda t: nrm[:, t, k * P:(k + 1) * P], h3_ps, b, h3_ok, k + 1)
                elif name == "route":
                    b.wait(pe, h3_ok)
                    ps = next_bank(name, 0, b, rt_c, 1)
                    for t in range(TB):
                        for k in range(KT):
                            ins = pe.matmul(ps[:, t * E:(t + 1) * E], h2T[:, k, t * P:(t + 1) * P], w_rt[:, k, :],
                                            start=(k == 0), stop=(k == KT - 1))
                    ins.then_inc(rt_ps.sem, 1)
                elif name == "lora":
                    ps = next_bank(name, 0, b, ax_ok, 1)
                    for t in range(TB):
                        for k in range(KT):
                            ins = pe.matmul(ps[:, t * P:(t + 1) * P], h2T[:, k, t * P:(t + 1) * P], w_la[:, k, :],
                                            start=(k == 0), stop=(k == KT - 1))
                    ins.then_inc(la_ps.sem, 1)
                elif name == "axt":
                    b.wait(pe, ax_ok)
                    turned(name, lambda t: ax[:, t, :], axt_ps, b, axt_ok, 1)
                elif name in ("out0", "out1"):
                    n = int(name[3])
                    b.wait(pe, axt_ok)
                    ps = next_bank(name, 0, b, o_sum, n + 1)
                    for t in range(2):
                        tok = slice((2 * n + t) * P, (2 * n + t + 1) * P)
                        for k in range(KT):
                            pe.matmul(ps[:, t * D:(t + 1) * D], h2T[:, k, tok], w_base[:, k, :],
                                      start=(k == 0), stop=False)
                        ins = pe.matmul(ps[:, t * D:(t + 1) * D], axT[:, tok], w_lb[:], start=False, stop=True)
                    ins.then_inc(out_ps.sem, 1)

            drive(pe, unit, step, banks, after=finish)

        @block.vector
        def _(dve):
            count = [0]

            def link(ins):
                count[0] += 1
                ins.then_inc(dve_c, 1)
                dve.wait_ge(dve_c, count[0])

            v = nc.vector
            dve.wait_ge(built, BUILT)
            dve.wait_ge(w_loaded, 16 * N_LOADS)
            dve.wait_ge(pe_c, 1)
            link(v.tensor_copy(cT, pM[0][:].rearrange("p (k b) -> p k b", b=P)[:, 0:KT, 0:B]))
            for n in range(3):
                dve.wait_ge(pe_c, 2 + n)
                link(v.tensor_copy(mods[0:B, n * 512:(n + 1) * 512], pM[0][0:B, :]))
            dve.wait_ge(pe_c, 5)
            link(v.tensor_copy(w_base[:].rearrange("p k (o q) -> p o k q", o=KT),
                               pM[0][:].rearrange("p (o k q) -> p o k q", o=KT, k=KT)))
            dve.wait_ge(pe_c, 6)
            link(v.tensor_copy(w_rt[:], pM[0][:].rearrange("p (k q) -> p k q", q=P)[:, 0:KT, 0:E]))
            for c in (1, 4):
                link(v.tensor_scalar(mods[0:B, c * D:(c + 1) * D], mods[0:B, c * D:(c + 1) * D], 1.0, None, ALU.add))
            for c in (2, 5):
                gate = mods[0:B, c * D:(c + 1) * D]
                link(v.tensor_scalar(sgn[0:B], gate, 0.0, 2.0, ALU.is_ge, ALU.mult))
                link(v.scalar_tensor_tensor(out=mag[0:B], in0=sgn[0:B], scalar=-1.0, in1=gate,
                                            op0=ALU.add, op1=ALU.mult))
                link(v.tensor_scalar(mag[0:B], mag[0:B], 0.25, None, ALU.max))
                link(v.scalar_tensor_tensor(out=gate, in0=sgn[0:B], scalar=-1.0, in1=mag[0:B],
                                            op0=ALU.add, op1=ALU.mult))
            assert count[0] == MODS_READY
            dve.wait_ge(pe_c, 7)
            link(v.tensor_copy(mod_t.rearrange("p b c -> p c b"),
                               pM[0][:].rearrange("p (c q) -> p c q", q=P)[:, :, 0:B]))
            assert count[0] == MODS_DONE
            link(v.tensor_copy(identb[:], ident[:]))
            link(v.tensor_copy(mask_qk[:], mask_f))
            dve.wait_ge(act_c, 1)
            link(v.tensor_scalar(nalpha, alpha, -1.0, 1.0, ALU.mult, ALU.add))
            link(v.tensor_tensor(w_o[:], w_o[:], alpha.unsqueeze(1).broadcast_to([P, KT, D]), ALU.mult))
            link(v.tensor_tensor(ob_row[:], ob_row[:], alpha, ALU.mult))
            link(v.tensor_tensor(w_ssm[:], w_ssm[:], nalpha.unsqueeze(1).broadcast_to([P, J, D]), ALU.mult))
            link(v.memset(pO[:], 0.0))
            assert count[0] == DVE_SETUP, count[0]

            def stats(b, n, src):
                st, mvt, _ = lns[n]
                for t in range(TB):
                    v.bn_stats(st[:, t, :], src[:, t, :]).then_inc(bn[n].sem, 1)
                b.wait(dve, bn[n])
                v.memset(held[:], 0.0)
                for t in range(TB):
                    v.bn_aggr(mvt[:, t, :], st[:, t, :]).then_inc(mv[n].sem, 1)

            def normalise(b, n, dst, src, sig_):
                _, mvt, rst = lns[n]
                b.wait(dve, rs[n])
                for t in range(TB):
                    v.tensor_scalar(dst[:, t, :], src[:, t, :], mvt[:, t, 0:1], rst[:, t:t + 1],
                                    ALU.subtract, ALU.mult).then_inc(sig_.sem, 1)

            def times_c(b, k):
                n = k // (J // JP)
                b.wait(dve, s_ok, k + 1)
                v.tensor_tensor(state[:, k % RING], state[:, k % RING],
                                bc[:, n % BC_SLOTS, 1, :].unsqueeze(1).broadcast_to([P, JP, L]),
                                ALU.mult).then_inc(p_ok.sem, 1)

            def unit(b, k, first, last):
                b.wait(dve, a_ok, JP * (k + 1))
                b.wait(dve, b_ok, k + 1)
                v.tensor_tensor_scan(state[:, k % RING].rearrange("p j t -> p (j t)"),
                                     decay[:, k % AR].rearrange("p j t -> p (j t)"),
                                     state[:, k % RING].rearrange("p j t -> p (j t)"),
                                     0.0, ALU.mult, ALU.add).then_inc(s_ok.sem, 1)
                if k:
                    times_c(b, k - 1)
                if k == UNITS - 1:
                    times_c(b, k)

            def step(name, b):
                if name == "l0s":
                    b.wait(dve, x_in)
                    stats(b, 0, xt)
                elif name == "l0a":
                    normalise(b, 0, xt, xt, n0)
                elif name == "l1a":
                    b.wait(dve, h_made, 2)
                    stats(b, 1, ht)
                    b.wait(dve, h_made)
                    normalise(b, 1, ht, ht, n1)
                elif name[:2] == "qk":
                    n = int(name[2])
                    b.wait(dve, qk_f, n + 1)
                    if n:
                        b.wait(dve, qk_out, 16 * n)
                    else:
                        b.wait_last(dve, qk_out)
                    v.tensor_copy(qkp[:, 0], qkf[:]).then_inc(qk_s.sem, 1)
                    b.wait(dve, qk_s, 4 * n + 1)
                    v.tensor_tensor(qkf[:], qkf[:], qkp[:, 0], ALU.subtract).then_inc(qk_s.sem, 1)
                    b.wait(dve, qk_s, 4 * n + 2)
                    v.tensor_copy(qkp[:, 1], qkf[:]).then_inc(qk_s.sem, 1)
                    b.wait(dve, qk_s, 4 * n + 3)
                    v.tensor_tensor(qkp[:, 2], qkf[:], qkp[:, 1], ALU.subtract).then_inc(qk_s.sem, 1)
                elif name in ("xs0", "xs1", "xs2", "xs3"):
                    j = int(name[2])
                    b.wait(dve, xs_a, j + 1)
                    for s in range(1, K_CONV):
                        if s > 1:
                            b.wait(dve, xs_c, 3 * j + s - 1)
                        v.scalar_tensor_tensor(
                            out=xc[:, j, s:L], in0=pM[bank_of(name, 0)][:, 0:L - s],
                            scalar=conv_w[:, j, K_CONV - 1 - s:K_CONV - s], in1=xc[:, j, s:L],
                            op0=ALU.mult, op1=ALU.add).then_inc(xs_c.sem, 1)
                elif name == "sp":
                    par = parity(b)
                    b.wait(dve, dt_x)
                    v.tensor_scalar(dts[:, par], us[:, par], SOFTPLUS_CAP, None, ALU.min).then_inc(dt_m.sem, 1)
                    b.wait(dve, dt_e)
                    v.tensor_tensor(dts[:, par], dts[:, par], us[:, par], ALU.max).then_inc(dt_ok.sem, 1)
                elif name == "u":
                    b.wait(dve, u_ok)
                    for j in range(J):
                        v.tensor_scalar(xc[:, j], xc[:, j], D_par[:, j:j + 1], None, ALU.mult).then_inc(xd_ok.sem, 1)
                elif name[:2] == "mx":
                    g = int(name[2])
                    if name[3] == "a" and g:
                        b.wait(dve, nm_ok, g)
                    mxv = mx[:, g % 2].rearrange("p (h q) -> p h q", q=TB)
                    for i, e in enumerate(MAX_PART[name[3]]):
                        qb, heads = MAX_FILLS[e]
                        n = (qb + 1) * P
                        b.wait(dve, s_ps, 12 * g + e + 1)
                        v.tensor_reduce(mxv[:, heads[0]:heads[-1] + 1, qb],
                                        pM[bank_of(name, i)][:, 0:len(heads) * n].rearrange("p (h k) -> p h k", k=n),
                                        AX_X, ALU.max).then_inc(mx_ok.sem, 1)
                    if name[3] == "c":
                        b.wait(dve, mx_ok, 11 * (g + 1))
                        if g:
                            b.wait(dve, s_ps, 12 * g)
                        else:
                            b.wait_last(dve, s_ps)
                        v.tensor_scalar(nmx[:], mx[:, g % 2], -1.0, None, ALU.mult).then_inc(nm_ok.sem, 1)
                elif name[:2] == "mt":
                    g = int(name[2])
                    b.wait(dve, s_ps, 12 * g + 12)
                    if g:
                        b.wait(dve, mrow_in, 32 * g)
                    else:
                        b.wait_last(dve, mrow_in)
                    pS = pM[bank_of(name, 0)]
                    v.tensor_copy(mrow[:, 0], pS[0:16, 0:P]).then_inc(mr_ok.sem, 1)
                    b.wait(dve, mr_ok, 2 * g + 1)
                    v.tensor_tensor(mrow[:, 1], pS[0:16, 0:P], mrow[:, 0], ALU.subtract)\
                     .then_inc(mr_ok.sem, 1)
                elif name[:2] == "on":
                    g = int(name[2])
                    ps = pM[bank_of(name, 0)][:].rearrange("p (t h r) -> p t h r", t=TB, r=32)
                    b.wait(dve, ot_ps, g + 1)
                    if g:
                        b.wait(dve, on_ok, g)
                    v.reciprocal(rden[:], ps[:, :, :, HD]).then_inc(rd_ok.sem, 1)
                    b.wait(dve, rd_ok, g + 1)
                    v.tensor_tensor(otok[:, :, g * G * HD:(g + 1) * G * HD].rearrange("p t (h r) -> p t h r", r=HD),
                                    ps[:, :, :, 0:HD], rden[:].unsqueeze(3).broadcast_to([P, TB, G, HD]),
                                    ALU.mult).then_inc(on_ok.sem, 1)
                elif name[:2] == "op":
                    n = int(name[2])
                    b.wait(dve, op_ps, n + 1)
                    b.wait(dve, x1p_in)
                    v.tensor_tensor(x1[:, 2 * n:2 * n + 2], x1[:, 2 * n:2 * n + 2],
                                    pM[bank_of(name, 0)][:].rearrange("p (t f) -> p t f", t=2), ALU.add)\
                     .then_inc(x1p_ok.sem, 1)
                elif name == "gate":
                    b.wait(dve, y_ok)
                    b.wait(dve, z_ok)
                    for t in range(TB):
                        v.tensor_tensor(zs[:, t], zs[:, t], pY[t][:], ALU.mult).then_inc(gated.sem, 1)
                elif name[:3] == "sso":
                    n = int(name[3])
                    b.wait(dve, so_ps, n + 1)
                    b.wait(dve, x1p_ok)
                    v.tensor_tensor(x1[:, 2 * n:2 * n + 2], x1[:, 2 * n:2 * n + 2],
                                    pM[bank_of(name, 0)][:].rearrange("p (t f) -> p t f", t=2), ALU.add)\
                     .then_inc(x1_ok.sem, 1)
                elif name == "l2s":
                    b.wait(dve, x1_ok)
                    stats(b, 2, x1)
                elif name == "l2a":
                    last_of_attention(b, dve)
                    b.wait_last(dve, out_done)
                    normalise(b, 2, nrm, x1, n2)
                elif name[:3] == "f2_":
                    n = int(name[3])
                    b.wait(dve, f2_ps, n + 1)
                    b.wait(dve, x1b)
                    v.tensor_tensor(x1[:, 2 * n:2 * n + 2], x1[:, 2 * n:2 * n + 2],
                                    pM[bank_of(name, 0)][:].rearrange("p (t f) -> p t f", t=2), ALU.add)\
                     .then_inc(r_ok.sem, 1)
                elif name == "l3a":
                    b.wait(dve, x2_ok)
                    stats(b, 3, xr)
                    normalise(b, 3, nrm, xr, n3)
                elif name == "route":
                    b.wait(dve, rt_ps)
                    v.tensor_tensor(lg[:], pM[bank_of(name, 0)][:, 0:TB * E].rearrange("p (t e) -> p t e", e=E),
                                    rb_row[:].unsqueeze(1).broadcast_to([P, TB, E]), ALU.add)\
                     .then_inc(rt_c.sem, 1)
                    b.wait(dve, rt_c, 1)
                    v.memset(held[:], 0.0)
                    for t in range(TB):
                        v.max(top[:, t, :], lg[:, t, :]).then_inc(rt_c.sem, 1)
                    b.wait(dve, rt_c, 5)
                    v.tensor_tensor(keep[:], lg[:], top[:, :, 1:2].broadcast_to([P, TB, E]), ALU.is_ge)\
                     .then_inc(rt_c.sem, 1)
                    b.wait(dve, rt_c, 6)
                    v.tensor_tensor(lg[:], lg[:], top[:, :, 0:1].broadcast_to([P, TB, E]), ALU.subtract)\
                     .then_inc(rt_c.sem, 1)
                elif name == "route2":
                    b.wait(dve, ex_ok)
                    v.tensor_tensor(ew[:], ew[:], keep[:], ALU.mult).then_inc(ew_ok.sem, 1)
                    b.wait(dve, ew_ok, 1)
                    v.tensor_reduce(esum[:], ew[:], AX_X, ALU.add).then_inc(ew_ok.sem, 1)
                    b.wait(dve, ew_ok, 2)
                    v.reciprocal(esum[:], esum[:]).then_inc(ew_ok.sem, 1)
                    b.wait(dve, ew_ok, 3)
                    v.scalar_tensor_tensor(out=ew[:], in0=ew[:], scalar=LORA_SCALE,
                                           in1=esum[:].unsqueeze(2).broadcast_to([P, TB, E]),
                                           op0=ALU.mult, op1=ALU.mult).then_inc(ew_ok.sem, 1)
                elif name == "lora":
                    b.wait(dve, la_ps)
                    b.wait(dve, ew_ok)
                    v.tensor_tensor(ax.rearrange("p t (e r) -> p t e r", e=E),
                                    pM[bank_of(name, 0)][:].rearrange("p (t e r) -> p t e r", t=TB, e=E),
                                    ew[:].unsqueeze(3).broadcast_to([P, TB, E, LR]), ALU.mult)\
                     .then_inc(ax_ok.sem, 1)
                elif name in ("out0", "out1"):
                    n = int(name[3])
                    b.wait(dve, out_ps, n + 1)
                    v.tensor_tensor(nrm[:, 2 * n:2 * n + 2], pM[bank_of(name, 0)][:].rearrange("p (t f) -> p t f", t=2),
                                    bb_row[:].unsqueeze(1).broadcast_to([P, 2, D]), ALU.add)\
                     .then_inc(o_sum.sem, 1)

            drive(dve, unit, step)


MAX_FILLS = ([(3, [h]) for h in range(G)] + [(2, [h]) for h in range(G)]
             + [(1, [0, 1]), (1, [2, 3]), (0, [0, 1, 2, 3])])
MAX_PART = {"a": range(0, 4), "b": range(4, 8), "c": range(8, 11)}
N_LOADS = 35
CLEARED = 4
BUILT = 11
MODS_READY = 16
MODS_DONE = MODS_READY + 1
DVE_SETUP = MODS_DONE + 7

FIN_SET, PREP_SET = set(FIN), set(PREP)


def make_schedule():
    slots = [[] for _ in range(UNITS)]

    def spread(names, first, last):
        for n, name in enumerate(names):
            slots[first + n * (last - first) // len(names)].append(name)

    spread(FIN, 1, 18)
    spread(Z, 4, 9)
    spread(PREP, 5, 32)
    spread(ATT, 16, 32)
    return slots


SCHEDULE = make_schedule()


def place_products():
    place, n = {}, 0
    for names in SCHEDULE:
        for name in names:
            if name[:2] == "mx":
                products = len(MAX_PART[name[3]])
            elif name[:2] == "st":
                products = G
            else:
                products = 0 if name in NO_PRODUCT else 1
            for i in range(products):
                place[name, i] = n % BANKS
                n += 1
    return place


NO_PRODUCT = {"gate", "l2s", "l2a", "gelu", "x2", "l3a", "route2", "put", "zsilu", "load", "l0s", "l0a", "l1a",
              "xsilu", "sp", "u", "ld0", "ld1", "ld2", "ld3"}
PLACE = place_products()


def bank_of(name, i):
    return PLACE[name, i]


_INS = ["x", "ln1_w", "ln1_b", "ln2_w", "ln2_b", "q_w", "q_b", "k_w", "k_b", "v_w", "v_b", "o_w", "o_b",
        "in_proj_w", "conv_w", "conv_b", "x_proj_w", "dt_w", "dt_b", "A_log", "D_param", "ssm_out_w",
        "mix_weight", "ffn_w1", "ffn_b1", "ffn_w2", "ffn_b2"]
_INS = {**{n: "L0_attn_" + n for n in _INS},
        **{n: "L0_ffn_" + n for n in ("base_w", "base_b", "lora_A", "lora_B", "router_w", "router_b")},
        "c": "L0_c", "wmod": "L0_wmod"}


def kernel(**inputs):
    import numpy as _np
    import concourse.bacc as _bacc
    from concourse import mybir as _mybir
    from concourse.bass_utils import run_bass_kernel_spmd as _run

    nc = _bacc.Bacc("TRN2", target_bir_lowering=False, num_devices=1)
    arrays, args = {}, {}
    for name, full in _INS.items():
        a = _np.ascontiguousarray(inputs[full])
        arrays[f"in_{name}_dram"] = a
        args[name] = nc.dram_tensor(f"in_{name}_dram", a.shape, _mybir.dt.from_np(a.dtype), kind="ExternalInput").ap()
    out = nc.dram_tensor("out_dram", (B, L, D), _mybir.dt.float32, kind="ExternalOutput").ap()
    adaln_block(nc, args, out)
    r = _run(nc, [arrays], core_ids=[0])
    return r.results[0]["out_dram"]
```

```python
from contextlib import ExitStack

import concourse.bass as bass
from concourse import mybir

ALU = mybir.AluOpType
ACT = mybir.ActivationFunctionType
F32 = mybir.dt.float32
BF16 = mybir.dt.bfloat16
AX_X = mybir.AxisListType.X

B, L, D = 32, 512, 256
P = 128
TB = L // P
KT = D // P
H, HD = 16, 16
G = 4
NG = H // G
DI = 2 * D
J = DI // P
N = 16
R = 16
K_CONV = 4
FF = 4 * D
FT = FF // P
E, LR = 8, 16
EPS = 1e-5
LORA_SCALE = 2.0
SOFTPLUS_CAP = 80.0
JP = 2
UNITS = N * J // JP
BANKS = 4
RING = 4
AR = 4
BC_SLOTS = 4
ACT_LEAD = 2
POOL_LEAD = 1
PE_LAG = 3
POOL_C = [k for k in range(UNITS) if k % 4 == 3]
PE_START = 4
Q_PART = [0, 0, 1, 1, 2, 0]
K_PART = [0, 1, 0, 1, 0, 2]
TERMS = len(Q_PART)
QK_LOADS = 8
PV_LAG = 2
QK_ROWS = TERMS * HD
MASKED = -1e30

FIN = ["oe3", "on3", "gate", "yt0", "yt1", "yt2", "yt3", "ot0", "ot1", "op0", "op1", "sso0", "sso1", "l2s", "l2a", "h2t0", "h2t1",
       "f1_0", "f1_1", "f1_2", "f1_3", "f1_4", "f1_5", "f1_6", "f1_7", "gelu", "f2_0", "f2_1",
       "x2", "x2b", "l3s", "l3a", "h3t0", "h3t1", "route", "route2", "lora", "axt", "out0", "out1",
       "gb", "put"]
Z = ["z0", "z1", "z2", "z3", "zsilu", "v0", "v1"]
MAXIMA = [f"{name}{part}" for g in range(NG)
          for name, parts in ((f"ld{g}", [""]), (f"mx{g}", "abcdef"), (f"mt{g}", [""])) for part in parts]
ATT = ([f"{name}{part}" for g in range(NG)
        for name, parts in ([(f"st{g}_{kb}", "ab") for kb in range(TB)] + [(f"oe{g}", [""]), (f"on{g}", [""])])
        for part in parts])[:-2]
PREP = ["load", "l0s", "l0a", "l0b", "l0c", "l1s", "l1a", "xt0", "xt1", "qk0", "qk1", "qk2", "qk3",
        "xs0", "xs1", "xs2", "xs3", "xsilu", "xp", "dt0", "dt1", "dt2", "dt3", "sp1", "sp2", "sp3", "u0", "u1",
        "ud"]


class Signal:

    def __init__(self, sem, per):
        self.sem, self.per = sem, per


class Batch:

    def __init__(self, reg, off):
        self.reg, self.off = reg, off

    @property
    def index(self):
        return self.off if self.reg is None else self.reg * 2 + self.off

    def next(self, n=1):
        return Batch(self.reg, self.off + n)

    def at(self, signal, n=None):
        n = signal.per if n is None else n
        fixed = self.off * signal.per + n
        return fixed if self.reg is None else self.reg * (2 * signal.per) + fixed

    def wait(self, engine, signal, n=None):
        engine.wait_ge(signal.sem, self.at(signal, n))

    def wait_last(self, engine, signal, n=None):
        n = signal.per if n is None else n
        if self.reg is None and self.off == 0:
            return
        engine.wait_ge(signal.sem, self.next(-1).at(signal, n))


class Bank:

    def __init__(self):
        self.last = None

    def fill(self, pe, b, freed_by, n):
        if self.last is not None:
            before, signal, count = self.last
            before.wait(pe, signal, count)
        self.last = b, freed_by, n

    def into_loop(self, reg):
        b, signal, n = self.last
        self.last = Batch(reg, b.off), signal, n
        self.entry = b.off, signal, n

    def out_of_loop(self, turns):
        b, signal, n = self.last
        assert self.entry == (b.off - 2, signal, n)
        self.last = Batch(None, b.off + turns - 2), signal, n


def adaln_block(nc: bass.Bass, d, out):
    ctx = ExitStack()
    with ctx:
        def sb(name, shape, dt=F32):
            return ctx.enter_context(nc.sbuf_tensor(name, shape, dt))

        def pb(name):
            return ctx.enter_context(nc.psum_tensor(name, [P, 512], F32))

        def sem(name):
            return ctx.enter_context(nc.semaphore(name))

        def sig(name, per):
            return Signal(sem(name), per)

        def dram(name, shape, dt=F32):
            return nc.dram_tensor(name, shape, dt).ap()

        mod_rows = dram("mod_rows", (B, 6 * D))
        mod_cols = dram("mod_cols", (B, P, 2 * KT))
        hres_d = dram("hres_d", (B, L, D))
        qk_d = dram("qk_d", (B, 2, 3, D, L), BF16)
        bc_d = dram("bc_d", (B, 2 * N, L))
        ones_d = dram("ones_d", (2, G, L), BF16)

        w_in = sb("w_in", [P, KT, 2 * DI])
        w_qkv = sb("w_qkv", [P, 3, KT, D])
        w_o = sb("w_o", [P, KT, D])
        w_ssm = sb("w_ssm", [P, J, D])
        w_f1 = sb("w_f1", [P, KT, FF])
        w_f2 = sb("w_f2", [P, FT, D])
        w_xp = sb("w_xp", [P, J, P])
        w_dt = sb("w_dt", [P, DI])
        w_base = sb("w_base", [P, KT, D])
        w_la = sb("w_la", [P, KT, E * LR])
        w_lb = sb("w_lb", [P, D])
        w_rt = sb("w_rt", [P, KT, E])
        ident = sb("ident", [P, P])
        identb = sb("identb", [P, P], BF16)
        mask_qk = sb("mask_qk", [P, P], BF16)
        A = sb("A", [P, J, N])
        D_par = sb("D_par", [P, J])
        conv_w = sb("conv_w", [P, J, K_CONV])
        conv_b = sb("conv_b", [P, J])
        dt_b = sb("dt_b", [P, J])
        ln1 = sb("ln1", [P, 2, KT])
        ln2 = sb("ln2", [P, 2, KT])
        qkv_b = sb("qkv_b", [P, 3, KT])
        f1_b = sb("f1_b", [P, FT])
        ob_row = sb("ob_row", [P, D])
        f2b_row = sb("f2b_row", [P, D])
        bb_row = sb("bb_row", [P, D])
        rb_row = sb("rb_row", [P, E])
        eps4 = sb("eps4", [P, TB])
        mhalf4 = sb("mhalf4", [P, TB])

        scan_in = sb("scan_in", [P, 2, 2, J, L])
        dts, us = scan_in[:, :, 0], scan_in[:, :, 1]
        xc = sb("xc", [P, J, L])
        zs = sb("zs", [P, TB, DI])
        decay = sb("decay", [P, AR, JP, L])
        state = sb("state", [P, RING, JP, L])
        bc = sb("bc", [P, BC_SLOTS, 2, L])

        xt = sb("xt", [P, TB, D])
        ht = sb("ht", [P, TB, D])
        mod_a = sb("mod_a", [P, 2, D])
        xnT = sb("xnT", [P, KT, L])
        qkp = sb("qkp", [P, 3, L], BF16)
        dbc = sb("dbc", [P, L])
        qkf = dbc
        vt = sb("vt", [P, TB, H, HD + 1])

        qk_raw = ht[:].rearrange("p (n k) f -> p n k f", n=2)

        def stats_tiles(name):
            return (sb(name + "_st", [P, TB, 6]), sb(name + "_mv", [P, TB, 2]), sb(name + "_rs", [P, TB]))

        lns = [stats_tiles(f"ln{n}") for n in range(4)]

        REGION = 8704
        region = sb("region", [P, REGION])
        at = [0]

        def view(words, dt=F32):
            v = region[:, at[0]:at[0] + words]
            at[0] += words
            assert at[0] <= REGION
            return v if dt == F32 else v.bitcast(dt)

        Qs, Ks = [], []
        for s in range(2):
            Qs.append(view(G * L // 2, BF16).rearrange("p (h t) -> p h t", h=G))
            Ks.append(view(G * L // 2, BF16).rearrange("p (h t) -> p h t", h=G))
        probs = view(G * L).rearrange("p (h t) -> p h t", h=G)
        shared = at[0]
        oT = view(L)
        otok = view(TB * D).rearrange("p (t f) -> p t f", t=TB)
        aoT = view(KT * L).rearrange("p (k t) -> p k t", k=KT)
        at[0] = shared
        h2T = view(KT * L).rearrange("p (k t) -> p k t", k=KT)
        xr = view(TB * D).rearrange("p (t f) -> p t f", t=TB)
        mod_g = view(2 * D).rearrange("p (a f) -> p a f", a=2)

        def gT(b):
            return scan_in[:, b.off % 2].rearrange("p a j t -> p (a j) t")

        def ygT(b):
            return dts[:, b.off % 2]

        def nrm(b):
            return us[:, b.off % 2, 0:2].rearrange("p a (t f) -> p (a t) f", f=D)

        def ax(b):
            return us[:, b.off % 2, 2].rearrange("p (t f) -> p t f", t=TB)

        def axT(b):
            return us[:, b.off % 2, 3]

        at[0] = 0
        c_raw = view(D)
        cT = view(KT * B).rearrange("p (k b) -> p k b", k=KT)
        w_mod = view(KT * 6 * D).rearrange("p (k n) -> p k n", k=KT)
        base_raw = view(KT * D).rearrange("p (o k) -> p o k", o=KT)
        rt_raw = view(D)
        mods = view(6 * D)
        alpha = view(D)
        nalpha = view(D)
        mod_t = view(2 * KT * B).rearrange("p (b c) -> p b c", c=2 * KT)
        ones_b = view(G * L // 2, BF16)
        sgn = view(D)
        mag = view(D)
        mask_f = view(P)

        held = sb("held", [P, 1])
        x1 = sb("x1", [P, TB, D])
        mod_f = sb("mod_f", [P, 2 * KT])
        mx = sb("mx", [P, 2, 16])
        nmx = sb("nmx", [P, 16])
        mrow = sb("mrow", [16, 2, P], BF16)
        rden = sb("rden", [P, TB, G])
        lg = sb("lg", [P, TB, E])
        top = sb("top", [P, TB, 8])
        keep = sb("keep", [P, TB, E])
        ew = top
        esum = sb("esum", [P, TB])

        pY = [pb(f"pY{t}") for t in range(TB)]
        pM = [pb(f"pM{m}") for m in range(BANKS)]
        pO = pM[BANKS - 1]

        w_loaded = sem("w_loaded")
        built = sem("built")
        pool_c, dve_c, act_c, pe_c = sem("pool_c"), sem("dve_c"), sem("act_c"), sem("pe_c")
        mod_stored, ones_stored = sem("mod_stored"), sem("ones_stored")
        x_in, moda_in = sig("x_in", 16), sig("moda_in", 16)
        bn = [sig(f"bn{n}", TB) for n in range(4)]
        mv = [sig(f"mv{n}", TB) for n in range(4)]
        ve = [sig(f"ve{n}", 1) for n in range(4)]
        rs = [sig(f"rs{n}", 1) for n in range(4)]
        n0 = sig("n0", TB)
        h_made = sig("h_made", 3)
        hres_out = sig("hres_out", 16)
        n1 = sig("n1", TB)
        xt_ps, xt_ok = sig("xt_ps", KT), sig("xt_ok", KT)
        qk_ps, qk_f, qk_s, qk_out = sig("qk_ps", 4), sig("qk_f", 4), sig("qk_s", 16), sig("qk_out", 64)
        v_ps, v_ok = sig("v_ps", 2), sig("v_ok", 2)
        xs_ps, xs_a, xs_c, xc_ok = sig("xs_ps", J), sig("xs_a", J), sig("xs_c", 3 * J), sig("xc_ok", 1)
        xp_ps, xp_ok, bc_out = sig("xp_ps", 1), sig("xp_ok", 1), sig("bc_out", 16)
        dt_ps, dt_x, dt_m, dt_e, dt_ok, u_ok = (sig("dt_ps", J), sig("dt_x", J), sig("dt_m", 1),
                                                sig("dt_e", 2), sig("dt_ok", 1), sig("u_ok", 2))
        xd_ok, d_done = sig("xd_ok", J), sig("d_done", 1)
        bc_in = [sem(f"bc_in{s}") for s in range(BC_SLOTS)]
        a_ok, b_ok, s_ok, p_ok, y_ok = (sig("a_ok", UNITS * JP), sig("b_ok", UNITS), sig("s_ok", UNITS),
                                        sig("p_ok", UNITS - len(POOL_C)), sig("y_ok", UNITS))
        pp_ok = sig("pp_ok", len(POOL_C))

        def b_ok_after(k):
            return (pp_ok, POOL_C.index(k) + 1) if k in POOL_C else (b_ok, k + 1)

        def product_after(k):
            return p_ok, k + 1 - sum(c < k for c in POOL_C)

        def wait_product(b, eng, k):
            if k in POOL_C:
                b.wait(eng, pp_ok, POOL_C.index(k) + 1)
            else:
                b.wait(eng, *product_after(k))

        z_ps, z_raw, z_ok = sig("z_ps", TB), sig("z_raw", TB), sig("z_ok", 1)
        qks_in = [sig(f"qks_in{s}", 2 * QK_LOADS * 16) for s in range(2)]
        s_ps, mx_ok = sig("s_ps", 12 * NG), sig("mx_ok", 11 * NG)
        nm_ok, mr_ok, mrow_in = sig("nm_ok", NG), sig("mr_ok", 2 * NG), sig("mrow_in", 32 * NG)
        t_ps, p_exp, pv_ok = sig("t_ps", H * TB), sig("p_exp", H * TB), sig("pv_ok", H * TB)
        o_ev, ot_ps, rd_ok, on_ok = sig("o_ev", NG), sig("ot_ps", NG), sig("rd_ok", NG), sig("on_ok", NG)
        at_ps, at_ok, op_ps, x1p_in, x1p_ok = (sig("at_ps", KT), sig("at_ok", KT), sig("op_ps", 2),
                                               sig("x1p_in", 16), sig("x1p_ok", 2))
        gated = sig("gated", TB)
        yt_ps, yt_ok, so_ps, x1_ok = sig("yt_ps", J), sig("yt_ok", J), sig("so_ps", 2), sig("x1_ok", 2)
        n2, h2_ps, h2_ok, x1b = sig("n2", TB), sig("h2_ps", KT), sig("h2_ok", KT), sig("x1b", 1)
        f1_ps, f1_raw, g_ok = sig("f1_ps", FT), sig("f1_raw", FT), sig("g_ok", 1)
        f2_ps, r_ok = sig("f2_ps", 2), sig("r_ok", 2)
        xr_in, modg_in, modf_in, x2_ok = sig("xr_in", 16), sig("modg_in", 32), sig("modf_in", 16), sig("x2_ok", 2)
        n3, h3_ps, h3_ok = sig("n3", TB), sig("h3_ps", KT), sig("h3_ok", KT)
        rt_ps, rt_c, ex_ok, ew_ok = sig("rt_ps", 1), sig("rt_c", 7), sig("ex_ok", 1), sig("ew_ok", 4)
        la_ps, ax_ok, axt_ps, axt_ok = sig("la_ps", 1), sig("ax_ok", 1), sig("axt_ps", 1), sig("axt_ok", 1)
        out_ps, o_sum, o_gb, o_fin, out_done = (sig("out_ps", 2), sig("o_sum", 2), sig("o_gb", 1),
                                                sig("o_fin", 1), sig("out_done", 16))

        block = ctx.enter_context(nc.Block())

        def last_of_attention(b, eng):
            b.wait(eng, op_ps)

        def drive(eng, unit, step, banks=(), before=None, after=None):
            def turn(b, first, last):
                for k, names in enumerate(SCHEDULE):
                    unit(b, k, first, last)
                    for name in names:
                        if name in FIN_SET:
                            if not first:
                                step(name, b.next(-1))
                        elif name in PREP_SET:
                            if not last:
                                step(name, b.next(1))
                        else:
                            step(name, b)

            for name in PREP:
                step(name, Batch(None, 0))
            if before:
                before(Batch(None, 0))
            turn(Batch(None, 0), True, False)
            with eng.Fori(0, (B - 2) // 2) as i:
                for bank in banks:
                    bank.into_loop(i)
                turn(Batch(i, 1), False, False)
                turn(Batch(i, 2), False, False)
            for bank in banks:
                bank.out_of_loop(B - 2)
            turn(Batch(None, B - 1), False, True)
            if after:
                after(Batch(None, B - 1))
            for name in FIN:
                step(name, Batch(None, B - 1))

        def parity(b):
            return b.off % 2

        @block.sync
        def _(sp):
            n_loads = [0]

            def load(dst, src):
                n_loads[0] += 1
                sp.dma_start(dst, src).then_inc(w_loaded, 16)

            sp.wait_ge(built, CLEARED)
            load(c_raw[0:B, :], d["c"])
            load(w_mod, d["wmod"].rearrange("(k p) n -> p k n", p=P))
            load(w_in[:], d["in_proj_w"].rearrange("(k p) n -> p k n", p=P))
            load(qk_raw[:, 0], d["q_w"].rearrange("(k p) n -> p k n", p=P))
            load(qk_raw[:, 1], d["k_w"].rearrange("(k p) n -> p k n", p=P))
            load(w_qkv[:, 2], d["v_w"].rearrange("(k p) n -> p k n", p=P))
            load(w_o[:], d["o_w"].rearrange("(k p) n -> p k n", p=P))
            load(w_ssm[:], d["ssm_out_w"].rearrange("(j p) n -> p j n", p=P))
            load(w_f1[:], d["ffn_w1"].rearrange("(k p) n -> p k n", p=P))
            load(w_f2[:], d["ffn_w2"].rearrange("(f p) n -> p f n", p=P))
            load(w_dt[0:R, :], d["dt_w"])
            load(base_raw, d["base_w"].rearrange("(o p) k -> p o k", p=P))
            load(rt_raw[0:E, :], d["router_w"])
            load(w_lb[:], d["lora_B"].rearrange("e r o -> (e r) o"))
            load(A[:], d["A_log"].rearrange("(j p) n -> p j n", p=P))
            load(conv_w[:], d["conv_w"].rearrange("(j p) k -> p j k", p=P))
            for row, name in ((ob_row, "o_b"), (f2b_row, "ffn_b2"), (bb_row, "base_b"), (rb_row, "router_b")):
                load(row[:], d[name].partition_broadcast(P))
            load(alpha, d["mix_weight"].partition_broadcast(P))
            with nc.allow_non_contiguous_dma(reason="small vectors, one element per partition"):
                load(w_xp[:, :, 0:R + 2 * N], d["x_proj_w"].rearrange("(j p) n -> p j n", p=P))
                for k in range(KT):
                    load(w_la[:, k, :].rearrange("p (e r) -> p e r", e=E),
                         d["lora_A"][:, k * P:(k + 1) * P, :].rearrange("e p r -> p e r"))
                load(D_par[:], d["D_param"].rearrange("(j p) -> p j", p=P))
                load(conv_b[:], d["conv_b"].rearrange("(j p) -> p j", p=P))
                load(dt_b[:], d["dt_b"].rearrange("(j p) -> p j", p=P))
                load(f1_b[:], d["ffn_b1"].rearrange("(j p) -> p j", p=P))
                for n, w in enumerate(("w", "b")):
                    load(ln1[:, n], d["ln1_" + w].rearrange("(j p) -> p j", p=P))
                    load(ln2[:, n], d["ln2_" + w].rearrange("(j p) -> p j", p=P))
                load(qkv_b[:, 2], d["v_b"].rearrange("(j p) -> p j", p=P))
                for n, w in enumerate(("q", "k")):
                    for g in range(NG):
                        rows = slice(g % 2 * G * HD, (g % 2 + 1) * G * HD)
                        load(qkv_b[rows, n, g // 2:g // 2 + 1],
                             d[w + "_b"][g * G * HD:(g + 1) * G * HD].rearrange("(h r) -> r h", h=G))
            assert n_loads[0] == N_LOADS, n_loads[0]
            sp.wait_ge(dve_c, MODS_DONE)
            sp.dma_start(ones_d.rearrange("o h t -> o (h t)"), ones_b[0:2, :]).then_inc(ones_stored, 16)
            sp.wait_ge(ones_stored, 16)
            sp.dma_start(mod_rows, mods[0:B, :]).then_inc(mod_stored, 16)
            sp.dma_start(mod_cols.rearrange("b p c -> p b c"), mod_t).then_inc(mod_stored, 16)
            sp.wait_ge(mod_stored, 32)

            def bc_row(b, n):
                slot = n % BC_SLOTS
                before, row = (b, n - BC_SLOTS) if n >= BC_SLOTS else (b.next(-1), n - BC_SLOTS + N)
                last = (row + 1) * J // JP - 1
                waits = [b_ok_after(last), product_after(last if last not in POOL_C else last - 1)]
                for a in range(2):
                    if before.reg is not None or before.off >= 0:
                        before.wait(sp, *waits[a])
                    if n == 0 and a == 0:
                        b.wait(sp, bc_out)
                    sp.dma_start(bc[:, slot, a], bc_d[b.index, a * N + n].partition_broadcast(P))\
                      .then_inc(bc_in[slot], 16)

            def unit(b, k, first, last):
                if k == 0:
                    for n in range(BC_SLOTS - 1):
                        bc_row(b, n)
                elif k % (J // JP) == 0:
                    n = k // (J // JP) + BC_SLOTS - 2
                    if n < N:
                        bc_row(b, n)

            def step(name, b):
                if name == "load":
                    b.wait_last(sp, hres_out)
                    b.wait_last(sp, h_made)
                    sp.dma_start(xt[:], d["x"][b.index].rearrange("(t p) f -> p t f", p=P)).then_inc(x_in.sem, 16)
                    sp.dma_start(mod_a[:].rearrange("p a f -> p (a f)"),
                                 mod_rows[b.index, 0:2 * D].partition_broadcast(P)).then_inc(moda_in.sem, 16)
                elif name == "l1a":
                    b.wait(sp, h_made)
                    sp.dma_start(hres_d[b.index].rearrange("(t p) f -> p t f", p=P), xt[:]).then_inc(hres_out.sem, 16)
                elif name[:2] == "qk":
                    n = int(name[2])
                    b.wait(sp, qk_s, 4 * n + 4)
                    sp.dma_start(qk_d[b.index, n // 2, :, (n % 2) * P:(n % 2 + 1) * P].rearrange("c p t -> p c t"),
                                 qkp[:]).then_inc(qk_out.sem, 16)
                elif name == "xp":
                    b.wait(sp, xp_ok)
                    sp.dma_start(bc_d[b.index], dbc[R:R + 2 * N, :]).then_inc(bc_out.sem, 16)
                elif name[:2] == "ld":
                    g = int(name[2])
                    s = g % 2
                    if g == 0:
                        b.wait(sp, qk_out)
                    if g >= 2:
                        b.wait(sp, t_ps, (g - 1) * G * TB)
                    q_src, k_src = (qk_d[b.index, op, :, g * G * HD:(g + 1) * G * HD]
                                    .rearrange("c (r h) t -> c r (h t)", h=G) for op in range(2))
                    pair = 2 * HD
                    for part in range(2):
                        sp.dma_start(Qs[s][part * pair:(part + 1) * pair],
                                     q_src[part:part + 1].broadcast_to([2, HD, G * L])).then_inc(qks_in[s].sem, 16)
                        sp.dma_start(Ks[s][part * pair:(part + 1) * pair], k_src[0:2]).then_inc(qks_in[s].sem, 16)
                    sp.dma_start(Qs[s][2 * pair:2 * pair + HD], q_src[2]).then_inc(qks_in[s].sem, 16)
                    sp.dma_start(Qs[s][2 * pair + HD:3 * pair], q_src[0]).then_inc(qks_in[s].sem, 16)
                    sp.dma_start(Ks[s][2 * pair:3 * pair], k_src[0:3:2]).then_inc(qks_in[s].sem, 16)
                    sp.dma_start(Ks[s][QK_ROWS:QK_ROWS + 2], ones_d).then_inc(qks_in[s].sem, 16)
                elif name[:2] == "mt":
                    g = int(name[2])
                    b.wait(sp, mr_ok, 2 * g + 2)
                    for part in range(2):
                        dst = Qs[g % 2][QK_ROWS + part:QK_ROWS + part + 1].rearrange("o h (q p) -> o (h q) p", p=P)
                        sp.dma_start(dst, mrow[:, part, :]).then_inc(mrow_in.sem, 16)
                    if g < NG - 1:
                        return
                    b.wait_last(sp, x2_ok, 1)
                    b.wait(sp, hres_out)
                    sp.dma_start(x1[:], hres_d[b.index].rearrange("(t p) f -> p t f", p=P)).then_inc(x1p_in.sem, 16)
                elif name == "sso0":
                    last_of_attention(b, sp)
                    b.wait(sp, at_ok)
                    b.wait_last(sp, o_fin)
                    b.wait_last(sp, h3_ok)
                    sp.dma_start(xr, d["x"][b.index].rearrange("(t p) f -> p t f", p=P)).then_inc(xr_in.sem, 16)
                    for a, col in ((0, 2), (1, 5)):
                        sp.dma_start(mod_g[:, a], mod_rows[b.index, col * D:(col + 1) * D].partition_broadcast(P))\
                          .then_inc(modg_in.sem, 16)
                    sp.dma_start(mod_f[:], mod_cols[b.index]).then_inc(modf_in.sem, 16)
                elif name == "put":
                    b.wait(sp, o_fin)
                    sp.dma_start(out[b.index].rearrange("(t p) f -> p t f", p=P), nrm(b)).then_inc(out_done.sem, 16)

            drive(sp, unit, step)
            sp.wait_ge(out_done.sem, 16 * B)
            sp.wait_ge(hres_out.sem, 16 * B)
            sp.wait_ge(qk_out.sem, 64 * B)
            sp.wait_ge(bc_out.sem, 16 * B)

        @block.gpsimd
        def _(pool):
            count = [0]

            def link(ins):
                count[0] += 1
                ins.then_inc(pool_c, 1)
                pool.wait_ge(pool_c, count[0])

            for tile, value in ((c_raw, 0.0), (rt_raw, 0.0), (w_xp[:], 0.0), (w_dt[:], 0.0)):
                nc.gpsimd.memset(tile, value).then_inc(built, 1)
            nc.gpsimd.memset(eps4[:], EPS).then_inc(built, 1)
            nc.gpsimd.memset(mhalf4[:], -0.5).then_inc(built, 1)
            nc.gpsimd.memset(decay[:], 0.0).then_inc(built, 1)
            nc.gpsimd.memset(vt[:], 1.0).then_inc(built, 1)
            nc.gpsimd.memset(ones_b, 1.0).then_inc(built, 1)
            link(nc.gpsimd.memset(ident[:], 0.0))
            nc.gpsimd.affine_select(out=ident[:], in_=ident[:], compare_op=ALU.not_equal, fill=1.0,
                                    base=0, pattern=[[-1, P]], channel_multiplier=1).then_inc(built, 1)
            link(nc.gpsimd.memset(mask_f, 0.0))
            nc.gpsimd.affine_select(out=mask_f, in_=mask_f, compare_op=ALU.is_ge, fill=MASKED,
                                    base=0, pattern=[[-1, P]], channel_multiplier=1).then_inc(built, 1)

            def rstd(b, n):
                b.wait(pool, mv[n])
                nc.gpsimd.tensor_tensor(lns[n][2][:], lns[n][1][:, :, 1], eps4[:], ALU.add).then_inc(ve[n].sem, 1)
                b.wait(pool, ve[n])
                nc.gpsimd.tensor_tensor(lns[n][2][:], lns[n][2][:], mhalf4[:], ALU.pow).then_inc(rs[n].sem, 1)

            def row(ap):
                return ap.unsqueeze(1).broadcast_to([P, TB, D])

            def unit(b, k, first, last):
                if k < UNITS - POOL_LEAD:
                    fill_state(b, k + POOL_LEAD)
                elif not last:
                    fill_state(b.next(1), k + POOL_LEAD - UNITS)
                if k in POOL_C:
                    b.wait(pool, s_ok, k + 1)
                    nc.gpsimd.tensor_tensor(state[:, k % RING], state[:, k % RING],
                                            bc[:, k // (J // JP) % BC_SLOTS, 1, :].unsqueeze(1)
                                            .broadcast_to([P, JP, L]), ALU.mult).then_inc(pp_ok.sem, 1)

            def start(b):
                for k in range(POOL_LEAD):
                    fill_state(b, k)

            def fill_state(b, k):
                n, jp = k // (J // JP), k % (J // JP)
                if k == 0:
                    b.wait(pool, u_ok)
                if jp == 0:
                    slot = n % BC_SLOTS
                    per = len(range(slot, N, BC_SLOTS))
                    b.wait(pool, Signal(bc_in[slot], 32 * per), 32 * (n // BC_SLOTS + 1))
                if k >= RING:
                    b.wait(pool, y_ok, k - RING + 1)
                else:
                    b.wait_last(pool, y_ok, UNITS + k - RING + 1)
                par = parity(b)
                nc.gpsimd.tensor_tensor(state[:, k % RING], us[:, par, jp * JP:(jp + 1) * JP, :],
                                        bc[:, n % BC_SLOTS, 0, :].unsqueeze(1).broadcast_to([P, JP, L]),
                                        ALU.mult).then_inc(b_ok.sem, 1)

            def step(name, b):
                if name == "l0s":
                    rstd(b, 0)
                elif name == "l0a":
                    b.wait(pool, n0)
                    b.wait(pool, moda_in)
                    b.wait_last(pool, xt_ps)
                    nc.gpsimd.tensor_tensor(ht[:], xt[:], row(mod_a[:, 1, :]), ALU.mult).then_inc(h_made.sem, 1)
                elif name == "l0b":
                    b.wait(pool, h_made, 1)
                    nc.gpsimd.tensor_tensor(ht[:], ht[:], row(mod_a[:, 0, :]), ALU.add).then_inc(h_made.sem, 1)
                elif name == "l0c":
                    b.wait(pool, h_made, 2)
                    nc.gpsimd.tensor_tensor(xt[:], ht[:], row(ob_row[:]), ALU.add).then_inc(h_made.sem, 1)
                elif name == "l1s":
                    rstd(b, 1)
                elif name in ("u0", "u1"):
                    par = parity(b)
                    half = slice(int(name[1]) * J // 2, (int(name[1]) + 1) * J // 2)
                    b.wait(pool, dt_ok)
                    nc.gpsimd.tensor_tensor(us[:, par, half], dts[:, par, half], xc[:, half], ALU.mult)\
                      .then_inc(u_ok.sem, 1)
                elif name == "l2s":
                    rstd(b, 2)
                elif name == "f1_0":
                    b.wait(pool, n2)
                    nc.gpsimd.tensor_tensor(x1[:], x1[:], row(f2b_row[:]), ALU.add).then_inc(x1b.sem, 1)
                elif name == "x2":
                    b.wait(pool, r_ok)
                    b.wait(pool, modg_in)
                    b.wait(pool, xr_in)
                    nc.gpsimd.tensor_tensor(nrm(b), x1[:], row(mod_g[:, 0, :]), ALU.mult).then_inc(x2_ok.sem, 1)
                elif name == "x2b":
                    b.wait(pool, x2_ok, 1)
                    nc.gpsimd.tensor_tensor(xr, xr, nrm(b), ALU.add).then_inc(x2_ok.sem, 1)
                elif name == "l3s":
                    rstd(b, 3)
                elif name == "gb":
                    b.wait(pool, o_sum)
                    nc.gpsimd.tensor_tensor(nrm(b), nrm(b), row(mod_g[:, 1, :]), ALU.mult).then_inc(o_gb.sem, 1)
                elif name == "put":
                    b.wait(pool, o_gb)
                    nc.gpsimd.tensor_tensor(nrm(b), nrm(b), xr, ALU.add).then_inc(o_fin.sem, 1)

            pool.wait_ge(built, BUILT)
            drive(pool, unit, step, before=start)

        @block.scalar
        def _(act):
            act.wait_ge(w_loaded, 16 * N_LOADS)
            act.activation(alpha, alpha, ACT.Sigmoid).then_inc(act_c, 1)
            act.activation(A[:], A[:], ACT.Exp).then_inc(act_c, 1)
            act.activation(c_raw, c_raw, ACT.Silu).then_inc(act_c, 1)
            act.wait_ge(act_c, 3)
            act.activation(A[:], A[:], ACT.Copy, scale=-1.0).then_inc(act_c, 1)
            act.wait_ge(built, BUILT)
            act.wait_ge(act_c, 4)

            def unit(b, k, first, last):
                if k < UNITS - ACT_LEAD:
                    decays(b, k + ACT_LEAD)
                elif not last:
                    decays(b.next(1), k + ACT_LEAD - UNITS)

            def start(b):
                for k in range(ACT_LEAD):
                    decays(b, k)

            def decays(b, k):
                n, jp = k // (J // JP), k % (J // JP)
                par = parity(b)
                if k == 0:
                    b.wait(act, dt_ok)
                if k >= AR:
                    b.wait(act, s_ok, k - AR + 1)
                else:
                    b.wait_last(act, s_ok, UNITS + k - AR + 1)
                for jj in range(JP):
                    j = jp * JP + jj
                    act.activation(decay[:, k % AR, jj, 1:L], dts[:, par, j, 1:L], ACT.Exp,
                                   scale=A[:, j, n:n + 1]).then_inc(a_ok.sem, 1)

            def step(name, b):
                if name[:2] == "xt":
                    k = int(name[2])
                    b.wait(act, xt_ps, k + 1)
                    if k == 0:
                        b.wait_last(act, z_ps)
                        b.wait_last(act, xs_ps)
                        b.wait_last(act, v_ps)
                    act.activation(xnT[:, k], pM[bank_of(name, 0)][:], ACT.Identity, scale=ln1[:, 0, k:k + 1],
                                   bias=ln1[:, 1, k:k + 1]).then_inc(xt_ok.sem, 1)
                elif name[:2] == "qk":
                    n = int(name[2])
                    b.wait(act, qk_ps, n + 1)
                    if n:
                        b.wait(act, qk_s, 4 * n)
                    else:
                        b.wait_last(act, qk_s)
                        b.wait_last(act, dt_ps)
                        b.wait_last(act, bc_out)
                    act.activation(qkf[:], pM[bank_of(name, 0)][:], ACT.Identity, bias=qkv_b[:, n // 2, n % 2:n % 2 + 1])\
                       .then_inc(qk_f.sem, 1)
                elif name[0] == "v":
                    n = int(name[1])
                    b.wait(act, v_ps, n + 1)
                    b.wait_last(act, pv_ok)
                    act.activation(vt[:, 2 * n:2 * n + 2, :, 0:HD],
                                   pM[bank_of(name, 0)][:].rearrange("p (t h r) -> p t h r", t=2, h=H),
                                   ACT.Copy).then_inc(v_ok.sem, 1)
                elif name[:3] in ("xs0", "xs1", "xs2", "xs3"):
                    j = int(name[2])
                    b.wait(act, xs_ps, j + 1)
                    b.wait_last(act, d_done)
                    act.activation(xc[:, j], pM[bank_of(name, 0)][:], ACT.Identity, scale=conv_w[:, j, K_CONV - 1:K_CONV],
                                   bias=conv_b[:, j:j + 1]).then_inc(xs_a.sem, 1)
                elif name == "xsilu":
                    b.wait(act, xs_c)
                    act.activation(xc[:], xc[:], ACT.Silu).then_inc(xc_ok.sem, 1)
                elif name == "xp":
                    b.wait(act, xp_ps)
                    b.wait(act, qk_s)
                    act.activation(dbc[:], pM[bank_of(name, 0)][:], ACT.Copy).then_inc(xp_ok.sem, 1)
                elif name[:2] == "dt":
                    j = int(name[2])
                    b.wait(act, dt_ps, j + 1)
                    if not (b.reg is None and b.off < 2):
                        b.next(-2).wait(act, out_done)
                    act.activation(us[:, parity(b), j], pM[bank_of(name, 0)][:], ACT.Identity, bias=dt_b[:, j:j + 1])\
                       .then_inc(dt_x.sem, 1)
                elif name == "sp2":
                    par = parity(b)
                    b.wait(act, dt_m)
                    act.activation(dts[:, par], dts[:, par], ACT.Exp).then_inc(dt_e.sem, 1)
                    b.wait(act, dt_e, 1)
                    act.activation(dts[:, par], dts[:, par], ACT.Ln, bias=1.0).then_inc(dt_e.sem, 1)
                elif name in ("z0", "z1", "z2", "z3"):
                    n = int(name[1])
                    b.wait(act, z_ps, n + 1)
                    b.wait_last(act, yt_ps)
                    act.activation(zs[:, n], pM[bank_of(name, 0)][:], ACT.Copy).then_inc(z_raw.sem, 1)
                elif name == "zsilu":
                    b.wait(act, z_raw)
                    act.activation(zs[:], zs[:], ACT.Silu).then_inc(z_ok.sem, 1)
                elif name[:2] == "st":
                    g, kb = int(name[2]), int(name[4])
                    for h in HALF[name[5]]:
                        e = (g * TB + kb) * G + h
                        n = L - kb * P
                        b.wait(act, t_ps, e + 1)
                        if e >= G:
                            b.wait(act, pv_ok, e - G + 1)
                        else:
                            b.wait_last(act, pv_ok, H * TB - G + e + 1)
                        act.activation(probs[:, h, 0:n], pM[bank_of(name, h % 2)][:, 0:n], ACT.Exp, scale=HD ** -0.5)\
                           .then_inc(p_exp.sem, 1)
                elif name[:2] == "oe":
                    g = int(name[2])
                    b.wait(act, pv_ok, (g + 1) * G * TB)
                    if g:
                        b.wait(act, ot_ps, g)
                    else:
                        b.wait_last(act, o_fin)
                    act.activation(oT, pO[:], ACT.Copy).then_inc(o_ev.sem, 1)
                elif name[:2] == "ot":
                    k = int(name[2])
                    b.wait(act, at_ps, k + 1)
                    act.activation(aoT[:, k], pM[bank_of(name, 0)][:], ACT.Identity, bias=qkv_b[:, 2, k:k + 1])\
                       .then_inc(at_ok.sem, 1)
                elif name[:2] == "yt":
                    j = int(name[2])
                    b.wait(act, yt_ps, j + 1)
                    b.wait_last(act, so_ps)
                    act.activation(ygT(b)[:, j], pM[bank_of(name, 0)][:], ACT.Copy).then_inc(yt_ok.sem, 1)
                elif name[:3] == "h2t":
                    k = int(name[3])
                    b.wait(act, h2_ps, k + 1)
                    act.activation(h2T[:, k], pM[bank_of(name, 0)][:], ACT.Identity, scale=ln2[:, 0, k:k + 1],
                                   bias=ln2[:, 1, k:k + 1]).then_inc(h2_ok.sem, 1)
                elif name[:3] == "f1_":
                    f = int(name[3])
                    b.wait(act, f1_ps, f + 1)
                    act.activation(gT(b)[:, f], pM[bank_of(name, 0)][:], ACT.Identity, bias=f1_b[:, f:f + 1])\
                       .then_inc(f1_raw.sem, 1)
                elif name == "gelu":
                    b.wait(act, f1_raw)
                    act.activation(gT(b), gT(b), ACT.Gelu).then_inc(g_ok.sem, 1)
                elif name[:3] == "h3t":
                    k = int(name[3])
                    b.wait(act, h3_ps, k + 1)
                    b.wait(act, modf_in)
                    act.activation(h2T[:, k], pM[bank_of(name, 0)][:], ACT.Identity, scale=mod_f[:, KT + k:KT + k + 1],
                                   bias=mod_f[:, k:k + 1]).then_inc(h3_ok.sem, 1)
                elif name == "route2":
                    b.wait(act, rt_c)
                    act.activation(ew[:], lg[:], ACT.Exp).then_inc(ex_ok.sem, 1)
                elif name == "axt":
                    b.wait(act, axt_ps)
                    act.activation(axT(b), pM[bank_of(name, 0)][:], ACT.Copy).then_inc(axt_ok.sem, 1)

            drive(act, unit, step, before=start)

        @block.tensor
        def _(pe):
            pe.wait_ge(w_loaded, 16 * N_LOADS)
            pe.wait_ge(built, BUILT)
            pe.wait_ge(act_c, 3)
            n_pe = [0]

            def done(ins, read_by):
                n_pe[0] += 1
                ins.then_inc(pe_c, 1)
                pe.wait_ge(dve_c, read_by)

            for k in range(KT):
                t = pe.transpose(pM[0][:, k * P:(k + 1) * P], c_raw[:, k * P:(k + 1) * P], ident[:])
            done(t, 1)
            for n in range(3):
                for k in range(KT):
                    t = pe.matmul(pM[0][0:B, :], cT[:, k, :], w_mod[:, k, n * 512:(n + 1) * 512],
                                  start=(k == 0), stop=(k == KT - 1))
                done(t, 2 + n)
            for o in range(KT):
                for k in range(KT):
                    t = pe.transpose(pM[0][:, (o * KT + k) * P:(o * KT + k + 1) * P],
                                     base_raw[:, o, k * P:(k + 1) * P], ident[:])
            done(t, 5)
            for k in range(KT):
                t = pe.transpose(pM[0][:, k * P:(k + 1) * P], rt_raw[:, k * P:(k + 1) * P], ident[:])
            done(t, 6)
            pe.wait_ge(dve_c, MODS_READY)
            for c in range(2 * KT):
                t = pe.transpose(pM[0][:, c * P:(c + 1) * P], mods[:, 3 * D + c * P:3 * D + (c + 1) * P], ident[:])
            done(t, MODS_DONE)
            pe.wait_ge(dve_c, DVE_SETUP)

            banks = [Bank() for _ in range(BANKS)]

            def next_bank(name, i, b, freed_by, n):
                banks[bank_of(name, i)].fill(pe, b, freed_by, n)
                return pM[bank_of(name, i)]


            def skip_part(b):
                b.wait(pe, xd_ok)
                b.wait_last(pe, gated)
                for j in range(J):
                    for t in range(TB):
                        ins = pe.matmul(pY[t][:, j * P:(j + 1) * P], xc[:, j, t * P:(t + 1) * P], ident[:],
                                        is_transpose=True, start=(j == 0), stop=False, skip_group_check=True)
                ins.then_inc(d_done.sem, 1)

            def add(b, a):
                wait_product(b, pe, a)
                for jj in range(JP):
                    j = (a % (J // JP)) * JP + jj
                    for t in range(TB):
                        ins = pe.matmul(pY[t][:, j * P:(j + 1) * P], state[:, a % RING, jj, t * P:(t + 1) * P],
                                        ident[:], is_transpose=True, start=False,
                                        stop=(a >= UNITS - J // JP), skip_group_check=True)
                ins.then_inc(y_ok.sem, 1)

            def unit(b, k, first, last):
                if k < PE_LAG:
                    if not first:
                        add(b.next(-1), UNITS - PE_LAG + k)
                elif k == PE_START:
                    skip_part(b)
                    for a in range(PE_START - PE_LAG + 1):
                        add(b, a)
                elif k > PE_START:
                    add(b, k - PE_LAG)

            def finish(b):
                for a in range(UNITS - PE_LAG, UNITS):
                    add(b, a)

            def turned(name, src, sig_, b, freed_by, n):
                ps = next_bank(name, 0, b, freed_by, n)
                for t in range(TB):
                    ins = pe.transpose(ps[:, t * P:(t + 1) * P], src(t), ident[:])
                ins.then_inc(sig_.sem, 1)

            def probs_v(b, e):
                g, kb, h = e // (TB * G), e // G % TB, e % G
                if e % (TB * G) == 0:
                    b.wait(pe, v_ok)
                    banks[BANKS - 1].fill(pe, b, o_ev, g + 1)
                b.wait(pe, p_exp, e + 1)
                pe.matmul(pO[32 * h:32 * h + HD + 1, kb * P:L], vt[:, kb, g * G + h, :],
                          probs[:, h, 0:L - kb * P], start=(kb == 0), stop=(kb == TB - 1),
                          skip_group_check=True).then_inc(pv_ok.sem, 1)

            def step(name, b):
                if name[:2] == "xt":
                    k = int(name[2])
                    b.wait(pe, n1)
                    turned(name, lambda t: ht[:, t, k * P:(k + 1) * P], xt_ps, b, xt_ok, k + 1)
                elif name[:2] == "qk":
                    n = int(name[2])
                    b.wait(pe, xt_ok)
                    ps = next_bank(name, 0, b, qk_f, n + 1)
                    for k in range(KT):
                        ins = pe.matmul(ps[:], w_qkv[:, n // 2, k, (n % 2) * P:(n % 2 + 1) * P], xnT[:, k],
                                        start=(k == 0), stop=(k == KT - 1))
                    ins.then_inc(qk_ps.sem, 1)
                elif name[0] == "v":
                    n = int(name[1])
                    ps = next_bank(name, 0, b, v_ok, n + 1)
                    for t in range(2):
                        for k in range(KT):
                            ins = pe.matmul(ps[:, t * D:(t + 1) * D], xnT[:, k, (2 * n + t) * P:(2 * n + t + 1) * P],
                                            w_qkv[:, 2, k, :], start=(k == 0), stop=(k == KT - 1))
                    ins.then_inc(v_ps.sem, 1)
                elif name in ("xs0", "xs1", "xs2", "xs3"):
                    j = int(name[2])
                    ps = next_bank(name, 0, b, xs_c, 3 * j + 3)
                    for k in range(KT):
                        ins = pe.matmul(ps[:], w_in[:, k, j * P:(j + 1) * P], xnT[:, k],
                                        start=(k == 0), stop=(k == KT - 1))
                    ins.then_inc(xs_ps.sem, 1)
                elif name == "xp":
                    b.wait(pe, xc_ok)
                    ps = next_bank(name, 0, b, xp_ok, 1)
                    for j in range(J):
                        ins = pe.matmul(ps[:], w_xp[:, j, :], xc[:, j], start=(j == 0), stop=(j == J - 1))
                    ins.then_inc(xp_ps.sem, 1)
                elif name[:2] == "dt":
                    j = int(name[2])
                    b.wait(pe, xp_ok)
                    ps = next_bank(name, 0, b, dt_x, j + 1)
                    pe.matmul(ps[:], w_dt[:, j * P:(j + 1) * P], dbc[:], start=True, stop=True)\
                      .then_inc(dt_ps.sem, 1)
                elif name in ("z0", "z1", "z2", "z3"):
                    n = int(name[1])
                    b.wait(pe, xt_ok)
                    ps = next_bank(name, 0, b, z_raw, n + 1)
                    for k in range(KT):
                        ins = pe.matmul(ps[:], xnT[:, k, n * P:(n + 1) * P], w_in[:, k, DI:2 * DI],
                                        start=(k == 0), stop=(k == KT - 1))
                    ins.then_inc(z_ps.sem, 1)
                elif name[:2] == "mx":
                    g = int(name[2])
                    q, kk = Qs[g % 2], Ks[g % 2]
                    if name[3] == "a":
                        b.wait(pe, qks_in[g % 2], (g // 2 + 1) * QK_LOADS * 16)
                    for i, e in enumerate(MAX_PART[name[3]]):
                        qb, heads = MAX_FILLS[e]
                        n = (qb + 1) * P
                        ps = next_bank(name, i, b, mx_ok, 11 * g + e + 1)
                        for s, h in enumerate(heads):
                            pe.matmul(ps[:, s * n:(s + 1) * n], q[0:QK_ROWS, h, qb * P:(qb + 1) * P],
                                      kk[0:QK_ROWS, h, 0:n], start=True, stop=False, skip_group_check=True)
                            ins = pe.matmul(ps[:, (s + 1) * n - P:(s + 1) * n], identb[:], mask_qk[:],
                                            start=False, stop=True, skip_group_check=True)
                        ins.then_inc(s_ps.sem, 1)
                elif name[:2] == "mt":
                    g = int(name[2])
                    b.wait(pe, nm_ok, g + 1)
                    ps = next_bank(name, 0, b, mr_ok, 2 * g + 2)
                    pe.transpose(ps[0:16, 0:P], nmx[:], ident[:]).then_inc(s_ps.sem, 1)
                elif name[:2] == "st":
                    g, kb = int(name[2]), int(name[4])
                    q, kk = Qs[g % 2], Ks[g % 2]
                    if kb == 0:
                        b.wait(pe, mrow_in, 32 * (g + 1))
                    for h in HALF[name[5]]:
                        e = (g * TB + kb) * G + h
                        n = L - kb * P
                        ps = next_bank(name, h % 2, b, p_exp, e + 1)
                        pe.matmul(ps[:, 0:n], kk[0:QK_ROWS + 2, h, kb * P:(kb + 1) * P],
                                  q[0:QK_ROWS + 2, h, kb * P:L], start=True, stop=False, skip_group_check=True)
                        pe.matmul(ps[:, 0:P], mask_qk[:], identb[:], start=False, stop=True,
                                  skip_group_check=True).then_inc(t_ps.sem, 1)
                        if kb * G + h >= PV_LAG:
                            probs_v(b, e - PV_LAG)
                    if kb == TB - 1 and name[5] == "b":
                        for late in range(PV_LAG):
                            probs_v(b, e - PV_LAG + 1 + late)
                elif name[:2] == "on":
                    g = int(name[2])
                    b.wait(pe, o_ev, g + 1)
                    turned(name, lambda t: oT[:, t * P:(t + 1) * P], ot_ps, b, on_ok, g + 1)
                elif name[:2] == "ot":
                    k = int(name[2])
                    b.wait(pe, on_ok)
                    turned(name, lambda t: otok[:, t, k * P:(k + 1) * P], at_ps, b, at_ok, k + 1)
                elif name[:2] == "op":
                    n = int(name[2])
                    b.wait(pe, at_ok)
                    ps = next_bank(name, 0, b, x1p_ok, n + 1)
                    for t in range(2):
                        for k in range(KT):
                            ins = pe.matmul(ps[:, t * D:(t + 1) * D], aoT[:, k, (2 * n + t) * P:(2 * n + t + 1) * P],
                                            w_o[:, k, :], start=(k == 0), stop=(k == KT - 1))
                    ins.then_inc(op_ps.sem, 1)
                elif name[:2] == "yt":
                    j = int(name[2])
                    b.wait(pe, gated)
                    turned(name, lambda t: zs[:, t, j * P:(j + 1) * P], yt_ps, b, yt_ok, j + 1)
                elif name[:3] == "sso":
                    n = int(name[3])
                    b.wait(pe, yt_ok)
                    ps = next_bank(name, 0, b, x1_ok, n + 1)
                    for t in range(2):
                        for j in range(J):
                            ins = pe.matmul(ps[:, t * D:(t + 1) * D], ygT(b)[:, j, (2 * n + t) * P:(2 * n + t + 1) * P],
                                            w_ssm[:, j, :], start=(j == 0), stop=(j == J - 1))
                    ins.then_inc(so_ps.sem, 1)
                elif name[:3] == "h2t":
                    k = int(name[3])
                    b.wait(pe, n2)
                    turned(name, lambda t: nrm(b)[:, t, k * P:(k + 1) * P], h2_ps, b, h2_ok, k + 1)
                elif name[:3] == "f1_":
                    f = int(name[3])
                    b.wait(pe, h2_ok)
                    ps = next_bank(name, 0, b, f1_raw, f + 1)
                    for k in range(KT):
                        ins = pe.matmul(ps[:], w_f1[:, k, f * P:(f + 1) * P], h2T[:, k],
                                        start=(k == 0), stop=(k == KT - 1))
                    ins.then_inc(f1_ps.sem, 1)
                elif name[:3] == "f2_":
                    n = int(name[3])
                    b.wait(pe, g_ok)
                    ps = next_bank(name, 0, b, r_ok, n + 1)
                    for t in range(2):
                        for f in range(FT):
                            ins = pe.matmul(ps[:, t * D:(t + 1) * D], gT(b)[:, f, (2 * n + t) * P:(2 * n + t + 1) * P],
                                            w_f2[:, f, :], start=(f == 0), stop=(f == FT - 1))
                    ins.then_inc(f2_ps.sem, 1)
                elif name[:3] == "h3t":
                    k = int(name[3])
                    b.wait(pe, n3)
                    turned(name, lambda t: nrm(b)[:, t, k * P:(k + 1) * P], h3_ps, b, h3_ok, k + 1)
                elif name == "route":
                    b.wait(pe, h3_ok)
                    ps = next_bank(name, 0, b, rt_c, 1)
                    for t in range(TB):
                        for k in range(KT):
                            ins = pe.matmul(ps[:, t * E:(t + 1) * E], h2T[:, k, t * P:(t + 1) * P], w_rt[:, k, :],
                                            start=(k == 0), stop=(k == KT - 1))
                    ins.then_inc(rt_ps.sem, 1)
                elif name == "lora":
                    ps = next_bank(name, 0, b, ax_ok, 1)
                    for t in range(TB):
                        for k in range(KT):
                            ins = pe.matmul(ps[:, t * P:(t + 1) * P], h2T[:, k, t * P:(t + 1) * P], w_la[:, k, :],
                                            start=(k == 0), stop=(k == KT - 1))
                    ins.then_inc(la_ps.sem, 1)
                elif name == "axt":
                    b.wait(pe, ax_ok)
                    turned(name, lambda t: ax(b)[:, t, :], axt_ps, b, axt_ok, 1)
                elif name in ("out0", "out1"):
                    n = int(name[3])
                    b.wait(pe, axt_ok)
                    ps = next_bank(name, 0, b, o_sum, n + 1)
                    for t in range(2):
                        tok = slice((2 * n + t) * P, (2 * n + t + 1) * P)
                        for k in range(KT):
                            pe.matmul(ps[:, t * D:(t + 1) * D], h2T[:, k, tok], w_base[:, k, :],
                                      start=(k == 0), stop=False)
                        ins = pe.matmul(ps[:, t * D:(t + 1) * D], axT(b)[:, tok], w_lb[:], start=False, stop=True)
                    ins.then_inc(out_ps.sem, 1)

            drive(pe, unit, step, banks, after=finish)

        @block.vector
        def _(dve):
            count = [0]

            def link(ins):
                count[0] += 1
                ins.then_inc(dve_c, 1)
                dve.wait_ge(dve_c, count[0])

            v = nc.vector
            dve.wait_ge(built, BUILT)
            dve.wait_ge(w_loaded, 16 * N_LOADS)
            dve.wait_ge(pe_c, 1)
            link(v.tensor_copy(cT, pM[0][:].rearrange("p (k b) -> p k b", b=P)[:, 0:KT, 0:B]))
            for n in range(3):
                dve.wait_ge(pe_c, 2 + n)
                link(v.tensor_copy(mods[0:B, n * 512:(n + 1) * 512], pM[0][0:B, :]))
            dve.wait_ge(pe_c, 5)
            link(v.tensor_copy(w_base[:].rearrange("p k (o q) -> p o k q", o=KT),
                               pM[0][:].rearrange("p (o k q) -> p o k q", o=KT, k=KT)))
            dve.wait_ge(pe_c, 6)
            link(v.tensor_copy(w_rt[:], pM[0][:].rearrange("p (k q) -> p k q", q=P)[:, 0:KT, 0:E]))
            for c in (1, 4):
                link(v.tensor_scalar(mods[0:B, c * D:(c + 1) * D], mods[0:B, c * D:(c + 1) * D], 1.0, None, ALU.add))
            for c in (2, 5):
                gate = mods[0:B, c * D:(c + 1) * D]
                link(v.tensor_scalar(sgn[0:B], gate, 0.0, 2.0, ALU.is_ge, ALU.mult))
                link(v.scalar_tensor_tensor(out=mag[0:B], in0=sgn[0:B], scalar=-1.0, in1=gate,
                                            op0=ALU.add, op1=ALU.mult))
                link(v.tensor_scalar(mag[0:B], mag[0:B], 0.25, None, ALU.max))
                link(v.scalar_tensor_tensor(out=gate, in0=sgn[0:B], scalar=-1.0, in1=mag[0:B],
                                            op0=ALU.add, op1=ALU.mult))
            assert count[0] == MODS_READY
            dve.wait_ge(pe_c, 7)
            link(v.tensor_copy(mod_t.rearrange("p b c -> p c b"),
                               pM[0][:].rearrange("p (c q) -> p c q", q=P)[:, :, 0:B]))
            assert count[0] == MODS_DONE
            link(v.tensor_copy(identb[:], ident[:]))
            for n in range(2):
                for k in range(KT):
                    link(v.tensor_copy(w_qkv[:, n, k].rearrange("p (g r h) -> p g r h", g=NG, h=G),
                                       qk_raw[:, n, k].rearrange("p (g h r) -> p g r h", g=NG, h=G)))
            link(v.tensor_copy(mask_qk[:], mask_f))
            dve.wait_ge(act_c, 1)
            link(v.tensor_scalar(nalpha, alpha, -1.0, 1.0, ALU.mult, ALU.add))
            link(v.tensor_tensor(w_o[:], w_o[:], alpha.unsqueeze(1).broadcast_to([P, KT, D]), ALU.mult))
            link(v.tensor_tensor(ob_row[:], ob_row[:], alpha, ALU.mult))
            link(v.tensor_tensor(w_ssm[:], w_ssm[:], nalpha.unsqueeze(1).broadcast_to([P, J, D]), ALU.mult))
            link(v.memset(pO[:], 0.0))
            assert count[0] == DVE_SETUP, count[0]

            def stats(b, n, src):
                st, mvt, _ = lns[n]
                for t in range(TB):
                    v.bn_stats(st[:, t, :], src[:, t, :]).then_inc(bn[n].sem, 1)
                b.wait(dve, bn[n])
                v.memset(held[:], 0.0)
                for t in range(TB):
                    v.bn_aggr(mvt[:, t, :], st[:, t, :]).then_inc(mv[n].sem, 1)

            def normalise(b, n, dst, src, sig_):
                _, mvt, rst = lns[n]
                b.wait(dve, rs[n])
                for t in range(TB):
                    v.tensor_scalar(dst[:, t, :], src[:, t, :], mvt[:, t, 0:1], rst[:, t:t + 1],
                                    ALU.subtract, ALU.mult).then_inc(sig_.sem, 1)

            def times_c(b, k):
                if k in POOL_C:
                    return
                n = k // (J // JP)
                b.wait(dve, s_ok, k + 1)
                v.tensor_tensor(state[:, k % RING], state[:, k % RING],
                                bc[:, n % BC_SLOTS, 1, :].unsqueeze(1).broadcast_to([P, JP, L]),
                                ALU.mult).then_inc(p_ok.sem, 1)

            def unit(b, k, first, last):
                b.wait(dve, a_ok, JP * (k + 1))
                b.wait(dve, b_ok, k + 1)
                v.tensor_tensor_scan(state[:, k % RING].rearrange("p j t -> p (j t)"),
                                     decay[:, k % AR].rearrange("p j t -> p (j t)"),
                                     state[:, k % RING].rearrange("p j t -> p (j t)"),
                                     0.0, ALU.mult, ALU.add).then_inc(s_ok.sem, 1)
                if k:
                    times_c(b, k - 1)
                if k == UNITS - 1:
                    times_c(b, k)

            def step(name, b):
                if name == "l0s":
                    b.wait(dve, x_in)
                    stats(b, 0, xt)
                elif name == "l0a":
                    normalise(b, 0, xt, xt, n0)
                elif name == "l1s":
                    b.wait(dve, h_made, 2)
                    stats(b, 1, ht)
                elif name == "l1a":
                    b.wait(dve, h_made)
                    normalise(b, 1, ht, ht, n1)
                elif name[:2] == "qk":
                    n = int(name[2])
                    b.wait(dve, qk_f, n + 1)
                    if n:
                        b.wait(dve, qk_out, 16 * n)
                    else:
                        b.wait_last(dve, qk_out)
                    v.tensor_copy(qkp[:, 0], qkf[:]).then_inc(qk_s.sem, 1)
                    b.wait(dve, qk_s, 4 * n + 1)
                    v.tensor_tensor(qkf[:], qkf[:], qkp[:, 0], ALU.subtract).then_inc(qk_s.sem, 1)
                    b.wait(dve, qk_s, 4 * n + 2)
                    v.tensor_copy(qkp[:, 1], qkf[:]).then_inc(qk_s.sem, 1)
                    b.wait(dve, qk_s, 4 * n + 3)
                    v.tensor_tensor(qkp[:, 2], qkf[:], qkp[:, 1], ALU.subtract).then_inc(qk_s.sem, 1)
                elif name in ("xs0", "xs1", "xs2", "xs3"):
                    j = int(name[2])
                    b.wait(dve, xs_a, j + 1)
                    for s in range(1, K_CONV):
                        if s > 1:
                            b.wait(dve, xs_c, 3 * j + s - 1)
                        v.scalar_tensor_tensor(
                            out=xc[:, j, s:L], in0=pM[bank_of(name, 0)][:, 0:L - s],
                            scalar=conv_w[:, j, K_CONV - 1 - s:K_CONV - s], in1=xc[:, j, s:L],
                            op0=ALU.mult, op1=ALU.add).then_inc(xs_c.sem, 1)
                elif name == "sp1":
                    par = parity(b)
                    b.wait(dve, dt_x)
                    v.tensor_scalar(dts[:, par], us[:, par], SOFTPLUS_CAP, None, ALU.min).then_inc(dt_m.sem, 1)
                elif name == "sp3":
                    par = parity(b)
                    b.wait(dve, dt_e)
                    v.tensor_tensor(dts[:, par], dts[:, par], us[:, par], ALU.max).then_inc(dt_ok.sem, 1)
                elif name == "ud":
                    b.wait(dve, u_ok)
                    for j in range(J):
                        v.tensor_scalar(xc[:, j], xc[:, j], D_par[:, j:j + 1], None, ALU.mult).then_inc(xd_ok.sem, 1)
                elif name[:2] == "mx":
                    g = int(name[2])
                    if name[3] == "a" and g:
                        b.wait(dve, nm_ok, g)
                    mxv = mx[:, g % 2].rearrange("p (h q) -> p h q", q=TB)
                    for i, e in enumerate(MAX_PART[name[3]]):
                        qb, heads = MAX_FILLS[e]
                        n = (qb + 1) * P
                        b.wait(dve, s_ps, 12 * g + e + 1)
                        v.tensor_reduce(mxv[:, heads[0]:heads[-1] + 1, qb],
                                        pM[bank_of(name, i)][:, 0:len(heads) * n].rearrange("p (h k) -> p h k", k=n),
                                        AX_X, ALU.max).then_inc(mx_ok.sem, 1)
                    if name[3] == "f":
                        b.wait(dve, mx_ok, 11 * (g + 1))
                        if g:
                            b.wait(dve, s_ps, 12 * g)
                        else:
                            b.wait_last(dve, s_ps)
                        v.tensor_scalar(nmx[:], mx[:, g % 2], -1.0, None, ALU.mult).then_inc(nm_ok.sem, 1)
                elif name[:2] == "mt":
                    g = int(name[2])
                    b.wait(dve, s_ps, 12 * g + 12)
                    if g:
                        b.wait(dve, mrow_in, 32 * g)
                    else:
                        b.wait_last(dve, mrow_in)
                    pS = pM[bank_of(name, 0)]
                    v.tensor_copy(mrow[:, 0], pS[0:16, 0:P]).then_inc(mr_ok.sem, 1)
                    b.wait(dve, mr_ok, 2 * g + 1)
                    v.tensor_tensor(mrow[:, 1], pS[0:16, 0:P], mrow[:, 0], ALU.subtract)\
                     .then_inc(mr_ok.sem, 1)
                elif name[:2] == "on":
                    g = int(name[2])
                    ps = pM[bank_of(name, 0)][:].rearrange("p (t h r) -> p t h r", t=TB, r=32)
                    b.wait(dve, ot_ps, g + 1)
                    if g:
                        b.wait(dve, on_ok, g)
                    v.reciprocal(rden[:], ps[:, :, :, HD]).then_inc(rd_ok.sem, 1)
                    b.wait(dve, rd_ok, g + 1)
                    v.tensor_tensor(otok[:, :, g * G * HD:(g + 1) * G * HD].rearrange("p t (h r) -> p t h r", r=HD),
                                    ps[:, :, :, 0:HD], rden[:].unsqueeze(3).broadcast_to([P, TB, G, HD]),
                                    ALU.mult).then_inc(on_ok.sem, 1)
                elif name[:2] == "op":
                    n = int(name[2])
                    b.wait(dve, op_ps, n + 1)
                    b.wait(dve, x1p_in)
                    v.tensor_tensor(x1[:, 2 * n:2 * n + 2], x1[:, 2 * n:2 * n + 2],
                                    pM[bank_of(name, 0)][:].rearrange("p (t f) -> p t f", t=2), ALU.add)\
                     .then_inc(x1p_ok.sem, 1)
                elif name == "gate":
                    b.wait(dve, y_ok)
                    b.wait(dve, z_ok)
                    for t in range(TB):
                        v.tensor_tensor(zs[:, t], zs[:, t], pY[t][:], ALU.mult).then_inc(gated.sem, 1)
                elif name[:3] == "sso":
                    n = int(name[3])
                    b.wait(dve, so_ps, n + 1)
                    b.wait(dve, x1p_ok)
                    v.tensor_tensor(x1[:, 2 * n:2 * n + 2], x1[:, 2 * n:2 * n + 2],
                                    pM[bank_of(name, 0)][:].rearrange("p (t f) -> p t f", t=2), ALU.add)\
                     .then_inc(x1_ok.sem, 1)
                elif name == "l2s":
                    b.wait(dve, x1_ok)
                    stats(b, 2, x1)
                elif name == "l2a":
                    last_of_attention(b, dve)
                    normalise(b, 2, nrm(b), x1, n2)
                elif name[:3] == "f2_":
                    n = int(name[3])
                    b.wait(dve, f2_ps, n + 1)
                    b.wait(dve, x1b)
                    v.tensor_tensor(x1[:, 2 * n:2 * n + 2], x1[:, 2 * n:2 * n + 2],
                                    pM[bank_of(name, 0)][:].rearrange("p (t f) -> p t f", t=2), ALU.add)\
                     .then_inc(r_ok.sem, 1)
                elif name == "l3s":
                    b.wait(dve, x2_ok)
                    stats(b, 3, xr)
                elif name == "l3a":
                    normalise(b, 3, nrm(b), xr, n3)
                elif name == "route":
                    b.wait(dve, rt_ps)
                    v.tensor_tensor(lg[:], pM[bank_of(name, 0)][:, 0:TB * E].rearrange("p (t e) -> p t e", e=E),
                                    rb_row[:].unsqueeze(1).broadcast_to([P, TB, E]), ALU.add)\
                     .then_inc(rt_c.sem, 1)
                    b.wait(dve, rt_c, 1)
                    v.memset(held[:], 0.0)
                    for t in range(TB):
                        v.max(top[:, t, :], lg[:, t, :]).then_inc(rt_c.sem, 1)
                    b.wait(dve, rt_c, 5)
                    v.tensor_tensor(keep[:], lg[:], top[:, :, 1:2].broadcast_to([P, TB, E]), ALU.is_ge)\
                     .then_inc(rt_c.sem, 1)
                    b.wait(dve, rt_c, 6)
                    v.tensor_tensor(lg[:], lg[:], top[:, :, 0:1].broadcast_to([P, TB, E]), ALU.subtract)\
                     .then_inc(rt_c.sem, 1)
                elif name == "lora":
                    b.wait(dve, ex_ok)
                    v.tensor_tensor(ew[:], ew[:], keep[:], ALU.mult).then_inc(ew_ok.sem, 1)
                    b.wait(dve, ew_ok, 1)
                    v.tensor_reduce(esum[:], ew[:], AX_X, ALU.add).then_inc(ew_ok.sem, 1)
                    b.wait(dve, ew_ok, 2)
                    v.reciprocal(esum[:], esum[:]).then_inc(ew_ok.sem, 1)
                    b.wait(dve, ew_ok, 3)
                    v.scalar_tensor_tensor(out=ew[:], in0=ew[:], scalar=LORA_SCALE,
                                           in1=esum[:].unsqueeze(2).broadcast_to([P, TB, E]),
                                           op0=ALU.mult, op1=ALU.mult).then_inc(ew_ok.sem, 1)
                    b.wait(dve, la_ps)
                    b.wait(dve, ew_ok)
                    v.tensor_tensor(ax(b).rearrange("p t (e r) -> p t e r", e=E),
                                    pM[bank_of(name, 0)][:].rearrange("p (t e r) -> p t e r", t=TB, e=E),
                                    ew[:].unsqueeze(3).broadcast_to([P, TB, E, LR]), ALU.mult)\
                     .then_inc(ax_ok.sem, 1)
                elif name in ("out0", "out1"):
                    n = int(name[3])
                    b.wait(dve, out_ps, n + 1)
                    v.tensor_tensor(nrm(b)[:, 2 * n:2 * n + 2], pM[bank_of(name, 0)][:].rearrange("p (t f) -> p t f", t=2),
                                    bb_row[:].unsqueeze(1).broadcast_to([P, 2, D]), ALU.add)\
                     .then_inc(o_sum.sem, 1)

            drive(dve, unit, step)


MAX_FILLS = ([(3, [h]) for h in range(G)] + [(2, [h]) for h in range(G)]
             + [(1, [0, 1]), (1, [2, 3]), (0, [0, 1, 2, 3])])
MAX_PART = {part: range(2 * i, min(2 * i + 2, 11)) for i, part in enumerate("abcdef")}
N_LOADS = 41
CLEARED = 4
BUILT = 11
MODS_READY = 16
MODS_DONE = MODS_READY + 1
DVE_SETUP = MODS_DONE + 11

FIN_SET, PREP_SET = set(FIN), set(PREP)


SCHEDULE = [names.split() for names in (
    "oe3 on3 v0",
    "v1 ot0 ot1",
    "gate op0 op1 yt0 yt1 yt2 yt3",
    "load sso0 sso1 l2s",
    "z0 z1 l2a z2 ld0 mx0a mx0b",
    "h2t0 h2t1 f1_0 f1_1 z3 mx0c",
    "mx0d l0s l0a l0b",
    "f1_2 f1_3 f1_4 l0c mx0e f1_5 mx0f",
    "f1_6 l1s f1_7 gelu",
    "l1a f2_0",
    "xt0 zsilu f2_1 xt1 x2 x2b mt0 ld1",
    "l3s qk0 st0_0a",
    "st0_0b mx1a l3a qk1 st0_1a h3t0",
    "h3t1 mx1b qk2 route st0_1b",
    "st0_2a qk3 xs0 xs1 xs2 route2 lora st0_2b",
    "axt out0 out1 gb put st0_3a",
    "st0_3b mx1c mx1d oe0 mx1e mx1f mt1 on0",
    "st1_0a st1_0b ld2 mx2a mx2b",
    "mx2c",
    "st1_1a st1_1b mx2d st1_2a mx2e",
    "st1_2b mx2f st1_3a mt2 st1_3b",
    "xs3 ld3 oe1 on1",
    "st2_0a mx3a xsilu st2_0b",
    "mx3b xp mx3c mx3d",
    "mx3e",
    "dt0 dt1 dt2 dt3 st2_1a mx3f st2_1b st2_2a",
    "mt3 sp1 st2_2b st2_3a",
    "st2_3b",
    "oe2 on2 st3_0a st3_0b sp2 st3_1a",
    "st3_1b st3_2a sp3 u0 u1",
    "st3_2b ud st3_3a",
    "st3_3b",
)]
assert len(SCHEDULE) == UNITS and sorted(sum(SCHEDULE, [])) == sorted(FIN + Z + PREP + MAXIMA + ATT)


def place_products():
    place, n, banks = {}, 0, BANKS
    for names in SCHEDULE:
        for name in names:
            if name == "st0_0a":
                n, banks = 0, BANKS - 1
            if name[:2] == "mx":
                products = len(MAX_PART[name[3]])
            elif name[:2] == "st":
                products = len(HALF[name[5]])
            else:
                products = 0 if name in NO_PRODUCT else 1
            for i in range(products):
                place[name, i] = n % banks
                n += 1
    return place


HALF = {"a": (0, 1), "b": (2, 3)}
NO_PRODUCT = {"gate", "l2s", "l2a", "gelu", "x2", "l3s", "l3a", "route2", "put", "zsilu", "load", "l0s", "l0a",
              "l1s", "l1a", "xsilu", "sp1", "sp2", "sp3", "u0", "u1", "ud", "l0b", "l0c", "x2b", "gb", "oe0", "oe1", "oe2", "oe3", "ld0", "ld1", "ld2", "ld3"}
PLACE = place_products()


def bank_of(name, i):
    return PLACE[name, i]


_INS = ["x", "ln1_w", "ln1_b", "ln2_w", "ln2_b", "q_w", "q_b", "k_w", "k_b", "v_w", "v_b", "o_w", "o_b",
        "in_proj_w", "conv_w", "conv_b", "x_proj_w", "dt_w", "dt_b", "A_log", "D_param", "ssm_out_w",
        "mix_weight", "ffn_w1", "ffn_b1", "ffn_w2", "ffn_b2"]
_INS = {**{n: "L0_attn_" + n for n in _INS},
        **{n: "L0_ffn_" + n for n in ("base_w", "base_b", "lora_A", "lora_B", "router_w", "router_b")},
        "c": "L0_c", "wmod": "L0_wmod"}


def kernel(**inputs):
    import numpy as _np
    import concourse.bacc as _bacc
    from concourse import mybir as _mybir
    from concourse.bass_utils import run_bass_kernel_spmd as _run

    nc = _bacc.Bacc("TRN2", target_bir_lowering=False, num_devices=1)
    arrays, args = {}, {}
    for name, full in _INS.items():
        a = _np.ascontiguousarray(inputs[full])
        arrays[f"in_{name}_dram"] = a
        args[name] = nc.dram_tensor(f"in_{name}_dram", a.shape, _mybir.dt.from_np(a.dtype), kind="ExternalInput").ap()
    out = nc.dram_tensor("out_dram", (B, L, D), _mybir.dt.float32, kind="ExternalOutput").ap()
    adaln_block(nc, args, out)
    r = _run(nc, [arrays], core_ids=[0])
    return r.results[0]["out_dram"]
```
